# Optimizing a Trainium2 kernel written in Bass

```python
import numpy as np
import jax
import jax.numpy as jnp

def _softmax(x, axis=-1):
    return jax.nn.softmax(x, axis=axis)

def _gelu(x):
    return jax.nn.gelu(x, approximate=True)

def _silu(x):
    return jax.nn.silu(x)

def _sigmoid(x):
    return jax.nn.sigmoid(x)

def _layernorm(x, axis=-1, eps=1e-05):
    m = jnp.mean(x, axis=axis, keepdims=True)
    v = jnp.var(x, axis=axis, keepdims=True)
    return (x - m) / jnp.sqrt(v + eps)

def _scatter_add(tgt, idx, src, axis=0):
    return tgt.at[idx].add(src)

def _segment_sum(src, seg, n):
    return jax.ops.segment_sum(src, seg, n)
kernel_name = 'mk_lm_tower_d1_tok_ids256_r4_ae6283'

def setup_inputs(seed: int=0):
    np.random.seed(seed)
    _w = jnp.asarray

    def _rec_inputs():
        import jax
        import jax.numpy as jnp
        _rk = jax.random.key(seed)
        x = jax.random.randint(jax.random.fold_in(_rk, 1), (2, 2048), 0, 99998, jnp.int32)
        return x
    x = _rec_inputs()

    def _L0_tok_setup():
        import jax, jax.numpy as jnp
        import numpy as np
        P = 100003
        M = 12500
        IC = 4
        NUM_SPECIAL = 4
        A_VALS = np.array([12345, 20011], dtype=np.int32)
        B_VALS = np.array([6789, 54321], dtype=np.int32)
        VOCAB = 25000
        EMBED = 64
        NUM_HASHES = 2
        B, S = (64, 512)
        key = jax.random.key(seed)
        k1, k2, k3 = jax.random.split(key, 3)
        x = jax.random.randint(k1, (B, S), 0, VOCAB, dtype=jnp.int32)
        shared = 0.02 * jax.random.normal(k2, (M + IC, EMBED), dtype=jnp.float32)
        shared = shared.at[0].set(0.0)
        hw = jax.random.normal(k3, (VOCAB, NUM_HASHES), dtype=jnp.float32)
        hw = hw.at[0].set(0.0)
        return {'x': x, 'shared_embedding': shared, 'hash_weights_table': hw}
    _L0_tok_all = _L0_tok_setup()
    _L0_tok_in = {k: v for k, v in _L0_tok_all.items() if k in ('shared_embedding', 'hash_weights_table')}
    del _L0_tok_all

    def _L0_attn_setup():
        import jax, jax.numpy as jnp
        import numpy as np
        STD = 0.02
        key = jax.random.key(seed)
        k1, k2, k3 = jax.random.split(key, 3)
        b, n_t, n, n_h = (2, 512, 64, 8)
        r_prime = jax.random.normal(k1, (b, n_t, n), dtype=jnp.float32)
        Q = STD * jax.random.normal(k2, (n_h, n, n), dtype=jnp.float32)
        E = STD * jax.random.normal(k3, (n_h, n, n), dtype=jnp.float32)
        return {'r_prime': r_prime, 'Q': Q, 'E': E}
    _L0_attn_all = _L0_attn_setup()
    _L0_attn_in = {k: v for k, v in _L0_attn_all.items() if k in ('Q', 'E')}
    del _L0_attn_all

    def _L0_ffn_setup():
        import jax, jax.numpy as jnp
        import numpy as np
        B, T, C = (64, 96, 64)
        NH, NKV = (4, 2)
        HD = C // NH
        NREP = NH // NKV
        NE, TOPK = (8, 2)
        HID = int(8 / 3 * C)
        EPS_RMS = 1e-06

        def _rope_tables(t_len):
            inv_freq = 1.0 / 10000.0 ** (np.arange(0, HD, 2, dtype=np.float32) / HD)
            t = np.arange(t_len, dtype=np.float32)
            freqs = np.outer(t, inv_freq)
            emb = np.concatenate([freqs, freqs], axis=-1)
            return (jnp.asarray(np.cos(emb)), jnp.asarray(np.sin(emb)))

        def _rotate_half(x):
            h = x.shape[-1] // 2
            return jnp.concatenate([-x[..., h:], x[..., :h]], axis=-1)

        def _rmsnorm(v, w):
            return v * jax.lax.rsqrt(jnp.mean(v * v, axis=-1, keepdims=True) + EPS_RMS) * w
        key = jax.random.key(seed)
        ks = jax.random.split(key, 10)
        s = lambda k, shape: jax.random.normal(k, shape, jnp.float32) * 0.02
        return {'x': jax.random.normal(ks[0], (B, T, C), jnp.float32), 'ln1_w': jnp.ones((C,), jnp.float32), 'ln2_w': jnp.ones((C,), jnp.float32), 'wq': s(ks[1], (NH * HD, C)), 'wk': s(ks[2], (NKV * HD, C)), 'wv': s(ks[3], (NKV * HD, C)), 'wo': s(ks[4], (C, C)), 'router_w': s(ks[5], (NE, C)), 'w1': s(ks[6], (NE, HID, C)), 'w2': s(ks[7], (NE, C, HID)), 'w3': s(ks[8], (NE, HID, C))}
    _L0_ffn_all = _L0_ffn_setup()
    _L0_ffn_in = {k: v for k, v in _L0_ffn_all.items() if k in ('ln1_w', 'ln2_w', 'wq', 'wk', 'wv', 'wo', 'router_w', 'w1', 'w2', 'w3')}
    del _L0_ffn_all
    return {'x': x, 'L0_tok_shared_embedding': _L0_tok_in['shared_embedding'], 'L0_tok_hash_weights_table': _L0_tok_in['hash_weights_table'], 'L0_attn_Q': _L0_attn_in['Q'], 'L0_attn_E': _L0_attn_in['E'], 'L0_ffn_ln1_w': _L0_ffn_in['ln1_w'], 'L0_ffn_ln2_w': _L0_ffn_in['ln2_w'], 'L0_ffn_wq': _L0_ffn_in['wq'], 'L0_ffn_wk': _L0_ffn_in['wk'], 'L0_ffn_wv': _L0_ffn_in['wv'], 'L0_ffn_wo': _L0_ffn_in['wo'], 'L0_ffn_router_w': _L0_ffn_in['router_w'], 'L0_ffn_w1': _L0_ffn_in['w1'], 'L0_ffn_w2': _L0_ffn_in['w2'], 'L0_ffn_w3': _L0_ffn_in['w3']}

def reference(x, L0_tok_shared_embedding, L0_tok_hash_weights_table, L0_attn_Q, L0_attn_E, L0_ffn_ln1_w, L0_ffn_ln2_w, L0_ffn_wq, L0_ffn_wk, L0_ffn_wv, L0_ffn_wo, L0_ffn_router_w, L0_ffn_w1, L0_ffn_w2, L0_ffn_w3):
    import jax
    import jax.numpy as jnp

    def _L0_tok_ref(x, shared_embedding, hash_weights_table):
        import jax, jax.numpy as jnp
        import numpy as np
        P = 100003
        M = 12500
        IC = 4
        NUM_SPECIAL = 4
        A_VALS = np.array([12345, 20011], dtype=np.int32)
        B_VALS = np.array([6789, 54321], dtype=np.int32)
        VOCAB = 25000
        EMBED = 64
        NUM_HASHES = 2
        B, S = (64, 512)
        hw = hash_weights_table[x]
        a = jnp.asarray(A_VALS)
        b = jnp.asarray(B_VALS)
        hashes = (a * x[..., None] + b) % P % M + IC
        hashes = jnp.where(x[..., None] < NUM_SPECIAL, x[..., None], hashes)
        embs = shared_embedding[hashes]
        return jnp.einsum('bsh,bshe->bse', hw, embs)

    def _L0_attn_ref(r_prime, Q, E):
        import jax, jax.numpy as jnp
        import numpy as np
        STD = 0.02
        Omega = jnp.einsum('bti,hij,buj->bhtu', r_prime, Q, r_prime)
        n_t = r_prime.shape[1]
        mask = jnp.tril(jnp.ones((n_t, n_t), dtype=r_prime.dtype))
        Omega = Omega * mask
        r = jnp.einsum('bhtu,hij,buj->bti', Omega, E, r_prime)
        return r

    def _L0_ffn_ref(x, ln1_w, ln2_w, wq, wk, wv, wo, router_w, w1, w2, w3):
        import jax, jax.numpy as jnp
        import numpy as np
        B, T, C = (64, 96, 64)
        NH, NKV = (4, 2)
        HD = C // NH
        NREP = NH // NKV
        NE, TOPK = (8, 2)
        HID = int(8 / 3 * C)
        EPS_RMS = 1e-06

        def _rope_tables(t_len):
            inv_freq = 1.0 / 10000.0 ** (np.arange(0, HD, 2, dtype=np.float32) / HD)
            t = np.arange(t_len, dtype=np.float32)
            freqs = np.outer(t, inv_freq)
            emb = np.concatenate([freqs, freqs], axis=-1)
            return (jnp.asarray(np.cos(emb)), jnp.asarray(np.sin(emb)))

        def _rotate_half(x):
            h = x.shape[-1] // 2
            return jnp.concatenate([-x[..., h:], x[..., :h]], axis=-1)

        def _rmsnorm(v, w):
            return v * jax.lax.rsqrt(jnp.mean(v * v, axis=-1, keepdims=True) + EPS_RMS) * w
        Bx, Tx, Cx = x.shape
        h = _rmsnorm(x, ln1_w)
        q = (h @ wq.T).reshape(Bx, Tx, NH, HD).transpose(0, 2, 1, 3)
        k = (h @ wk.T).reshape(Bx, Tx, NKV, HD).transpose(0, 2, 1, 3)
        v = (h @ wv.T).reshape(Bx, Tx, NKV, HD).transpose(0, 2, 1, 3)
        cos, sin = _rope_tables(Tx)
        cos, sin = (cos[None, None], sin[None, None])
        q = q * cos + _rotate_half(q) * sin
        k = k * cos + _rotate_half(k) * sin
        k = jnp.repeat(k, NREP, axis=1)
        v = jnp.repeat(v, NREP, axis=1)
        scores = jnp.einsum('bhtd,bhsd->bhts', q, k) / jnp.sqrt(jnp.float32(HD))
        causal = jnp.tril(jnp.ones((Tx, Tx), dtype=bool))
        scores = jnp.where(causal[None, None], scores, jnp.float32(-1e+30))
        att = jax.nn.softmax(scores, axis=-1)
        y = jnp.einsum('bhts,bhsd->bhtd', att, v).transpose(0, 2, 1, 3).reshape(Bx, Tx, Cx)
        x = x + y @ wo.T
        flat = _rmsnorm(x, ln2_w).reshape(-1, Cx)
        probs = jax.nn.softmax(flat @ router_w.T, axis=-1)
        tp, ti = jax.lax.top_k(probs, TOPK)
        tp = tp / (jnp.sum(tp, axis=-1, keepdims=True) + 1e-09)
        weights = jnp.sum(tp[..., None] * jax.nn.one_hot(ti, NE, dtype=flat.dtype), axis=1)
        out = jnp.zeros_like(flat)
        for e in range(NE):
            hh = jax.nn.silu(flat @ w1[e].T) * (flat @ w3[e].T)
            out = out + weights[:, e:e + 1] * (hh @ w2[e].T)
        return x + out.reshape(Bx, Tx, Cx)
    h = _L0_tok_ref(x, L0_tok_shared_embedding, L0_tok_hash_weights_table)
    h = h + _L0_attn_ref(_layernorm(h, axis=-1), L0_attn_Q, L0_attn_E)
    h = h + _L0_ffn_ref(_layernorm(h, axis=-1), L0_ffn_ln1_w, L0_ffn_ln2_w, L0_ffn_wq, L0_ffn_wk, L0_ffn_wv, L0_ffn_wo, L0_ffn_router_w, L0_ffn_w1, L0_ffn_w2, L0_ffn_w3)
    return h

_drawn_inputs = setup_inputs


def setup_inputs(seed=0):
    import zlib

    import numpy as np

    out = dict(_drawn_inputs(seed))
    spreads = {'L0_ffn_ln1_w': (1.0, 0.6), 'L0_ffn_ln2_w': (1.0, 0.6)}
    factors = {'L0_ffn_wq': 8.0,
     'L0_ffn_wk': 8.0,
     'L0_ffn_wv': 8.0,
     'L0_ffn_wo': 8.0,
     'L0_ffn_router_w': 8.0,
     'L0_ffn_w1': 8.0,
     'L0_ffn_w2': 8.0,
     'L0_ffn_w3': 8.0}
    for name, (base, spread) in spreads.items():
        noise = np.random.default_rng([zlib.crc32(name.encode()), seed]).standard_normal(out[name].shape)
        drawn = base * np.exp(spread * noise) if base else spread * noise
        out[name] = jnp.asarray(drawn.astype(out[name].dtype))
    for name, factor in factors.items():
        out[name] = (out[name] * factor).astype(out[name].dtype)
    return out
```

```python
from contextlib import ExitStack

import concourse.bass as bass
from concourse import mybir

F32 = mybir.dt.float32
BF16 = mybir.dt.bfloat16
I32 = mybir.dt.int32
U32 = mybir.dt.uint32
ALU = mybir.AluOpType
ACT = mybir.ActivationFunctionType
AX = mybir.AxisListType.X

P = 128
C = 64
NB, T = 2, 2048
BLK = 512
TPB = BLK // P
NBLK = NB * T // BLK
BPS = T // BLK
NT = NB * T // P
LH = 8
NPAIR = LH // 2
NH, NKV, HD = 4, 2, 16
VW = 32
NQK = (NH + NKV) * HD
NTERM = 6
KSC = NTERM * HD
KROWS = KSC + 3
QPART = [0, 0, 1, 1, 0, 2]
KPART = [0, 1, 0, 1, 2, 0]
NE, HID = 8, 170
EW = 32
NHID = NE * HID
NKT = (NHID + P - 1) // P
HASHP, HASHM, IC, NSPECIAL, VOCAB = 100003, 12500, 4, 4, 25000
HASH_A, HASH_B = (12345, 20011), (6789, 54321)
EPS_LN, EPS_RMS = 1e-5, 1e-6
NEG = -1e30


def at(n, k=1, per=1):
    return per * n + k + 1


def bcast(ap, n):
    return ap.unsqueeze(len(ap.shape)).to_broadcast([*ap.shape, n])


def program(nc, ids, table, hash_w, lq, le, ln1, ln2, wqk, wrot, wv, wo, wr, w1, w3, w2, sel, cos, sin, out):
    with ExitStack() as ctx:
        def sb(name, shape, dt=F32):
            return ctx.enter_context(nc.sbuf_tensor(name, shape, dt))

        sems = []

        def sem(name, first=1):
            s = ctx.enter_context(nc.semaphore(name))
            if first:
                sems.append(s)
            return s

        ps = ctx.enter_context(nc.psum_tensor("ps", [P, 8, 512], F32))
        bank = [ps[:, i, :] for i in range(8)]
        parts_dram = nc.dram_tensor("qk_parts", (NBLK, NQK, 3, BLK), BF16, kind="Internal").ap()

        ident = sb("ident", [P, P])
        identb = sb("identb", [P, P], BF16)
        keep_t_ge_u = sb("keep_t_ge_u", [P, P])
        h_all = sb("h_all", [P, NT, C])
        x_all = sb("x_all", [P, NT, C])
        Qs = sb("Qs", [KROWS, NBLK, NH, BLK], BF16)
        Ks = sb("Ks", [KROWS, NBLK, NKV, BLK], BF16)
        Vn = sb("Vn", [P, NT, NKV * VW])
        xid = sb("xid", [P, NT], I32)
        dig = sb("dig", [P, 3, NT], I32)
        hsh = sb("hsh", [P, NT])
        quo = sb("quo", [P, NT], I32)
        quf = sb("quf", [P, NT])
        rows = sb("rows", [P, NT, 3], U32)
        emb = sb("emb", [P, TPB, 2, C])
        embw = sb("embw", [P, TPB, 2])
        t2 = sb("t2", [P, TPB, 2, C])
        xc = sb("xc", [P, TPB, C])
        sq = sb("sq", [P, TPB, C])
        st = sb("st", [P, 4, TPB])
        rr = sb("rr", [P, TPB, 2 * C])
        res = sb("res", [P, TPB, C])
        Sx = sb("Sx", [P, TPB, 4 * C], BF16)
        AB = sb("AB", [P, 2, BLK], BF16)
        rTe = sb("rTe", [P, BLK])
        rTo = sb("rTo", [P, BLK])
        qh = sb("qh", [P, NPAIR, BLK])
        om = sb("om", [P, 2, NPAIR, P])
        Gs = sb("Gs", [P, NPAIR, BLK])
        oT = sb("oT", [P, 2 * P])
        Cd = sb("Cd", [P, TPB, P])
        keep = sb("keep", [P, NBLK])
        hn = sb("hn", [P, TPB, C])
        ln1b = sb("ln1b", [P, C])
        csb = sb("csb", [NQK, 2, BLK])
        rp = sb("rp", [NQK, 3, BLK])
        qkp = sb("qkp", [NQK, 3, BLK], BF16)
        wtmp = sb("wtmp", [P, NHID])
        wres = sb("wres", [P, NHID])

        def weight3(name, n):
            return sb(name, [P, 3, n], BF16)

        lq3 = weight3("lq3", NPAIR * P)
        wqk3 = weight3("wqk3", 2 * NQK)
        wv3 = weight3("wv3", NKV * HD)
        wo3 = weight3("wo3", C)
        wr3 = weight3("wr3", NE)
        w13 = weight3("w13", NHID)
        w33 = weight3("w33", NHID)
        leS = sb("leS", [P, NPAIR, C])
        w2S = sb("w2S", [P, NKT, C])
        ln2b = sb("ln2b", [P, C])
        selb = sb("selb", [3 * EW, NKT * P], BF16)
        neg_t_lt_s = sb("neg_t_lt_s", [P, P], BF16)
        neg_s_gt_t = sb("neg_s_gt_t", [P, P], BF16)
        mxc = sb("mxc", [P, NH, TPB, BPS])
        mneg = sb("mneg", [P, 2, NH * TPB])
        m3 = sb("m3", [P, 3, NH * TPB], BF16)
        mrow = sb("mrow", [3 * NH * TPB, P], BF16)
        pexp = sb("pexp", [P, 2, NH, BLK])
        yT = sb("yT", [P, BLK])
        rden = sb("rden", [P, TPB, NH])
        y_all = sb("y_all", [P, NT, C])
        ABf = pexp[:, :, :, :].bitcast(BF16).rearrange("p a h (s t) -> p (a h) s t", s=2)
        var2 = sb("var2", [P, NT])
        lg = sb("lg", [P, NT, NE])
        pr = sb("pr", [P, NT, NE])
        tk = sb("tk", [P, NT, NE])
        tr = sb("tr", [P, NT, NE])
        cols = sb("cols", [P, 4, NT])
        rank = sb("rank", [P, NE])
        w3s = sb("w3s", [P, NT, 3, EW], BF16)
        WT = sb("WT", [3 * EW, BLK], BF16)
        sg, hu, hh = qh[:, 0:2, :], qh[:, 2:4, :], Gs[:, 0:2, :]
        fin = sb("fin", [P, TPB, C])

        consts_in = sem("consts_in")
        weight_in = sem("weight_in")
        weight_free = sem("weight_free")
        dve_w = sem("dve_w")
        masks_ok = sem("masks_ok")
        init_ok = sem("init_ok")
        rows_ok = sem("rows_ok")
        gathered = sem("gathered", first=0)
        emb_used = sem("emb_used")
        var_r, sd_r = sem("var_r"), sem("sd_r")
        xr_ok, x1_ok, split_ok = sem("xr_ok"), sem("x1_ok"), sem("split_ok")
        stacked, ab_ok = sem("stacked"), sem("ab_ok")
        rT_ps, rT_ok = sem("rT_ps"), sem("rT_ok")
        cup_ps, cup_ok = sem("cup_ps"), sem("cup_ok")
        qh_ps, qh_ok = sem("qh_ps"), sem("qh_ok")
        om_ps, om_ok = sem("om_ps"), sem("om_ok")
        g_ps, g_ok = sem("g_ps"), sem("g_ok")
        inter_done = sem("inter_done")
        oT_ps, oT_ok = sem("oT_ps"), sem("oT_ok")
        on_ps, on_ok = sem("on_ps"), sem("on_ok")
        qk_ps, v_ps, rope_ok, v_ok = sem("qk_ps"), sem("v_ps"), sem("rope_ok"), sem("v_ok")
        cs_in = sem("cs_in")
        p1_ok, parts_ok = sem("p1_ok"), sem("parts_ok")
        parts_out, qk_in = sem("parts_out"), sem("qk_in")
        out_done = sem("out_done")
        qs_free = sem("qs_free")
        mx_ps, mx_ok, m3_ok, mt_ps, mrow_ok, m_in = sem("mx_ps"), sem("mx_ok"), sem("m3_ok"), sem("mt_ps"), sem("mrow_ok"), sem("m_in")
        st_ps, exp_ok, pv_ok = sem("st_ps"), sem("exp_ok"), sem("pv_ok")
        yT_ps, yT_ok, yn_ps, yn_ok = sem("yT_ps"), sem("yT_ok"), sem("yn_ps"), sem("yn_ok")
        xb_ok, xb1_ok, sb_ok, stb, abb_ok = sem("xb_ok"), sem("xb1_ok"), sem("sb_ok"), sem("stb"), sem("abb_ok")
        wo_ps, wo_ok = sem("wo_ps"), sem("wo_ok")
        var2_ok, sd2_ok = sem("var2_ok"), sem("sd2_ok")
        lg_ps, lg_ok, lm_ok, pe_ok, w_ok = sem("lg_ps"), sem("lg_ok"), sem("lm_ok"), sem("pe_ok"), sem("w_ok")
        WT_ps, WT_ok = sem("WT_ps"), sem("WT_ok")
        gu_ps, wb_ps, sg_ok, hu_ok, hh_ok, w2_done = sem("gu_ps"), sem("wb_ps"), sem("sg_ok"), sem("hu_ok"), sem("hh_ok"), sem("w2_done")
        eT_ok, en_ps, fin_ok = sem("eT_ok"), sem("en_ps"), sem("fin_ok")

        block = ctx.enter_context(nc.Block())
        outv = out.rearrange("b (t p) c -> p (b t) c", p=P)
        WEIGHTS = [(lq, lq3, NPAIR * P), (wqk, wqk3[:, :, 0:NQK], NQK), (wrot, wqk3[:, :, NQK:], NQK), (wv, wv3, NKV * HD),
                   (wo, wo3, C), (wr, wr3, NE), (w1, w13, NHID), (w3, w33, NHID)]
        M_UNITS = [[(i, h, c) for i in range(TPB) for h in range(NH) for c in range(k + 1)] for k in range(BPS)]
        M_BEFORE = [sum(len(u) for u in M_UNITS[:k]) for k in range(BPS + 1)]
        STEPS = [TPB * (k + 1) for k in range(BPS)]
        S_BEFORE = [sum(STEPS[:k]) for k in range(BPS + 1)]
        NM, NS = M_BEFORE[-1], S_BEFORE[-1]

        def m_after(k, s):
            return 0 if k + 1 == BPS else min(len(M_UNITS[k + 1]), len(M_UNITS[k + 1]) * (s + 1) // (STEPS[k] - 2))


        @block.sync
        def _(sp):
            for s in sems:
                sp.sem_inc(s, 1)
            sp.dma_start(xid[:, :], ids).then_inc(consts_in, 16)
            sp.dma_start(leS[:, :, :], le).then_inc(consts_in, 16)
            sp.dma_start(ln1b[:, :], ln1.to_broadcast([P, C])).then_inc(consts_in, 16)
            sp.dma_start(ln2b[:, :], ln2.to_broadcast([P, C])).then_inc(consts_in, 16)
            sp.dma_start(w2S[:, :, :], w2).then_inc(consts_in, 16)
            sp.dma_start(selb[:, :], sel).then_inc(consts_in, 16)
            for i, (src, _, n) in enumerate(WEIGHTS):
                if i:
                    sp.wait_ge(weight_free, at(i - 1))
                sp.dma_start(wtmp[:, 0:n], src).then_inc(weight_in, 16)
            with sp.Fori(0, NBLK) as n:
                sp.wait_ge(rope_ok, at(n, 0))
                sp.dma_start(csb[:, 0, :], cos[:, bass.ts(n, BLK)]).then_inc(cs_in, 16)
                sp.dma_start(csb[:, 1, :], sin[:, bass.ts(n, BLK)]).then_inc(cs_in, 16)
                sp.wait_ge(parts_ok, at(n))
                sp.dma_start(parts_dram[bass.ts(n, 1), :, :, :].rearrange("a p s t -> (a p) s t"), qkp[:, :, :]).then_inc(parts_out, 16)
                sp.wait_ge(parts_out, at(n, 16, 16))
                for g in range(NTERM):
                    src = parts_dram[bass.ts(n, 1), 0:NH * HD, QPART[g], :].rearrange("a (h d) t -> d (a h) t", d=HD)
                    sp.dma_start(Qs[g * HD:(g + 1) * HD, bass.ts(n, 1), :, :].rearrange("p a h t -> p (a h) t"), src).then_inc(qk_in, 16)
                    src = parts_dram[bass.ts(n, 1), NH * HD:NQK, KPART[g], :].rearrange("a (h d) t -> d (a h) t", d=HD)
                    sp.dma_start(Ks[g * HD:(g + 1) * HD, bass.ts(n, 1), :, :].rearrange("p a h t -> p (a h) t"), src).then_inc(qk_in, 16)
            sp.wait_ge(qk_in, at(NBLK - 1, 12 * 16, 12 * 16))
            for b in range(NB):
                for k in range(BPS):
                    sp.wait_ge(mrow_ok, at(b, k + 1, BPS))
                    for g in range(3):
                        sp.dma_start(Qs[KSC + g:KSC + g + 1, b * BPS + k, :, :].rearrange("p h (i t) -> p (h i) t", t=P),
                                     mrow[g * NH * TPB:(g + 1) * NH * TPB, :]).then_inc(m_in, 16)
            with sp.Fori(0, NBLK) as n:
                sp.wait_ge(fin_ok, at(n))
                sp.dma_start(outv[:, bass.ts(n, TPB), :], fin[:, :, :]).then_inc(out_done, 16)
            sp.wait_ge(out_done, at(NBLK - 1, 16, 16))

        @block.gpsimd
        def _(pool):
            nc.gpsimd.memset(ident[:, :], 0.0)
            nc.gpsimd.memset(keep_t_ge_u[:, :], 1.0)
            nc.gpsimd.memset(Vn[:, :, :], 0.0)
            pool.drain()
            nc.gpsimd.memset(Ks[KSC:KROWS, :, :, :], 1.0)
            pool.drain()
            nc.gpsimd.affine_select(out=ident[:, :], in_=ident[:, :], compare_op=ALU.not_equal, fill=1.0,
                                    base=0, pattern=[[-1, P]], channel_multiplier=1)
            nc.gpsimd.affine_select(out=keep_t_ge_u[:, :], in_=keep_t_ge_u[:, :], compare_op=ALU.is_ge, fill=0.0,
                                    base=0, pattern=[[1, P]], channel_multiplier=-1)
            nc.gpsimd.memset(neg_t_lt_s[:, :], 0.0)
            nc.gpsimd.memset(neg_s_gt_t[:, :], 0.0)
            for e in range(NE):
                nc.gpsimd.memset(rank[:, e:e + 1], float(NE - e))
            pool.drain()
            nc.gpsimd.affine_select(out=neg_t_lt_s[:, :], in_=neg_t_lt_s[:, :], compare_op=ALU.is_ge, fill=NEG,
                                    base=0, pattern=[[-1, P]], channel_multiplier=1)
            nc.gpsimd.affine_select(out=neg_s_gt_t[:, :], in_=neg_s_gt_t[:, :], compare_op=ALU.is_ge, fill=NEG,
                                    base=0, pattern=[[1, P]], channel_multiplier=-1)
            for g in range(NKV):
                nc.gpsimd.memset(Vn[:, :, g * VW + HD:g * VW + HD + 1], 1.0)
            pool.drain()
            nc.gpsimd.tensor_copy(identb[:, :], ident[:, :]).then_inc(masks_ok, 1)
            pool.wait_ge(rows_ok, at(0))
            for n in range(NBLK):
                if n:
                    pool.wait_ge(emb_used, at(n, 0))
                for t in range(TPB):
                    for h in range(2):
                        pool.indirect_dma_start(emb[:, t, h, :], None, table,
                                                bass.IndirectOffsetOnAxis(ap=rows[:, n * TPB + t, h:h + 1], axis=0)).then_inc(gathered, 16)
                    pool.indirect_dma_start(embw[:, t, :], None, hash_w,
                                            bass.IndirectOffsetOnAxis(ap=rows[:, n * TPB + t, 2:3], axis=0)).then_inc(gathered, 16)

        @block.scalar
        def _(act):
            a = nc.scalar

            def split_copies(n, i, src):
                act.wait_ge(xr_ok, at(n, i, 2))
                act.wait_ge(stacked, at(n, i - 1, 2))
                a.activation(Sx[:, :, 0:C], src, ACT.Copy)
                a.activation(Sx[:, :, 2 * C:3 * C], src, ACT.Copy).then_inc(x1_ok, 1)

            def sqrt(n, i, k):
                act.wait_ge(var_r, at(n, i, 3))
                a.activation(st[:, k, :], st[:, k, :], ACT.Sqrt).then_inc(sd_r, 1)

            def evac_ab(n, i):
                act.wait_ge(stacked, at(n, i, 2))
                act.wait_ge(*((v_ps, at(n, 0)) if i == 1 else (qh_ps, at(n, NPAIR, NPAIR))))
                a.activation(AB[:, :, :], bank[0].bitcast(BF16).rearrange("p (s t) -> p s t", s=2),
                             ACT.Copy).then_inc(ab_ok, 1)

            with act.Fori(0, NBLK) as n:
                sqrt(n, 1, 2)
                split_copies(n, 1, rr[:, :, 0:C])
                evac_ab(n, 1)
                for p in range(NPAIR):
                    act.wait_ge(qh_ps, at(n, p + 1, NPAIR))
                    a.activation(qh[:, p, :], bank[2 + p % 2], ACT.Copy).then_inc(qh_ok, 1)
                for c in range(TPB):
                    act.wait_ge(g_ps, at(n, c + 1, TPB))
                    a.activation(Gs[:, :, c * P:(c + 1) * P], bank[6 + c % 2].rearrange("p (a t) -> p a t", a=NPAIR),
                                 ACT.Copy).then_inc(g_ok, 1)
                act.wait_ge(oT_ps, at(n))
                a.activation(oT[:, :], bank[2][:, 0:2 * P], ACT.Copy).then_inc(oT_ok, 1)
                sqrt(n, 2, 2)
                sqrt(n, 3, 3)
                split_copies(n, 2, hn[:, :, :])
                evac_ab(n, 2)
                act.wait_ge(v_ps, at(n))
                a.activation(Vn[:, bass.ts(n, TPB), :].rearrange("p t (g w) -> p t g w", g=NKV)[:, :, :, 0:HD],
                             bank[1][:, 0:TPB * NKV * HD].rearrange("p (t g d) -> p t g d", t=TPB, g=NKV),
                             ACT.Copy).then_inc(v_ok, 1)
                act.wait_ge(rope_ok, at(n))
                act.wait_ge(parts_out, at(n, 0, 16))
                a.activation(qkp[:, 0, :], rp[:, 0, :], ACT.Copy).then_inc(p1_ok, 1)

            for b in range(NB):
                def mrow_copy(k):
                    act.wait_ge(mt_ps, at(b, k + 1, BPS))
                    act.wait_ge(m_in, at(b, 48 * k, 48 * BPS))
                    a.activation(mrow[:, :], bank[6].bitcast(BF16)[0:3 * NH * TPB, 0:P], ACT.Copy).then_inc(mrow_ok, 1)

                mrow_copy(0)
                for k in range(BPS):
                    for s in range(STEPS[k]):
                        i = S_BEFORE[k] + s
                        off = max(0, s - TPB * k) * P
                        for hp in range(2):
                            act.wait_ge(st_ps, at(b, 2 * i + hp + 1, 2 * NS))
                            if i >= 2:
                                act.wait_ge(pv_ok, at(b, i - 1, NS))
                            a.activation(pexp[:, i % 2, 2 * hp:2 * hp + 2, off:], ps[:, 2 * hp:2 * hp + 2, off:], ACT.Exp,
                                         scale=float(HD) ** -0.5).then_inc(exp_ok, 1)
                        if s == STEPS[k] - 3 and k + 1 < BPS:
                            mrow_copy(k + 1)
                    act.wait_ge(pv_ok, at(b, S_BEFORE[k + 1], NS))
                    act.wait_ge(yn_ps, at(b, k, BPS))
                    a.activation(yT[:, :], bank[7], ACT.Copy).then_inc(yT_ok, 1)

            with act.Fori(0, NBLK) as n:
                act.wait_ge(stb, at(n, 0))
                act.wait_ge(yn_ok, at(NB * BPS - 1))
                a.activation(Sx[:, :, 0:C], y_all[:, bass.ts(n, TPB), :], ACT.Copy)
                a.activation(Sx[:, :, 2 * C:3 * C], y_all[:, bass.ts(n, TPB), :], ACT.Copy).then_inc(xb1_ok, 1)
                act.wait_ge(stb, at(n))
                act.wait_ge(wo_ps, at(n, 0))
                a.activation(AB[:, :, :], bank[0].bitcast(BF16).rearrange("p (s t) -> p s t", s=2), ACT.Copy).then_inc(abb_ok, 1)
            act.wait_ge(var2_ok, at(0))
            a.activation(var2[:, :], var2[:, :], ACT.Sqrt).then_inc(sd2_ok, 1)
            with act.Fori(0, NBLK) as n:
                act.wait_ge(stb, at(n, NBLK))
                act.wait_ge(xb_ok, at(n))
                a.activation(Sx[:, :, 0:C], hn[:, :, :], ACT.Copy)
                a.activation(Sx[:, :, 2 * C:3 * C], hn[:, :, :], ACT.Copy).then_inc(xb1_ok, 1)
                act.wait_ge(stb, at(n, NBLK + 1))
                act.wait_ge(stb, 1)
                a.activation(ABf[:, bass.ts(n, 1), :, :].rearrange("p a s t -> p (a s) t"),
                             bank[0].bitcast(BF16).rearrange("p (s t) -> p s t", s=2), ACT.Copy).then_inc(abb_ok, 1)
            act.wait_ge(lm_ok, at(0))
            a.activation(pr[:, :, :], lg[:, :, :], ACT.Exp).then_inc(pe_ok, 1)
            with act.Fori(0, NBLK) as n:
                act.wait_ge(WT_ps, at(n))
                act.wait_ge(wb_ps, at(n, 0, NKT))
                a.activation(WT[:, :], bank[7].bitcast(BF16)[0:3 * EW, 0:BLK], ACT.Copy).then_inc(WT_ok, 1)
                for j in range(NKT):
                    m = min(P, NHID - j * P)
                    act.wait_ge(gu_ps, at(n, j + 1, NKT))
                    act.wait_ge(hu_ok, at(n, j - 1, NKT))
                    a.activation(sg[0:m, j % 2, :], bank[j % 2][0:m, :], ACT.Silu).then_inc(sg_ok, 1)
                act.wait_ge(w2_done, at(n, NKT, NKT))
                a.activation(yT[:, :], bank[6], ACT.Copy).then_inc(eT_ok, 1)

        @block.vector
        def _(dve):
            v = nc.vector
            v.memset(rTe[:, :], 0.0)
            v.memset(w3s[:, :, :, :], 0.0)
            v.memset(rTo[:, :], 0.0)
            v.memset(Cd[:, :, :], 0.0)
            v.memset(keep[:, :], 1.0)
            dve.drain()
            for s in range(1, NB + 1):
                v.memset(keep[:, s * BPS - 1:s * BPS], 0.0)
            dve.wait_ge(consts_in, at(0, 96, 16))
            v.tensor_scalar(dig[:, 0, :], xid[:, :], 63, None, ALU.bitwise_and)
            v.tensor_scalar(dig[:, 1, :], xid[:, :], 6, 63, ALU.logical_shift_right, ALU.bitwise_and)
            v.tensor_scalar(dig[:, 2, :], xid[:, :], 12, None, ALU.logical_shift_right)
            dve.drain()

            def reduce_mod(m):
                v.tensor_scalar(quo[:, :], hsh[:, :], 1.0 / m, None, ALU.mult)
                dve.drain()
                v.tensor_copy(quf[:, :], quo[:, :])
                dve.drain()
                v.scalar_tensor_tensor(hsh[:, :], quf[:, :], -float(m), hsh[:, :], ALU.mult, ALU.add)
                dve.drain()
                v.tensor_scalar(quf[:, :], hsh[:, :], 0.0, float(m), ALU.is_lt, ALU.mult)
                dve.drain()
                v.tensor_tensor(hsh[:, :], hsh[:, :], quf[:, :], ALU.add)
                dve.drain()
                v.tensor_scalar(quf[:, :], hsh[:, :], float(m), -float(m), ALU.is_ge, ALU.mult)
                dve.drain()
                v.tensor_tensor(hsh[:, :], hsh[:, :], quf[:, :], ALU.add)
                dve.drain()

            for i in range(2):
                c = [float(HASH_A[i] * 64 ** k % HASHP) for k in range(3)]
                v.tensor_scalar(hsh[:, :], dig[:, 2, :], c[2], float(HASH_B[i]), ALU.mult, ALU.add)
                dve.drain()
                v.scalar_tensor_tensor(hsh[:, :], dig[:, 1, :], c[1], hsh[:, :], ALU.mult, ALU.add)
                dve.drain()
                v.scalar_tensor_tensor(hsh[:, :], dig[:, 0, :], c[0], hsh[:, :], ALU.mult, ALU.add)
                dve.drain()
                reduce_mod(HASHP)
                reduce_mod(HASHM)
                v.tensor_scalar(hsh[:, :], hsh[:, :], float(IC), None, ALU.add)
                dve.drain()
                v.tensor_tensor(quf[:, :], xid[:, :], hsh[:, :], ALU.subtract)
                dve.drain()
                v.scalar_tensor_tensor(quf[:, :], xid[:, :], float(NSPECIAL), quf[:, :], ALU.is_lt, ALU.mult)
                dve.drain()
                v.tensor_tensor(rows[:, :, i], hsh[:, :], quf[:, :], ALU.add)
                dve.drain()
            v.tensor_scalar(rows[:, :, 2], xid[:, :], float(VOCAB - 1), None, ALU.min)
            dve.drain()
            v.tensor_copy(quf[:, :], quf[:, :]).then_inc(rows_ok, 1)

            for i, (_, dst, n) in enumerate(WEIGHTS):
                dve.wait_ge(weight_in, at(0, 16 * (i + 1), 16))
                v.tensor_copy(dst[:, 0, :], wtmp[:, 0:n])
                dve.drain()
                v.tensor_tensor(wres[:, 0:n], wtmp[:, 0:n], dst[:, 0, :], ALU.subtract).then_inc(weight_free, 1)
                v.tensor_copy(dst[C:P, 2, :], dst[C:P, 0, :])
                dve.drain()
                v.tensor_copy(dst[:, 1, :], wres[:, 0:n])
                dve.drain()
                v.tensor_tensor(dst[0:C, 2, :], wres[0:C, 0:n], dst[0:C, 1, :], ALU.subtract)
                dve.drain()
            v.tensor_copy(quf[:, :], quf[:, :]).then_inc(init_ok, 1)
            dve.wait_ge(masks_ok, at(0))

            def inv_norm(n, i, k, x, eps):
                v.tensor_tensor(sq[:, :, :], x, x, ALU.mult)
                dve.drain()
                v.tensor_reduce(st[:, 1, :], sq[:, :, :], AX, ALU.add)
                dve.drain()
                v.tensor_scalar(st[:, k, :], st[:, 1, :], 1.0 / C, eps, ALU.mult, ALU.add).then_inc(var_r, 1)
                dve.wait_ge(sd_r, at(n, i, 3))
                v.reciprocal(st[:, k, :], st[:, k, :])
                dve.drain()

            def center(x):
                v.tensor_reduce(st[:, 0, :], x, AX, ALU.add)
                dve.drain()
                v.tensor_scalar(st[:, 0, :], st[:, 0, :], -1.0 / C, None, ALU.mult)
                dve.drain()
                v.tensor_tensor(xc[:, :, :], x, bcast(st[:, 0, :], C), ALU.add)
                dve.drain()

            def split_rest(n, i, x):
                dve.wait_ge(x1_ok, at(n, i, 2))
                v.tensor_tensor(res[:, :, :], x, Sx[:, :, 0:C], ALU.subtract)
                dve.drain()
                v.tensor_copy(Sx[:, :, C:2 * C], res[:, :, :])
                dve.drain()
                v.tensor_tensor(Sx[:, :, 3 * C:4 * C], res[:, :, :], Sx[:, :, C:2 * C], ALU.subtract).then_inc(split_ok, 1)

            with dve.Fori(0, NBLK) as n:
                h0 = h_all[:, bass.ts(n, TPB), :]
                dve.wait_ge(gathered, 16 * 3 * TPB * (n + 1))
                v.tensor_tensor(t2[:, :, :, :], emb[:, :, :, :], bcast(embw[:, :, :], C), ALU.mult).then_inc(emb_used, 1)
                dve.drain()
                v.tensor_tensor(h0, t2[:, :, 0, :], t2[:, :, 1, :], ALU.add)
                dve.drain()
                center(h0)
                inv_norm(n, 1, 2, xc[:, :, :], EPS_LN)
                dve.wait_ge(g_ps, at(n, 0, TPB))
                v.tensor_tensor(rr[:, :, 0:C], xc[:, :, :], bcast(st[:, 2, :], C), ALU.mult).then_inc(xr_ok, 1)
                v.tensor_tensor(rr[:, :, C:2 * C], xc[:, :, :], bcast(st[:, 2, :], C), ALU.mult)
                dve.drain()
                split_rest(n, 1, rr[:, :, 0:C])
                dve.wait_ge(rT_ps, at(n))
                v.tensor_copy(rTe[0:C, :], bank[1][0:C, :])
                v.tensor_copy(rTo[C:P, :], bank[1][C:P, :]).then_inc(rT_ok, 1)
                dve.wait_ge(cup_ps, at(n))
                for c in range(TPB - 1):
                    for s in (slice(0, C), slice(C, P)):
                        last = v.tensor_tensor(Cd[s, c + 1, s], Cd[s, c, s], bank[1][s, c * C:(c + 1) * C], ALU.add)
                    dve.drain()
                last.then_inc(cup_ok, 1)
                for c in range(TPB):
                    for e in range(2):
                        dve.wait_ge(om_ps, at(n, 2 * c + e + 1, 2 * TPB))
                        if c:
                            dve.wait_ge(g_ps, at(n, c, TPB))
                        v.tensor_tensor(om[:, e, :, :], bank[4 + e].rearrange("p (a t) -> p a t", a=NPAIR),
                                        keep_t_ge_u[:, :].unsqueeze(1).to_broadcast([P, NPAIR, P]), ALU.mult).then_inc(om_ok, 1)
                    if c == 0:
                        dve.wait_ge(inter_done, at(n, 1, TPB))
                        for s in (slice(0, C), slice(C, P)):
                            v.tensor_tensor(Cd[s, 0, s], Cd[s, 3, s], bank[1][s, 3 * C:4 * C], ALU.add)
                        dve.drain()
                        for s in (slice(0, C), slice(C, P)):
                            last = v.tensor_scalar(Cd[s, 0, s], Cd[s, 0, s], keep[s, bass.ts(n, 1)], None, ALU.mult)
                        last.then_inc(cup_ok, 1)
                dve.wait_ge(on_ps, at(n))
                v.tensor_tensor(h0.rearrange("p (s m) d -> p m s d", s=2), h0.rearrange("p (s m) d -> p m s d", s=2),
                                bank[3][:, 0:2 * P].rearrange("p (m s d) -> p m s d", m=2, s=2), ALU.add).then_inc(on_ok, 1)
                dve.drain()
                center(h0)
                inv_norm(n, 2, 2, xc[:, :, :], EPS_LN)
                z = x_all[:, bass.ts(n, TPB), :]
                v.tensor_tensor(z, xc[:, :, :], bcast(st[:, 2, :], C), ALU.mult)
                dve.drain()
                inv_norm(n, 3, 3, z, EPS_RMS)
                v.tensor_tensor(xc[:, :, :], z, bcast(st[:, 3, :], C), ALU.mult)
                dve.drain()
                v.tensor_tensor(hn[:, :, :], xc[:, :, :], ln1b[:, :].unsqueeze(1).to_broadcast([P, TPB, C]), ALU.mult).then_inc(xr_ok, 1)
                dve.drain()
                split_rest(n, 2, hn[:, :, :])
                dve.wait_ge(qk_ps, at(n))
                dve.wait_ge(cs_in, at(n, 32, 32))
                v.tensor_tensor(rp[:, 1, :], bank[2][0:NQK, :], csb[:, 0, :], ALU.mult)
                v.tensor_tensor(rp[:, 2, :], bank[3][0:NQK, :], csb[:, 1, :], ALU.mult)
                dve.drain()
                v.tensor_tensor(rp[:, 0, :], rp[:, 1, :], rp[:, 2, :], ALU.add).then_inc(rope_ok, 1)
                dve.wait_ge(p1_ok, at(n))
                v.tensor_tensor(rp[:, 1, :], rp[:, 0, :], qkp[:, 0, :], ALU.subtract)
                dve.drain()
                v.tensor_copy(qkp[:, 1, :], rp[:, 1, :])
                dve.drain()
                v.tensor_tensor(qkp[:, 2, :], rp[:, 1, :], qkp[:, 1, :], ALU.subtract).then_inc(parts_ok, 1)

            for b in range(NB):
                def maxima(k, first, last):
                    for u in range(first, last):
                        i, h, c = M_UNITS[k][u]
                        r = M_BEFORE[k] + u
                        w = BLK if c < k else (i + 1) * P
                        dve.wait_ge(mx_ps, at(b, r + 1, NM))
                        v.tensor_reduce(mxc[:, h, i, c:c + 1], bank[4 + r % 2][:, 0:w], AX, ALU.max).then_inc(mx_ok, 1)
                    if last == len(M_UNITS[k]) and last > first:
                        dve.drain()
                        if k:
                            v.tensor_reduce(mneg[:, 0, :], mxc[:, :, :, 0:k + 1].rearrange("p h i c -> p (h i) c"), AX, ALU.max, negate=True)
                        else:
                            v.tensor_scalar(mneg[:, 0, :], mxc[:, :, :, 0].rearrange("p h i -> p (h i)"), -1.0, None, ALU.mult)
                        dve.drain()
                        dve.wait_ge(mt_ps, at(b, k, BPS))
                        v.tensor_copy(m3[:, 0, :], mneg[:, 0, :])
                        dve.drain()
                        v.tensor_tensor(mneg[:, 1, :], mneg[:, 0, :], m3[:, 0, :], ALU.subtract)
                        dve.drain()
                        v.tensor_copy(m3[:, 1, :], mneg[:, 1, :])
                        dve.drain()
                        v.tensor_tensor(m3[:, 2, :], mneg[:, 1, :], m3[:, 1, :], ALU.subtract).then_inc(m3_ok, 1)
                        dve.drain()

                maxima(0, 0, len(M_UNITS[0]))
                for k in range(BPS):
                    done = 0
                    for s in range(STEPS[k]):
                        upto = m_after(k, s)
                        if upto > done:
                            maxima(k + 1, done, upto)
                        done = upto
                    dve.wait_ge(yn_ps, at(b, k + 1, BPS))
                    yn = bank[6].rearrange("p (t h w) -> p t h w", t=TPB, h=NH)
                    v.reciprocal(rden[:, :, :], yn[:, :, :, HD])
                    dve.drain()
                    v.tensor_tensor(y_all[:, bass.ds(b * (T // P) + k * TPB, TPB), :].rearrange("p t (h d) -> p t h d", h=NH),
                                    yn[:, :, :, 0:HD], bcast(rden[:, :, :], HD), ALU.mult).then_inc(yn_ok, 1)
                    dve.drain()

            def split_rest_b(x):
                v.tensor_tensor(res[:, :, :], x, Sx[:, :, 0:C], ALU.subtract)
                dve.drain()
                v.tensor_copy(Sx[:, :, C:2 * C], res[:, :, :])
                dve.drain()
                v.tensor_tensor(Sx[:, :, 3 * C:4 * C], res[:, :, :], Sx[:, :, C:2 * C], ALU.subtract).then_inc(sb_ok, 1)
                dve.drain()

            with dve.Fori(0, NBLK) as n:
                dve.wait_ge(xb1_ok, at(n))
                split_rest_b(y_all[:, bass.ts(n, TPB), :])
                x = x_all[:, bass.ts(n, TPB), :]
                dve.wait_ge(wo_ps, at(n))
                v.tensor_tensor(x, x, bank[1][:, 0:TPB * C].rearrange("p (t c) -> p t c", t=TPB), ALU.add).then_inc(wo_ok, 1)
                dve.drain()
                v.tensor_tensor(sq[:, :, :], x, x, ALU.mult)
                dve.drain()
                v.tensor_reduce(var2[:, bass.ts(n, TPB)], sq[:, :, :], AX, ALU.add)
                dve.drain()
            v.tensor_scalar(var2[:, :], var2[:, :], 1.0 / C, EPS_RMS, ALU.mult, ALU.add).then_inc(var2_ok, 1)
            dve.wait_ge(sd2_ok, at(0))
            v.reciprocal(var2[:, :], var2[:, :])
            dve.drain()
            with dve.Fori(0, NBLK) as n:
                v.tensor_tensor(xc[:, :, :], x_all[:, bass.ts(n, TPB), :], bcast(var2[:, bass.ts(n, TPB)], C), ALU.mult)
                dve.drain()
                v.tensor_tensor(hn[:, :, :], xc[:, :, :], ln2b[:, :].unsqueeze(1).to_broadcast([P, TPB, C]), ALU.mult).then_inc(xb_ok, 1)
                dve.drain()
                dve.wait_ge(xb1_ok, at(n, NBLK + 1))
                split_rest_b(hn[:, :, :])
                dve.wait_ge(lg_ps, at(n))
                dve.wait_ge(lg_ps, 1)
                v.tensor_copy(lg[:, bass.ts(n, TPB), :], bank[1][:, 0:TPB * NE].rearrange("p (t c) -> p t c", t=TPB)).then_inc(lg_ok, 1)
                dve.drain()
            v.tensor_reduce(cols[:, 0, :], lg[:, :, :], AX, ALU.max)
            dve.drain()
            v.tensor_tensor(lg[:, :, :], lg[:, :, :], bcast(cols[:, 0, :], NE), ALU.subtract).then_inc(lm_ok, 1)
            dve.wait_ge(pe_ok, at(0))
            v.tensor_reduce(cols[:, 0, :], pr[:, :, :], AX, ALU.add)
            dve.drain()
            v.reciprocal(cols[:, 1, :], cols[:, 0, :])
            dve.drain()
            v.tensor_tensor(pr[:, :, :], pr[:, :, :], bcast(cols[:, 1, :], NE), ALU.mult)
            dve.drain()
            rk = rank[:, :].unsqueeze(1).to_broadcast([P, NT, NE])
            for i in range(2):
                v.tensor_reduce(cols[:, 1 + i, :], pr[:, :, :], AX, ALU.max)
                dve.drain()
                v.tensor_tensor(tk[:, :, :], pr[:, :, :], bcast(cols[:, 1 + i, :], NE), ALU.is_equal)
                dve.drain()
                v.tensor_tensor(tk[:, :, :], tk[:, :, :], rk, ALU.mult)
                dve.drain()
                v.tensor_reduce(cols[:, 0, :], tk[:, :, :], AX, ALU.max)
                dve.drain()
                v.tensor_tensor(tk[:, :, :], tk[:, :, :], bcast(cols[:, 0, :], NE), ALU.is_equal)
                dve.drain()
                if i == 0:
                    v.tensor_tensor(tr[:, :, :], tk[:, :, :], pr[:, :, :], ALU.mult)
                    dve.drain()
                    v.scalar_tensor_tensor(pr[:, :, :], tk[:, :, :], -2.0, pr[:, :, :], ALU.mult, ALU.add)
                    dve.drain()
                else:
                    v.tensor_tensor(tk[:, :, :], tk[:, :, :], pr[:, :, :], ALU.mult)
                    dve.drain()
                    v.tensor_tensor(tr[:, :, :], tk[:, :, :], tr[:, :, :], ALU.add)
                    v.scalar_tensor_tensor(cols[:, 0, :], cols[:, 1, :], 1e-9, cols[:, 2, :], ALU.add, ALU.add)
                    dve.drain()
            v.reciprocal(cols[:, 3, :], cols[:, 0, :])
            dve.drain()
            v.tensor_tensor(tr[:, :, :], tr[:, :, :], bcast(cols[:, 3, :], NE), ALU.mult)
            dve.drain()
            v.tensor_copy(w3s[:, :, 0, 0:NE], tr[:, :, :])
            dve.drain()
            v.tensor_tensor(tk[:, :, :], tr[:, :, :], w3s[:, :, 0, 0:NE], ALU.subtract)
            dve.drain()
            v.tensor_copy(w3s[:, :, 1, 0:NE], tk[:, :, :])
            dve.drain()
            v.tensor_tensor(w3s[:, :, 2, 0:NE], tk[:, :, :], w3s[:, :, 1, 0:NE], ALU.subtract).then_inc(w_ok, 1)
            with dve.Fori(0, NBLK) as n:
                for j in range(NKT):
                    m = min(P, NHID - j * P)
                    dve.wait_ge(sg_ok, at(n, j + 1, NKT))
                    v.tensor_tensor(hu[0:m, j % 2, :], sg[0:m, j % 2, :], bank[2 + j % 2][0:m, :], ALU.mult).then_inc(hu_ok, 1)
                    dve.drain()
                    dve.wait_ge(wb_ps, at(n, j + 1, NKT))
                    dve.wait_ge(w2_done, at(n, j - 1, NKT))
                    v.tensor_tensor(hh[0:m, j % 2, :], hu[0:m, j % 2, :], bank[4 + j % 2][0:m, :], ALU.mult).then_inc(hh_ok, 1)
                dve.wait_ge(en_ps, at(n))
                en = bank[7].rearrange("p (t s c) -> p t s c", t=TPB, s=2)
                v.tensor_tensor(xc[:, :, :], x_all[:, bass.ts(n, TPB), :], en[:, :, 0, :], ALU.add)
                dve.drain()
                v.tensor_tensor(sq[:, :, :], xc[:, :, :], en[:, :, 1, :], ALU.add)
                dve.drain()
                dve.wait_ge(out_done, at(n, 0, 16))
                v.tensor_tensor(fin[:, :, :], sq[:, :, :], h_all[:, bass.ts(n, TPB), :], ALU.add).then_inc(fin_ok, 1)
                dve.drain()

        @block.tensor
        def _(pe):
            mm = nc.tensor.matmul

            def stack_transposes(n, i):
                pe.wait_ge(split_ok, at(n, i, 2))
                pe.wait_ge(ab_ok, at(n, i - 1, 2))
                dst = bank[0].bitcast(BF16).rearrange("p (s t) -> p s t", s=2)
                for t in range(TPB):
                    for s in range(2):
                        last = nc.tensor.transpose(dst[:, s, t * P:(t + 1) * P], Sx[:, t, s * P:(s + 1) * P], identb[:, :])
                last.then_inc(stacked, 1)

            def split3(dst, w, cols, x):
                for k in range(3):
                    last = mm(dst, w[:, k, cols], AB[:, k // 2, x], start=(k == 0), stop=(k == 2))
                return last

            pe.wait_ge(init_ok, at(0))
            pe.wait_ge(masks_ok, at(0))
            pe.wait_ge(consts_in, at(0, 96, 16))
            with pe.Fori(0, NBLK) as n:
                stack_transposes(n, 1)
                pe.wait_ge(v_ok, at(n, 0))
                for t in range(TPB):
                    last = nc.tensor.transpose(bank[1][:, t * P:(t + 1) * P], rr[:, t, :], ident[:, :])
                last.then_inc(rT_ps, 1)
                pe.wait_ge(ab_ok, at(n, 1, 2))
                pe.wait_ge(rope_ok, at(n, 0))
                for p in range(NPAIR):
                    if p >= 2:
                        pe.wait_ge(qh_ok, at(n, p - 1, NPAIR))
                    last = split3(bank[2 + p % 2], lq3, slice(p * P, (p + 1) * P), slice(0, BLK))
                    last.then_inc(qh_ps, 1)
                pe.wait_ge(rT_ok, at(n))
                for c in range(TPB):
                    last = mm(bank[1][:, c * C:(c + 1) * C], rr[:, c, :], rr[:, c, 0:C], start=True, stop=True)
                last.then_inc(cup_ps, 1)
                pe.wait_ge(qh_ok, at(n, NPAIR, NPAIR))

                def omega(c):
                    for e, rT in enumerate((rTe, rTo)):
                        pe.wait_ge(om_ok, at(n, 2 * (c - 1) + e + 1, 2 * TPB))
                        last = mm(bank[4 + e], rT[:, c * P:(c + 1) * P], qh[:, :, c * P:(c + 1) * P], start=True, stop=True)
                        last.then_inc(om_ps, 1)

                omega(0)
                pe.wait_ge(cup_ok, at(n, 1, 2))
                for c in range(TPB):
                    pe.wait_ge(g_ok, at(n, c - 1, TPB))
                    mm(bank[6 + c % 2], Cd[:, c, :], qh[:, :, c * P:(c + 1) * P], start=True, stop=False).then_inc(inter_done, 1)
                    if c + 1 < TPB:
                        omega(c + 1)
                    for e in range(2):
                        pe.wait_ge(om_ok, at(n, 2 * c + e + 1, 2 * TPB))
                        last = mm(bank[6 + c % 2][e * C:(e + 1) * C, :], rr[:, c, 0:C], om[:, e, :, :], start=False, stop=True)
                    last.then_inc(g_ps, 1)
                pe.wait_ge(g_ok, at(n, TPB, TPB))
                for p in range(NPAIR):
                    for s in range(2):
                        last = mm(bank[2][s * C:(s + 1) * C, 0:2 * P], leS[:, p, :], Gs[:, p, s * 2 * P:(s + 1) * 2 * P],
                                  start=(p == 0), stop=(p == NPAIR - 1))
                last.then_inc(oT_ps, 1)
                pe.wait_ge(oT_ok, at(n))
                for m in range(2):
                    last = nc.tensor.transpose(bank[3][:, m * P:(m + 1) * P], oT[:, m * P:(m + 1) * P], ident[:, :])
                last.then_inc(on_ps, 1)
                stack_transposes(n, 2)
                pe.wait_ge(ab_ok, at(n, 2, 2))
                split3(bank[2][0:NQK, :], wqk3, slice(0, NQK), slice(0, BLK))
                pe.wait_ge(on_ok, at(n))
                split3(bank[3][0:NQK, :], wqk3, slice(NQK, 2 * NQK), slice(0, BLK)).then_inc(qk_ps, 1)
                pe.wait_ge(cup_ok, at(n, 2, 2))
                for t in range(TPB):
                    for k in range(3):
                        last = mm(bank[1][:, t * NKV * HD:(t + 1) * NKV * HD], AB[:, k // 2, t * P:(t + 1) * P], wv3[:, k, :],
                                  start=(k == 0), stop=(k == 2))
                last.then_inc(v_ps, 1)

            pe.wait_ge(rope_ok, at(NBLK - 1))
            pe.wait_ge(v_ok, at(NBLK - 1))
            for b in range(NB):
                def max_units(k, first, last):
                    if first == 0:
                        pe.wait_ge(qk_in, at(b, 12 * 16 * (k + 1), 12 * 16 * BPS))
                    for u in range(first, last):
                        i, h, c = M_UNITS[k][u]
                        r = M_BEFORE[k] + u
                        w = BLK if c < k else (i + 1) * P
                        pe.wait_ge(mx_ok, at(b, r - 1, NM) if r >= 2 else at(b, 0, NM))
                        dst = bank[4 + r % 2]
                        last_mm = mm(dst[:, 0:w], Qs[0:KSC, b * BPS + k, h, i * P:(i + 1) * P],
                                     Ks[0:KSC, b * BPS + c, h // 2, 0:w], start=True, stop=(c < k))
                        if c == k:
                            last_mm = mm(dst[:, i * P:(i + 1) * P], identb[:, :], neg_t_lt_s[:, :], start=False, stop=True)
                        last_mm.then_inc(mx_ps, 1)

                def max_transpose(k):
                    pe.wait_ge(m3_ok, at(b, k + 1, BPS))
                    pe.wait_ge(yn_ok, at(b, max(0, k - 1), BPS))
                    nc.tensor.transpose(bank[6].bitcast(BF16)[0:3 * NH * TPB, 0:P], m3[:, :, :].rearrange("p g c -> p (g c)"),
                                        identb[:, :]).then_inc(mt_ps, 1)

                def score(k, s, hp):
                    i = S_BEFORE[k] + s
                    d = s - TPB * k
                    off = max(0, d) * P
                    pe.wait_ge(exp_ok, at(b, max(0, 2 * (i - 1) + hp + 1), 2 * NS))
                    for h in (2 * hp, 2 * hp + 1):
                        last = mm(ps[:, h, off:], Ks[:, b * BPS + s // TPB, hp, s % TPB * P:(s % TPB + 1) * P],
                                  Qs[:, b * BPS + k, h, off:], start=True, stop=(d < 0))
                        if d >= 0:
                            last = mm(ps[:, h, off:off + P], identb[:, :], neg_s_gt_t[:, :], start=False, stop=True)
                    last.then_inc(st_ps, 1)

                def weigh(k, s):
                    i = S_BEFORE[k] + s
                    off = max(0, s - TPB * k) * P
                    pe.wait_ge(exp_ok, at(b, 2 * i + 2, 2 * NS))
                    if s == 0:
                        pe.wait_ge(yT_ok, at(b, k, BPS))
                    for h in range(NH):
                        last = mm(bank[7][h * VW:(h + 1) * VW, off:], Vn[:, b * (T // P) + s, h // 2 * VW:(h // 2 + 1) * VW],
                                  pexp[:, i % 2, h, off:], start=(s == 0), stop=(s == STEPS[k] - 1))
                    last.then_inc(pv_ok, 1)

                max_units(0, 0, len(M_UNITS[0]))
                max_transpose(0)
                for k in range(BPS):
                    pe.wait_ge(m_in, at(b, 48 * (k + 1), 48 * BPS))
                    done = 0
                    for s in range(STEPS[k]):
                        upto = m_after(k, s)
                        half = (done + upto) // 2
                        score(k, s, 0)
                        if half > done:
                            max_units(k + 1, done, half)
                        score(k, s, 1)
                        if s:
                            weigh(k, s - 1)
                        if upto > half:
                            max_units(k + 1, half, upto)
                        done = upto
                        if s == STEPS[k] - 2 and k + 1 < BPS:
                            max_transpose(k + 1)
                    weigh(k, STEPS[k] - 1)
                    pe.wait_ge(yT_ok, at(b, k + 1, BPS))
                    pe.wait_ge(yn_ok, at(b, k, BPS))
                    if k + 1 < BPS:
                        pe.wait_ge(mrow_ok, at(b, k + 2, BPS))
                    for t in range(TPB):
                        last = nc.tensor.transpose(bank[6][:, t * P:(t + 1) * P], yT[:, t * P:(t + 1) * P], ident[:, :])
                    last.then_inc(yn_ps, 1)

            def stack_transposes_b(n, r):
                pe.wait_ge(sb_ok, at(n, r + 1))
                pe.wait_ge(abb_ok, at(n, r))
                dst = bank[0].bitcast(BF16).rearrange("p (s t) -> p s t", s=2)
                for t in range(TPB):
                    for s in range(2):
                        last = nc.tensor.transpose(dst[:, s, t * P:(t + 1) * P], Sx[:, t, s * P:(s + 1) * P], identb[:, :])
                last.then_inc(stb, 1)

            pe.wait_ge(exp_ok, at(NB - 1, 2 * NS, 2 * NS))
            with pe.Fori(0, NBLK) as n:
                stack_transposes_b(n, 0)
                pe.wait_ge(abb_ok, at(n))
                pe.wait_ge(wo_ok, at(n, 0))
                for t in range(TPB):
                    for i in range(3):
                        last = mm(bank[1][:, t * C:(t + 1) * C], AB[:, i // 2, t * P:(t + 1) * P], wo3[:, i, :], start=(i == 0), stop=(i == 2))
                last.then_inc(wo_ps, 1)
            pe.wait_ge(wo_ok, at(NBLK - 1))
            with pe.Fori(0, NBLK) as n:
                stack_transposes_b(n, NBLK)
                pe.wait_ge(abb_ok, at(n, NBLK + 1))
                pe.wait_ge(lg_ok, at(n, 0))
                for t in range(TPB):
                    for i in range(3):
                        last = mm(bank[1][:, t * NE:(t + 1) * NE], ABf[:, bass.ts(n, 1), i // 2, t * P:(t + 1) * P].rearrange("p a t -> p (a t)"),
                                  wr3[:, i, :], start=(i == 0), stop=(i == 2))
                last.then_inc(lg_ps, 1)

            pe.wait_ge(w_ok, at(0))
            with pe.Fori(0, NBLK) as n:
                pe.wait_ge(fin_ok, at(n, 0))
                for t in range(TPB):
                    last = nc.tensor.transpose(bank[7].bitcast(BF16)[0:3 * EW, t * P:(t + 1) * P],
                                               w3s[:, bass.ds(n * TPB + t, 1), :, :].rearrange("p a g e -> p (a g e)"), identb[:, :])
                last.then_inc(WT_ps, 1)
                pe.wait_ge(WT_ok, at(n))

                def down(j):
                    m = min(P, NHID - j * P)
                    s = j % 2 * C
                    pe.wait_ge(hh_ok, at(n, j + 1, NKT))
                    if j == 0:
                        pe.wait_ge(eT_ok, at(n, 0))
                    mm(bank[6][s:s + C, :], w2S[0:m, j, :], hh[0:m, j % 2, :], start=(j < 2), stop=(j >= NKT - 2)).then_inc(w2_done, 1)

                for j in range(NKT):
                    m = min(P, NHID - j * P)
                    pe.wait_ge(hu_ok, at(n, j - 1, NKT))
                    for dst, w in ((bank[j % 2], w13), (bank[2 + j % 2], w33)):
                        for i in range(3):
                            last = mm(dst[0:m, :], w[:, i, j * P:j * P + m], ABf[:, bass.ts(n, 1), i // 2, :].rearrange("p a t -> p (a t)"),
                                      start=(i == 0), stop=(i == 2))
                    last.then_inc(gu_ps, 1)
                    pe.wait_ge(hh_ok, at(n, j - 1, NKT))
                    mm(bank[4 + j % 2][0:m, :], selb[:, j * P:j * P + m], WT[:, :], start=True, stop=True).then_inc(wb_ps, 1)
                    if j:
                        down(j - 1)
                down(NKT - 1)
                pe.wait_ge(eT_ok, at(n))
                for t in range(TPB):
                    last = nc.tensor.transpose(bank[7][:, t * P:(t + 1) * P], yT[:, t * P:(t + 1) * P], ident[:, :])
                last.then_inc(en_ps, 1)


def rope_tables():
    import numpy as np
    inv_freq = 1.0 / 10000.0 ** (np.arange(0, HD, 2, dtype=np.float32) / HD)
    freqs = np.outer(np.arange(T, dtype=np.float32), inv_freq)
    emb = np.concatenate([freqs, freqs], axis=-1)
    cos, sin = np.cos(emb).astype(np.float32), np.sin(emb).astype(np.float32)
    sin = np.concatenate([-sin[:, :HD // 2], sin[:, HD // 2:]], axis=-1)
    return [np.ascontiguousarray(np.tile(x.T, (NH + NKV, NB))) for x in (cos, sin)]


def kernel(x, L0_tok_shared_embedding, L0_tok_hash_weights_table, L0_attn_Q, L0_attn_E, L0_ffn_ln1_w, L0_ffn_ln2_w,
           L0_ffn_wq, L0_ffn_wk, L0_ffn_wv, L0_ffn_wo, L0_ffn_router_w, L0_ffn_w1, L0_ffn_w2, L0_ffn_w3):
    import ml_dtypes
    import numpy as np
    import concourse.bacc as bacc
    from concourse.bass_utils import run_bass_kernel_spmd

    def twice(w):
        return np.concatenate([w, w], axis=0)

    qk = np.concatenate([L0_ffn_wq, L0_ffn_wk], axis=0)
    rot = np.roll(qk.reshape(NH + NKV, 2, HD // 2, C), 1, axis=1).reshape(NQK, C)
    w2 = np.zeros((NKT * P, C), np.float32)
    w2[:NHID] = L0_ffn_w2.transpose(0, 2, 1).reshape(NHID, C)
    cos, sin = rope_tables()
    arrays = {
        "ids": x.reshape(NT, P).T,
        "table": L0_tok_shared_embedding,
        "hash_w": L0_tok_hash_weights_table,
        "lq": twice(L0_attn_Q.transpose(1, 0, 2).reshape(C, LH * C)),
        "le": L0_attn_E.reshape(NPAIR, 2, C, C).transpose(1, 3, 0, 2).reshape(P, NPAIR, C),
        "ln1": L0_ffn_ln1_w.reshape(1, C),
        "ln2": L0_ffn_ln2_w.reshape(1, C),
        "wqk": twice(qk.T),
        "wrot": twice(rot.T),
        "wv": twice(L0_ffn_wv.T),
        "wo": twice(L0_ffn_wo.T),
        "wr": twice(L0_ffn_router_w.T),
        "w1": twice(L0_ffn_w1.reshape(NHID, C).T),
        "w3": twice(L0_ffn_w3.reshape(NHID, C).T),
        "w2": w2.reshape(NKT, P, C).transpose(1, 0, 2),
        "sel": np.tile(np.arange(NKT * P)[None, :] // HID == np.arange(EW)[:, None], (3, 1)).astype(ml_dtypes.bfloat16),
        "cos": cos,
        "sin": sin,
    }
    arrays = {k: np.ascontiguousarray(a) for k, a in arrays.items()}
    nc = bacc.Bacc("TRN2", target_bir_lowering=False, num_devices=1)
    args = [nc.dram_tensor(k, a.shape, mybir.dt.from_np(a.dtype), kind="ExternalInput").ap() for k, a in arrays.items()]
    out = nc.dram_tensor("out", (NB, T, C), F32, kind="ExternalOutput").ap()
    program(nc, *args, out)
    r = run_bass_kernel_spmd(nc, [arrays], core_ids=[0])
    return r.results[0]["out"]
```

```python
from contextlib import ExitStack

import concourse.bass as bass
from concourse import mybir

F32 = mybir.dt.float32
BF16 = mybir.dt.bfloat16
I32 = mybir.dt.int32
U32 = mybir.dt.uint32
ALU = mybir.AluOpType
ACT = mybir.ActivationFunctionType
AX = mybir.AxisListType.X

P = 128
C = 64
NB, T = 2, 2048
BLK = 512
TPB = BLK // P
NBLK = NB * T // BLK
BPS = T // BLK
NT = NB * T // P
LH = 8
NPAIR = LH // 2
NH, NKV, HD = 4, 2, 16
VW = 32
NQK = (NH + NKV) * HD
NTERM = 6
KSC = NTERM * HD
KROWS = KSC + 3
QPART = [0, 0, 1, 1, 0, 2]
KPART = [0, 1, 0, 1, 2, 0]
NE, HID = 8, 170
EW = 32
NHID = NE * HID
NKT = (NHID + P - 1) // P
HASHP, HASHM, IC, NSPECIAL, VOCAB = 100003, 12500, 4, 4, 25000
HASH_A, HASH_B = (12345, 20011), (6789, 54321)
EPS_LN, EPS_RMS = 1e-5, 1e-6
NEG = -1e30


def at(n, k=1, per=1):
    return per * n + k + 1


def wait(eng, s, value):
    if not (isinstance(value, int) and value < 2):
        eng.wait_ge(s, value)


def bcast(ap, n):
    return ap.unsqueeze(len(ap.shape)).to_broadcast([*ap.shape, n])


def program(nc, ids, table, hash_w, lq, le, ln1, ln2, wqk, wrot, wv, wo, wr, w1, w3, w2, sel, cos, sin, out):
    with ExitStack() as ctx:
        def sb(name, shape, dt=F32):
            return ctx.enter_context(nc.sbuf_tensor(name, shape, dt))

        sems = []

        def sem(name, first=1):
            s = ctx.enter_context(nc.semaphore(name))
            if first:
                sems.append(s)
            return s

        ps = ctx.enter_context(nc.psum_tensor("ps", [P, 8, 512], F32))
        bank = [ps[:, i, :] for i in range(8)]
        parts_dram = nc.dram_tensor("qk_parts", (NBLK, NQK, 3, BLK), BF16, kind="Internal").ap()

        ident = sb("ident", [P, P])
        identb = sb("identb", [P, P], BF16)
        keep_t_ge_u = sb("keep_t_ge_u", [P, P])
        h_all = sb("h_all", [P, NT, C])
        x_all = sb("x_all", [P, NT, C])
        Qs = sb("Qs", [KROWS, NBLK, NH, BLK], BF16)
        Ks = sb("Ks", [KROWS, NBLK, NKV, BLK], BF16)
        Vn = sb("Vn", [P, NT, NKV * VW])
        xid = sb("xid", [P, NT], I32)
        dig = sb("dig", [P, 3, NT], I32)
        hsh = sb("hsh", [P, 2, NT])
        quo = sb("quo", [P, 2, NT], I32)
        quf = sb("quf", [P, 2, NT])
        rows = sb("rows", [P, NT, 3], U32)
        emb = sb("emb", [P, TPB, 2, C])
        embw = sb("embw", [P, TPB, 2])
        t2 = sb("t2", [P, TPB, 2, C])
        xc = sb("xc", [P, TPB, C])
        sq = sb("sq", [P, TPB, C])
        st = sb("st", [P, 5, TPB])
        rn = sb("rn", [P, TPB, C])
        xp = t2[:, :, 0, :]
        rr = sb("rr", [P, TPB, 2 * C])
        res = sb("res", [P, TPB, C])
        Sx = sb("Sx", [P, TPB, 4 * C], BF16)
        AB = sb("AB", [P, 2, BLK], BF16)
        rTe = sb("rTe", [P, BLK])
        rTo = sb("rTo", [P, BLK])
        products = sb("products", [P, 2 * NPAIR, BLK])
        qh = products[:, 0:NPAIR, :]
        om = sb("om", [P, 2, NPAIR, P])
        Gs = products[:, NPAIR:, :]
        oT = sb("oT", [P, 2 * P])
        Cd = sb("Cd", [P, TPB, P])
        keep = sb("keep", [P, NBLK])
        hn = sb("hn", [P, TPB, C])
        ln1b = sb("ln1b", [P, C])
        csb = sb("csb", [NQK, 2, BLK])
        rp = sb("rp", [NQK, 4, BLK])
        qkp = sb("qkp", [NQK, 3, BLK], BF16)
        wtmp = sb("wtmp", [P, NHID])
        wres = sb("wres", [P, NHID])

        def weight3(name, n):
            return sb(name, [P, 3, n], BF16)

        lq3 = weight3("lq3", NPAIR * P)
        wqk3 = weight3("wqk3", 2 * NQK)
        wv3 = weight3("wv3", NKV * HD)
        wo3 = weight3("wo3", C)
        wr3 = weight3("wr3", NE)
        w13 = weight3("w13", NHID)
        w33 = weight3("w33", NHID)
        leS = sb("leS", [P, NPAIR, C])
        w2S = sb("w2S", [P, NKT, C])
        ln2b = sb("ln2b", [P, C])
        selb = sb("selb", [3 * EW, NKT * P], BF16)
        neg_t_lt_s = sb("neg_t_lt_s", [P, P], BF16)
        neg_s_gt_t = sb("neg_s_gt_t", [P, P], BF16)
        mxc = sb("mxc", [P, NH, TPB, BPS])
        mneg = sb("mneg", [P, 2, NH * TPB])
        m3 = sb("m3", [P, 3, NH * TPB], BF16)
        mrow = sb("mrow", [3 * NH * TPB, P], BF16)
        pexp = sb("pexp", [P, 2, NH, BLK])
        yT = rTe
        rden = sb("rden", [P, TPB, NH])
        y_all = sb("y_all", [P, NT, C])
        ABf = products[:, :, :].bitcast(BF16).rearrange("p a (s t) -> p a s t", s=2)
        var2 = sb("var2", [P, NT])
        lg = sb("lg", [P, NT, NE])
        pr = sb("pr", [P, NT, NE])
        tk = sb("tk", [P, NT, NE])
        tr = sb("tr", [P, NT, NE])
        cols = sb("cols", [P, 4, NT])
        rank = sb("rank", [P, NE])
        w3s = sb("w3s", [P, NT, 3, EW], BF16)
        WT = rp[:, :, :].bitcast(BF16).rearrange("p a (s t) -> p (a s) t", s=2)
        sg, hu, hh = pexp[:, 0, 0:2, :], pexp[:, 0, 2:4, :], pexp[:, 1, :, :]
        SLOTS = NH
        fin = rn

        consts_in = sem("consts_in")
        weight_in = sem("weight_in")
        weight_free = sem("weight_free")
        dve_w = sem("dve_w")
        masks_ok = sem("masks_ok")
        init_ok, late_ok = sem("init_ok"), sem("late_ok")
        rows_ok = sem("rows_ok")
        gathered = sem("gathered", first=0)
        emb_used = sem("emb_used")
        var_r = [sem(f"var_r{i}") for i in range(3)]
        xr_ok, x1_ok, split_ok, stacked, ab_ok = ([sem(f"{x}{i}") for i in range(2)] for x in ("xr_ok", "x1_ok", "split_ok", "stacked", "ab_ok"))
        sd_r = [sem(f"sd_r{i}") for i in range(3)]
        rr_ok, sum_ok = sem("rr_ok"), sem("sum_ok")
        rT_ps, rT_ok = sem("rT_ps"), sem("rT_ok")
        cup_ps, cup_ok = sem("cup_ps"), sem("cup_ok")
        qh_ps, qh_ok = sem("qh_ps"), sem("qh_ok")
        om_ps, om_ok = sem("om_ps"), sem("om_ok")
        g_ps, g_ok = sem("g_ps"), sem("g_ok")
        inter_done = sem("inter_done")
        oT_ps, oT_ok = sem("oT_ps"), sem("oT_ok")
        on_ps, on_ok = sem("on_ps"), sem("on_ok")
        qk_ps, v_ps, rope_ok, v_ok = sem("qk_ps"), sem("v_ps"), sem("rope_ok"), sem("v_ok")
        cs_in = sem("cs_in")
        parts_ok = sem("parts_ok")
        parts_out, qk_in = sem("parts_out"), sem("qk_in")
        out_done = sem("out_done")
        qs_free = sem("qs_free")
        mx_ps, mx_ok, m3_ok, mt_ps, mrow_ok, m_in = sem("mx_ps"), sem("mx_ok"), sem("m3_ok"), sem("mt_ps"), sem("mrow_ok"), sem("m_in")
        st_ps, exp_ok, pv_ok = sem("st_ps"), sem("exp_ok"), sem("pv_ok")
        yT_ps, yT_ok, yn_ps, yn_ok = sem("yT_ps"), sem("yT_ok"), sem("yn_ps"), sem("yn_ok")
        xb_ok, xb1_ok, sb_ok, stb, abb_ok = sem("xb_ok"), sem("xb1_ok"), sem("sb_ok"), sem("stb"), sem("abb_ok")
        wo_ps, wo_ok = sem("wo_ps"), sem("wo_ok")
        var2_ok, sd2_ok = sem("var2_ok"), sem("sd2_ok")
        lg_ps, lg_ok, lm_ok, pe_ok, w_ok = sem("lg_ps"), sem("lg_ok"), sem("lm_ok"), sem("pe_ok"), sem("w_ok")
        WT_ps, WT_ok = sem("WT_ps"), sem("WT_ok")
        gu_ps, wb_ps, sg_ok, hu_ok, hh_ok, w2_done = sem("gu_ps"), sem("wb_ps"), sem("sg_ok"), sem("hu_ok"), sem("hh_ok"), sem("w2_done")
        eT_ok, en_ps, en_ok, fin_ok = sem("eT_ok"), sem("en_ps"), sem("en_ok"), sem("fin_ok")

        block = ctx.enter_context(nc.Block())
        outv = out.rearrange("b (t p) c -> p (b t) c", p=P)
        WEIGHTS = [(lq, lq3, NPAIR * P), (wqk, wqk3[:, :, 0:NQK], NQK), (wrot, wqk3[:, :, NQK:], NQK), (wv, wv3, NKV * HD),
                   (wo, wo3, C), (wr, wr3, NE), (w1, w13, NHID), (w3, w33, NHID)]
        WEIGHTS_A = 4
        STEPS = [(i, s) for i in range(NBLK) for s in range(TPB * (i % BPS + 1))]
        LAST = [max(g for g, (i, _) in enumerate(STEPS) if i == k) for k in range(NBLK)]
        UNITS = []
        for j in range(NBLK):
            for t in range(TPB):
                UNITS += [(j, t, h, 1, c) for h in range(NH) for c in range(j % BPS)]
                together = TPB // (t + 1)
                UNITS += [(j, t, h, together, j % BPS) for h in range(0, NH, together)]
        U_END = [sum(1 for u in UNITS if u[0] <= j) for j in range(NBLK)]

        EARLY = 2

        def attention_bank(i):
            return 6 if i < NBLK - 1 else 7

        def router_bank(i):
            return 6 if i < BPS else 7

        def unit_bank(u):
            return bank[(6, 7, 4, 5)[u % 4]] if u < U_END[0] else bank[4 + u % 2]

        def step_cost(g):
            i, s = STEPS[g]
            return (NH * 2 + 1) * (BLK - max(0, s - TPB * (i % BPS)) * P)

        def plan_units():
            due = [(max(LAST[j - 1] - 2, 1), U_END[j]) for j in range(1, NBLK)]
            done, out = U_END[0] + EARLY, []
            for g in range(len(STEPS)):
                ahead = [(u - done) * step_cost(g) / sum(map(step_cost, range(g, d))) for d, u in due if d > g]
                n = int(max([0, *ahead]) + 0.999)
                out.append((done, done + n))
                done += n
            return out

        IN_STEP = plan_units()
        TOP_TWO = ("top_shares", "top_first", "top_second", "top_split")
        FLUSH = 16
        EVENTS = {e: [[] for _ in range(len(STEPS) + FLUSH)] for e in ("pe", "act", "dve")}
        bank6_steps = set()
        splits_free = 0

        def put(name, i, **steps):
            for engine, g in steps.items():
                EVENTS[engine][g].append((name, i))

        def free_step(g):
            while g in bank6_steps:
                g += 1
            bank6_steps.add(g)
            return g

        def put_y(i, g):
            nonlocal splits_free
            put("norm", i, act=g + 1)
            turned = free_step(g + 2)
            copied = max(turned + 1, splits_free)
            put("norm", i, pe=turned, dve=turned + 1)
            stacked = free_step(copied + 2)
            put("y_copy", i, act=copied, dve=copied + 2)
            put("y_stack", i, pe=stacked, act=stacked + 1)
            product = free_step(stacked + 2)
            put("y_product", i, pe=product)
            put("y_sum", i, dve=product + 1)
            splits_free = stacked + 1
            return product + 1

        def put_x(i, g):
            nonlocal splits_free
            start = max(g, splits_free)
            put("x_norm", i, dve=start)
            stacked = free_step(start + 2)
            put("x_copy", i, act=start, dve=start + 2)
            put("x_stack", i, pe=stacked, act=stacked + 1)
            product = free_step(stacked + 2)
            put("x_product", i, pe=product)
            put("x_keep", i, dve=product + 1)
            splits_free = stacked + 1
            return product + 1

        for j in range(1, NBLK):
            g = free_step(next(g for g, (_, u) in enumerate(IN_STEP) if u >= U_END[j]))
            put("row", j, pe=g, act=g + 1)
        for i in range(BPS):
            summed = put_y(i, LAST[i])
        put("root", 0, dve=summed, act=summed)
        put("inverse", 0, dve=summed + 1)
        routed = summed + 1
        put_y(BPS, LAST[BPS])
        for i in range(BPS):
            routed = put_x(i, summed + 1)
        put("top_exp", 0, dve=routed, act=routed + 1)
        for d, name in enumerate(TOP_TWO):
            put(name, 0, dve=routed + 2 + 2 * d)
        for i in range(BPS):
            g = free_step(routed + 3 + 2 * len(TOP_TWO))
            put("turn", i, pe=g, act=g + 1)
        for i in range(BPS + 1, NBLK - 1):
            put_y(i, LAST[i])
        FINISH_AT = 3
        TILE_EVENTS = {e: [[] for _ in range(BPS * NKT)] for e in ("pe", "act", "dve")}
        bank7_tiles = {n * NKT + FINISH_AT for n in range(1, BPS)}

        def beside(name, i, **tiles):
            for engine, g in tiles.items():
                TILE_EVENTS[engine][g].append((name, i))

        def free_tile(g):
            while g in bank7_tiles:
                g += 1
            bank7_tiles.add(g)
            return g

        beside("norm", NBLK - 1, pe=free_tile(0), dve=0)
        beside("y_copy", NBLK - 1, act=1, dve=2)
        stack_at = free_tile(3)
        beside("y_stack", NBLK - 1, pe=stack_at, act=stack_at + 1)
        product_at = free_tile(stack_at + 2)
        beside("y_product", NBLK - 1, pe=product_at)
        beside("y_sum", NBLK - 1, dve=product_at)
        beside("root", 1, dve=product_at, act=product_at + 1)
        beside("inverse", 1, dve=product_at + 2)
        x_at = product_at + 2
        for i in range(BPS, NBLK):
            beside("x_norm", i, dve=x_at)
            beside("x_copy", i, act=x_at + 2, dve=x_at + 2)
            stack_at = free_tile(x_at + 4)
            beside("x_stack", i, pe=stack_at, act=stack_at + 1)
            product_at = free_tile(stack_at + 2)
            beside("x_product", i, pe=product_at)
            beside("x_keep", i, dve=product_at)
            x_at = stack_at - 1
        beside("top_exp", 1, dve=product_at, act=product_at + 1)
        for d, name in enumerate(TOP_TWO):
            beside(name, 1, dve=product_at + 2 + d)
        for i in range(BPS, NBLK):
            g = free_tile(product_at + 4 + len(TOP_TWO))
            beside("turn", i, pe=g, act=g + 1)
        ROUND = {(e[0], i): r for r, (e, i) in enumerate([x for ev in (*EVENTS["act"], *TILE_EVENTS["act"]) for x in ev if x[0] in ("y_copy", "x_copy")])}

        @block.sync
        def _(sp):
            for s in sems:
                sp.sem_inc(s, 1)
            sp.dma_start(xid[:, :], ids).then_inc(consts_in, 16)
            sp.dma_start(leS[:, :, :], le).then_inc(consts_in, 16)
            sp.dma_start(ln1b[:, :], ln1.to_broadcast([P, C])).then_inc(consts_in, 16)
            sp.dma_start(ln2b[:, :], ln2.to_broadcast([P, C])).then_inc(consts_in, 16)
            sp.dma_start(w2S[:, :, :], w2).then_inc(consts_in, 16)
            sp.dma_start(selb[:, :], sel).then_inc(consts_in, 16)

            def load_weights(first, last):
                for i in range(first, last):
                    src, _, n = WEIGHTS[i]
                    wait(sp, weight_free, at(i - 1))
                    sp.dma_start(wtmp[:, 0:n], src).then_inc(weight_in, 16)

            load_weights(0, WEIGHTS_A)
            with sp.Fori(0, NBLK) as n:
                sp.wait_ge(rope_ok, at(n, 0, 2))
                sp.dma_start(csb[:, 0, :], cos[:, bass.ts(n, BLK)]).then_inc(cs_in, 16)
                sp.dma_start(csb[:, 1, :], sin[:, bass.ts(n, BLK)]).then_inc(cs_in, 16)
                sp.wait_ge(parts_ok, at(n))
                sp.dma_start(parts_dram[bass.ts(n, 1), :, :, :].rearrange("a p s t -> (a p) s t"), qkp[:, :, :]).then_inc(parts_out, 16)
                sp.wait_ge(parts_out, at(n, 16, 16))
                for g in range(NTERM):
                    src = parts_dram[bass.ts(n, 1), 0:NH * HD, QPART[g], :].rearrange("a (h d) t -> d (a h) t", d=HD)
                    sp.dma_start(Qs[g * HD:(g + 1) * HD, bass.ts(n, 1), :, :].rearrange("p a h t -> p (a h) t"), src).then_inc(qk_in, 16)
                    src = parts_dram[bass.ts(n, 1), NH * HD:NQK, KPART[g], :].rearrange("a (h d) t -> d (a h) t", d=HD)
                    sp.dma_start(Ks[g * HD:(g + 1) * HD, bass.ts(n, 1), :, :].rearrange("p a h t -> p (a h) t"), src).then_inc(qk_in, 16)
            sp.wait_ge(qk_in, at(NBLK - 1, 12 * 16, 12 * 16))
            load_weights(WEIGHTS_A, len(WEIGHTS))
            with sp.Fori(0, NBLK) as n:
                sp.wait_ge(fin_ok, at(n))
                sp.dma_start(outv[:, bass.ts(n, TPB), :], fin[:, :, :]).then_inc(out_done, 16)
            sp.wait_ge(out_done, at(NBLK - 1, 16, 16))

        @block.gpsimd
        def _(pool):
            nc.gpsimd.memset(ident[:, :], 0.0)
            nc.gpsimd.memset(keep_t_ge_u[:, :], 1.0)
            nc.gpsimd.memset(Vn[:, :, :], 0.0)
            pool.drain()
            nc.gpsimd.memset(Ks[KSC:KROWS, :, :, :], 1.0)
            pool.drain()
            nc.gpsimd.affine_select(out=ident[:, :], in_=ident[:, :], compare_op=ALU.not_equal, fill=1.0,
                                    base=0, pattern=[[-1, P]], channel_multiplier=1)
            nc.gpsimd.affine_select(out=keep_t_ge_u[:, :], in_=keep_t_ge_u[:, :], compare_op=ALU.is_ge, fill=0.0,
                                    base=0, pattern=[[1, P]], channel_multiplier=-1)
            nc.gpsimd.memset(neg_t_lt_s[:, :], 0.0)
            nc.gpsimd.memset(neg_s_gt_t[:, :], 0.0)
            for e in range(NE):
                nc.gpsimd.memset(rank[:, e:e + 1], float(NE - e))
            pool.drain()
            nc.gpsimd.affine_select(out=neg_t_lt_s[:, :], in_=neg_t_lt_s[:, :], compare_op=ALU.is_ge, fill=NEG,
                                    base=0, pattern=[[-1, P]], channel_multiplier=1)
            nc.gpsimd.affine_select(out=neg_s_gt_t[:, :], in_=neg_s_gt_t[:, :], compare_op=ALU.is_ge, fill=NEG,
                                    base=0, pattern=[[1, P]], channel_multiplier=-1)
            for g in range(NKV):
                nc.gpsimd.memset(Vn[:, :, g * VW + HD:g * VW + HD + 1], 1.0)
            pool.drain()
            nc.gpsimd.tensor_copy(identb[:, :], ident[:, :]).then_inc(masks_ok, 1)
            pool.wait_ge(rows_ok, at(0))
            g = nc.gpsimd

            def gather(n):
                wait(pool, emb_used, at(n, 0))
                for t in range(TPB):
                    for h in range(2):
                        pool.indirect_dma_start(emb[:, t, h, :], None, table,
                                                bass.IndirectOffsetOnAxis(ap=rows[:, n * TPB + t, h:h + 1], axis=0)).then_inc(gathered, 16)
                    pool.indirect_dma_start(embw[:, t, :], None, hash_w,
                                            bass.IndirectOffsetOnAxis(ap=rows[:, n * TPB + t, 2:3], axis=0)).then_inc(gathered, 16)

            def rotated(n):
                pool.wait_ge(rope_ok, at(n, 2, 2))
                wait(pool, parts_out, at(n, 0, 16))
                g.tensor_tensor(rp[:, 0, :], rp[:, 1, :], rp[:, 2, :], ALU.add)
                g.tensor_tensor(qkp[:, 0, :], rp[:, 1, :], rp[:, 2, :], ALU.add).then_inc(sum_ok, 1)
                pool.drain()
                g.tensor_tensor(rp[:, 3, :], rp[:, 0, :], qkp[:, 0, :], ALU.subtract)
                g.tensor_tensor(qkp[:, 1, :], rp[:, 0, :], qkp[:, 0, :], ALU.subtract)
                pool.drain()
                g.tensor_tensor(qkp[:, 2, :], rp[:, 3, :], qkp[:, 1, :], ALU.subtract).then_inc(parts_ok, 1)

            gather(0)
            gather(1)
            for n in range(NBLK):
                if n + 2 < NBLK:
                    gather(n + 2)
                if n:
                    rotated(n - 1)
            rotated(NBLK - 1)
            for i, (_, dst, n) in enumerate(WEIGHTS):
                if i < WEIGHTS_A:
                    continue
                pool.wait_ge(weight_in, at(0, 16 * (i + 1), 16))
                g.tensor_copy(dst[:, 0, :], wtmp[:, 0:n])
                pool.drain()
                g.tensor_tensor(wres[:, 0:n], wtmp[:, 0:n], dst[:, 0, :], ALU.subtract).then_inc(weight_free, 1)
                pool.drain()
                g.tensor_copy(dst[:, 1, :], wres[:, 0:n])
                pool.drain()
                g.tensor_tensor(dst[0:C, 2, :], wres[0:C, 0:n], dst[0:C, 1, :], ALU.subtract)
                g.tensor_copy(dst[C:P, 2, :], dst[C:P, 0, :]).then_inc(late_ok, 1)
                pool.drain()

        @block.scalar
        def _(act):
            a = nc.scalar

            def split_copies(n, i, src):
                act.wait_ge(xr_ok[i], at(n))
                if i == 0:
                    wait(act, stacked[0], at(n - 1))
                    wait(act, stacked[1], at(n - 2))
                else:
                    if isinstance(n, int) and n == NBLK - 1:
                        act.wait_ge(stacked[1], at(n - 1))
                    else:
                        act.wait_ge(stacked[0], at(n + 1))
                a.activation(Sx[:, :, 0:C], src, ACT.Copy)
                a.activation(Sx[:, :, 2 * C:3 * C], src, ACT.Copy).then_inc(x1_ok[i], 1)

            def sqrt(n, i):
                act.wait_ge(var_r[i], at(n))
                a.activation(st[:, 2 + i, :], st[:, 2 + i, :], ACT.Sqrt).then_inc(sd_r[i], 1)

            def evac_ab(n, i):
                act.wait_ge(stacked[i], at(n))
                if i == 0:
                    wait(act, v_ps, at(n - 2))
                elif not (isinstance(n, int) and n == NBLK - 1):
                    act.wait_ge(qh_ps, at(n + 1, NPAIR, NPAIR))
                else:
                    act.wait_ge(v_ps, at(n - 1))
                a.activation(AB[:, :, :], bank[0].bitcast(BF16).rearrange("p (s t) -> p s t", s=2), ACT.Copy).then_inc(ab_ok[i], 1)

            def g_copy(n, c):
                act.wait_ge(g_ps, at(n, c + 1, TPB))
                a.activation(Gs[:, :, c * P:(c + 1) * P], bank[6 + c % 2].rearrange("p (a t) -> p a t", a=NPAIR),
                             ACT.Copy).then_inc(g_ok, 1)

            def v_copy(n):
                act.wait_ge(v_ps, at(n))
                act.wait_ge(v_ps, 1)
                a.activation(Vn[:, bass.ts(n, TPB), :].rearrange("p t (g w) -> p t g w", g=NKV)[:, :, :, 0:HD],
                             bank[1][:, 0:TPB * NKV * HD].rearrange("p (t g d) -> p t g d", t=TPB, g=NKV),
                             ACT.Copy).then_inc(v_ok, 1)

            def main(n, post, prep):
                evac_ab(n, 0)
                for p in range(NPAIR):
                    act.wait_ge(qh_ps, at(n, p + 1, NPAIR))
                    a.activation(qh[:, p, :], bank[2 + p % 2], ACT.Copy).then_inc(qh_ok, 1)
                if post:
                    sqrt(n - 1, 1)
                g_copy(n, 0)
                if post:
                    sqrt(n - 1, 2)
                g_copy(n, 1)
                if post:
                    split_copies(n - 1, 1, hn[:, :, :])
                g_copy(n, 2)
                if post:
                    evac_ab(n - 1, 1)
                g_copy(n, 3)
                if prep:
                    sqrt(n + 1, 0)
                if prep:
                    split_copies(n + 1, 0, rn[:, :, :])
                act.wait_ge(oT_ps, at(n))
                a.activation(oT[:, :], bank[4][:, 0:2 * P], ACT.Copy).then_inc(oT_ok, 1)
                if post:
                    v_copy(n - 1)

            sqrt(0, 0)
            split_copies(0, 0, rn[:, :, :])
            main(0, False, True)
            with act.Fori(1, NBLK - 1) as n:
                main(n, True, True)
            main(NBLK - 1, True, False)
            sqrt(NBLK - 1, 1)
            sqrt(NBLK - 1, 2)
            split_copies(NBLK - 1, 1, hn[:, :, :])
            def row(j):
                act.wait_ge(mt_ps, at(j))
                wait(act, m_in, at(j, 0, 48))
                a.activation(mrow[:, :], bank[6].bitcast(BF16)[0:3 * NH * TPB, 0:P], ACT.Copy).then_inc(mrow_ok, 1)
                act.wait_ge(mrow_ok, at(j))
                for g in range(3):
                    act.dma_start(Qs[KSC + g:KSC + g + 1, j, :, :].rearrange("p h (i t) -> p (h i) t", t=P),
                                  mrow[g * NH * TPB:(g + 1) * NH * TPB, :]).then_inc(m_in, 16)

            def norm(i):
                act.wait_ge(pv_ok, at(LAST[i]))
                wait(act, yn_ps, at(i - 1))
                a.activation(yT[:, :], bank[7], ACT.Copy).then_inc(yT_ok, 1)

            def first_split(r, src):
                wait(act, stb, at(r - 1))
                a.activation(Sx[:, :, 0:C], src, ACT.Copy)
                a.activation(Sx[:, :, 2 * C:3 * C], src, ACT.Copy).then_inc(xb1_ok, 1)

            def y_copy(i):
                act.wait_ge(yn_ok, at(i))
                first_split(ROUND["y", i], y_all[:, i * TPB:(i + 1) * TPB, :])

            def x_copy(i):
                act.wait_ge(xb_ok, at(i))
                first_split(ROUND["x", i], hn[:, :, :])

            def stack_copy(r, dst, misc):
                act.wait_ge(stb, at(r))
                a.activation(dst, bank[misc].bitcast(BF16).rearrange("p (s t) -> p s t", s=2), ACT.Copy).then_inc(abb_ok, 1)

            def y_stack(i):
                wait(act, wo_ps, at(i - 1))
                stack_copy(ROUND["y", i], AB[:, :, :], attention_bank(i))

            def x_stack(i):
                stack_copy(ROUND["x", i], ABf[:, i, :, :], router_bank(i))

            def root(b):
                act.wait_ge(var2_ok, at(b))
                part = var2[:, b * (T // P):(b + 1) * (T // P)]
                a.activation(part, part, ACT.Sqrt).then_inc(sd2_ok, 1)

            def top_exp(b):
                act.wait_ge(lm_ok, at(b))
                part = slice(b * (T // P), (b + 1) * (T // P))
                a.activation(pr[:, part, :], lg[:, part, :], ACT.Exp).then_inc(pe_ok, 1)

            def turn(i):
                act.wait_ge(WT_ps, at(i))
                a.activation(WT[:, i, :], bank[router_bank(i)].bitcast(BF16)[0:3 * EW, 0:BLK], ACT.Copy).then_inc(WT_ok, 1)

            does = {"row": row, "norm": norm, "y_copy": y_copy, "x_copy": x_copy, "y_stack": y_stack, "x_stack": x_stack,
                    "root": root, "top_exp": top_exp, "turn": turn}

            def events(found):
                for e, i in found:
                    if does.get(e):
                        does[e](i)

            row(0)
            evac_ab(NBLK - 1, 1)
            v_copy(NBLK - 1)
            act.wait_ge(parts_ok, at(NBLK - 1))
            for g, (i, s) in enumerate(STEPS):
                off = max(0, s - TPB * (i % BPS)) * P
                for hp in range(2):
                    act.wait_ge(st_ps, at(g, hp + 1, 2))
                    wait(act, pv_ok, at(g - 2))
                    a.activation(pexp[:, g % 2, 2 * hp:2 * hp + 2, off:], ps[:, 2 * hp:2 * hp + 2, off:], ACT.Exp,
                                 scale=float(HD) ** -0.5).then_inc(exp_ok, 1)
                events(EVENTS["act"][g])
            for found in EVENTS["act"][len(STEPS):]:
                events(found)
            norm(NBLK - 1)


            def finish_copy(n):
                act.wait_ge(w2_done, at(n, NKT, NKT))
                wait(act, en_ps, at(n - 1))
                a.activation(yT[:, :], bank[6], ACT.Copy).then_inc(eT_ok, 1)

            def experts(n, q):
                for j in range(NKT):
                    m = min(P, NHID - j * P)
                    slot = (q + j) % 2
                    act.wait_ge(gu_ps, at(n, j + 1, NKT))
                    wait(act, hu_ok, at(n, j - 1, NKT))
                    a.activation(sg[0:m, slot, :], bank[slot][0:m, :], ACT.Silu).then_inc(sg_ok, 1)
                    if j == 1 and not (isinstance(n, int) and n == 0):
                        finish_copy(n - 1)
                    if isinstance(n, int):
                        events(TILE_EVENTS["act"][n * NKT + j])

            for n in range(BPS):
                experts(n, n % 2)
            with act.Fori(BPS // 2, NBLK // 2) as p:
                experts(2 * p, 0)
                experts(2 * p + 1, 1)
            finish_copy(NBLK - 1)

        @block.vector
        def _(dve):
            v = nc.vector
            v.memset(rTe[:, :], 0.0)
            v.memset(w3s[:, :, :, :], 0.0)
            v.memset(rTo[:, :], 0.0)
            v.memset(Cd[:, :, :], 0.0)
            v.memset(keep[:, :], 1.0)
            dve.drain()
            for s in range(1, NB + 1):
                v.memset(keep[:, s * BPS - 1:s * BPS], 0.0)
            dve.wait_ge(consts_in, at(0, 96, 16))
            v.tensor_scalar(dig[:, 0, :], xid[:, :], 63, None, ALU.bitwise_and)
            v.tensor_scalar(dig[:, 1, :], xid[:, :], 6, 63, ALU.logical_shift_right, ALU.bitwise_and)
            v.tensor_scalar(dig[:, 2, :], xid[:, :], 12, None, ALU.logical_shift_right)
            dve.drain()

            def reduce_mod(m):
                v.tensor_scalar(quo[:, :, :], hsh[:, :, :], 1.0 / m, None, ALU.mult)
                dve.drain()
                v.tensor_copy(quf[:, :, :], quo[:, :, :])
                dve.drain()
                v.scalar_tensor_tensor(hsh[:, :, :], quf[:, :, :], -float(m), hsh[:, :, :], ALU.mult, ALU.add)
                dve.drain()
                v.tensor_scalar(quf[:, :, :], hsh[:, :, :], 0.0, float(m), ALU.is_lt, ALU.mult)
                dve.drain()
                v.tensor_tensor(hsh[:, :, :], hsh[:, :, :], quf[:, :, :], ALU.add)
                dve.drain()
                v.tensor_scalar(quf[:, :, :], hsh[:, :, :], float(m), -float(m), ALU.is_ge, ALU.mult)
                dve.drain()
                v.tensor_tensor(hsh[:, :, :], hsh[:, :, :], quf[:, :, :], ALU.add)
                dve.drain()

            c = [[float(a * 64 ** k % HASHP) for k in range(3)] for a in HASH_A]
            for i in range(2):
                v.tensor_scalar(hsh[:, i, :], dig[:, 2, :], c[i][2], float(HASH_B[i]), ALU.mult, ALU.add)
            dve.drain()
            for k in (1, 0):
                for i in range(2):
                    v.scalar_tensor_tensor(hsh[:, i, :], dig[:, k, :], c[i][k], hsh[:, i, :], ALU.mult, ALU.add)
                dve.drain()
            reduce_mod(HASHP)
            reduce_mod(HASHM)
            x2 = xid[:, :].unsqueeze(1).to_broadcast([P, 2, NT])
            v.tensor_scalar(hsh[:, :, :], hsh[:, :, :], float(IC), None, ALU.add)
            dve.drain()
            v.tensor_tensor(quf[:, :, :], x2, hsh[:, :, :], ALU.subtract)
            dve.drain()
            v.scalar_tensor_tensor(quf[:, :, :], x2, float(NSPECIAL), quf[:, :, :], ALU.is_lt, ALU.mult)
            dve.drain()
            v.tensor_tensor(rows[:, :, 0:2].rearrange("p t i -> p i t"), hsh[:, :, :], quf[:, :, :], ALU.add)
            v.tensor_scalar(rows[:, :, 2], xid[:, :], float(VOCAB - 1), None, ALU.min)
            dve.drain()
            v.tensor_copy(quf[:, :, :], quf[:, :, :]).then_inc(rows_ok, 1)

            for i, (_, dst, n) in enumerate(WEIGHTS[:WEIGHTS_A]):
                dve.wait_ge(weight_in, at(0, 16 * (i + 1), 16))
                v.tensor_copy(dst[:, 0, :], wtmp[:, 0:n])
                dve.drain()
                v.tensor_tensor(wres[:, 0:n], wtmp[:, 0:n], dst[:, 0, :], ALU.subtract).then_inc(weight_free, 1)
                v.tensor_copy(dst[C:P, 2, :], dst[C:P, 0, :])
                dve.drain()
                v.tensor_copy(dst[:, 1, :], wres[:, 0:n])
                dve.drain()
                v.tensor_tensor(dst[0:C, 2, :], wres[0:C, 0:n], dst[0:C, 1, :], ALU.subtract)
                dve.drain()
            v.tensor_copy(quf[:, :, :], quf[:, :, :]).then_inc(init_ok, 1)
            dve.wait_ge(masks_ok, at(0))

            def mean_square(n, i, x, eps):
                v.tensor_tensor(sq[:, :, :], x, x, ALU.mult)
                dve.drain()
                v.tensor_reduce(st[:, 1, :], sq[:, :, :], AX, ALU.add)
                dve.drain()
                v.tensor_scalar(st[:, 2 + i, :], st[:, 1, :], 1.0 / C, eps, ALU.mult, ALU.add).then_inc(var_r[i], 1)

            def inverse(n, i):
                dve.wait_ge(sd_r[i], at(n))
                v.reciprocal(st[:, 2 + i, :], st[:, 2 + i, :])
                dve.drain()

            def center(dst, x):
                v.tensor_reduce(st[:, 0, :], x, AX, ALU.add)
                dve.drain()
                v.tensor_scalar(st[:, 0, :], st[:, 0, :], -1.0 / C, None, ALU.mult)
                dve.drain()
                v.tensor_tensor(dst, x, bcast(st[:, 0, :], C), ALU.add)
                dve.drain()

            def split_rest(n, i, x):
                dve.wait_ge(x1_ok[i], at(n))
                v.tensor_tensor(res[:, :, :], x, Sx[:, :, 0:C], ALU.subtract)
                v.tensor_tensor(Sx[:, :, C:2 * C], x, Sx[:, :, 0:C], ALU.subtract)
                dve.drain()
                v.tensor_tensor(Sx[:, :, 3 * C:4 * C], res[:, :, :], Sx[:, :, C:2 * C], ALU.subtract).then_inc(split_ok[i], 1)
                dve.drain()

            def block_of(x, n):
                return x[:, bass.ds(n * TPB, TPB), :]

            def prep_embed(n):
                h0 = block_of(h_all, n)
                dve.wait_ge(gathered, 16 * 3 * TPB * (n + 1))
                v.tensor_tensor(t2[:, :, :, :], emb[:, :, :, :], bcast(embw[:, :, :], C), ALU.mult).then_inc(emb_used, 1)
                dve.drain()
                v.tensor_tensor(h0, t2[:, :, 0, :], t2[:, :, 1, :], ALU.add)
                dve.drain()
                center(xp, h0)
                mean_square(n, 0, xp, EPS_LN)

            def prep_norm(n):
                inverse(n, 0)
                v.tensor_tensor(rn[:, :, :], xp, bcast(st[:, 2, :], C), ALU.mult).then_inc(xr_ok[0], 1)
                dve.drain()
                split_rest(n, 0, rn[:, :, :])

            def post_add(n):
                h = block_of(h_all, n).rearrange("p (s m) d -> p m s d", s=2)
                dve.wait_ge(on_ps, at(n))
                v.tensor_tensor(h, h, bank[5][:, 0:2 * P].rearrange("p (m s d) -> p m s d", m=2, s=2), ALU.add).then_inc(on_ok, 1)
                dve.drain()

            def post_center(n):
                center(xc[:, :, :], block_of(h_all, n))
                mean_square(n, 1, xc[:, :, :], EPS_LN)

            def post_norm(n):
                inverse(n, 1)
                v.tensor_tensor(block_of(x_all, n), xc[:, :, :], bcast(st[:, 3, :], C), ALU.mult)
                dve.drain()
                mean_square(n, 2, block_of(x_all, n), EPS_RMS)

            def post_split(n):
                inverse(n, 2)
                v.tensor_tensor(xc[:, :, :], block_of(x_all, n), bcast(st[:, 4, :], C), ALU.mult)
                dve.drain()
                v.tensor_tensor(hn[:, :, :], xc[:, :, :], ln1b[:, :].unsqueeze(1).to_broadcast([P, TPB, C]), ALU.mult).then_inc(xr_ok[1], 1)
                dve.drain()
                split_rest(n, 1, hn[:, :, :])

            def post_rotate(n, b=2):
                dve.wait_ge(qk_ps, at(n))
                dve.wait_ge(cs_in, at(n, 32, 32))
                wait(dve, sum_ok, at(n, 0))
                v.tensor_tensor(rp[:, 1, :], bank[b][0:NQK, :], csb[:, 0, :], ALU.mult).then_inc(rope_ok, 1)
                v.tensor_tensor(rp[:, 2, :], bank[b + 1][0:NQK, :], csb[:, 1, :], ALU.mult).then_inc(rope_ok, 1)

            def omega_mask(n, c):
                for e in range(2):
                    dve.wait_ge(om_ps, at(n, 2 * c + e + 1, 2 * TPB))
                    wait(dve, g_ps, at(n, c, TPB))
                    v.tensor_tensor(om[:, e, :, :], bank[4 + e].rearrange("p (a t) -> p a t", a=NPAIR),
                                    keep_t_ge_u[:, :].unsqueeze(1).to_broadcast([P, NPAIR, P]), ALU.mult).then_inc(om_ok, 1)

            def double_r(n):
                wait(dve, g_ps, at(n, 0, TPB))
                v.tensor_copy(rr[:, :, 0:C], rn[:, :, :]).then_inc(rr_ok, 1)
                v.tensor_copy(rr[:, :, C:2 * C], rn[:, :, :]).then_inc(rr_ok, 1)

            def main(n, post, prep):
                dve.wait_ge(rT_ps, at(n))
                v.tensor_copy(rTe[0:C, :], bank[1][0:C, :])
                v.tensor_copy(rTo[C:P, :], bank[1][C:P, :]).then_inc(rT_ok, 1)
                if prep:
                    prep_embed(n + 1)
                dve.wait_ge(cup_ps, at(n))
                for c in range(TPB - 1):
                    for s in (slice(0, C), slice(C, P)):
                        last = v.tensor_tensor(Cd[s, c + 1, s], Cd[s, c, s], bank[1][s, c * C:(c + 1) * C], ALU.add)
                    dve.drain()
                last.then_inc(cup_ok, 1)
                omega_mask(n, 0)
                dve.wait_ge(inter_done, at(n, 1, TPB))
                for s in (slice(0, C), slice(C, P)):
                    v.tensor_tensor(Cd[s, 0, s], Cd[s, 3, s], bank[1][s, 3 * C:4 * C], ALU.add)
                dve.drain()
                for s in (slice(0, C), slice(C, P)):
                    last = v.tensor_scalar(Cd[s, 0, s], Cd[s, 0, s], keep[s, bass.ds(n, 1)], None, ALU.mult)
                last.then_inc(cup_ok, 1)
                dve.drain()
                if post:
                    post_center(n - 1)
                omega_mask(n, 1)
                if post:
                    post_norm(n - 1)
                omega_mask(n, 2)
                if post:
                    post_split(n - 1)
                omega_mask(n, 3)
                if prep:
                    prep_norm(n + 1)
                post_add(n)
                if prep:
                    double_r(n + 1)
                if post:
                    post_rotate(n - 1)

            prep_embed(0)
            prep_norm(0)
            double_r(0)
            main(0, False, True)
            with dve.Fori(1, NBLK - 1) as n:
                main(n, True, True)
            main(NBLK - 1, True, False)

            def maxima(first, last):
                for u in range(first, last):
                    j, t, h, together, c = UNITS[u]
                    k = j % BPS
                    w = BLK if c < k else (t + 1) * P
                    dve.wait_ge(mx_ps, at(u))
                    v.tensor_reduce(mxc[:, h:h + together, t, c], unit_bank(u)[:, 0:together * w].rearrange("p (h s) -> p h s", s=w),
                                    AX, ALU.max).then_inc(mx_ok, 1)
                    if u + 1 < U_END[j]:
                        continue
                    dve.drain()
                    if k:
                        v.tensor_reduce(mneg[:, 0, :], mxc[:, :, :, 0:k + 1].rearrange("p h i c -> p (h i) c"), AX, ALU.max, negate=True)
                    else:
                        v.tensor_scalar(mneg[:, 0, :], mxc[:, :, :, 0].rearrange("p h i -> p (h i)"), -1.0, None, ALU.mult)
                    dve.drain()
                    wait(dve, mt_ps, at(j - 1))
                    v.tensor_copy(m3[:, 0, :], mneg[:, 0, :])
                    dve.drain()
                    v.tensor_tensor(mneg[:, 1, :], mneg[:, 0, :], m3[:, 0, :], ALU.subtract)
                    v.tensor_tensor(m3[:, 1, :], mneg[:, 0, :], m3[:, 0, :], ALU.subtract)
                    dve.drain()
                    v.tensor_tensor(m3[:, 2, :], mneg[:, 1, :], m3[:, 1, :], ALU.subtract).then_inc(m3_ok, 1)
                    dve.drain()

            maxima(0, 3)
            post_center(NBLK - 1)
            maxima(3, 6)
            post_norm(NBLK - 1)
            maxima(6, U_END[0])
            post_split(NBLK - 1)
            maxima(U_END[0], U_END[0] + EARLY)

            def norm(i):
                dve.wait_ge(yn_ps, at(i))
                yn = bank[attention_bank(i)].rearrange("p (t h w) -> p t h w", t=TPB, h=NH)
                v.reciprocal(rden[:, :, :], yn[:, :, :, HD])
                dve.drain()
                v.tensor_tensor(y_all[:, i * TPB:(i + 1) * TPB, :].rearrange("p t (h d) -> p t h d", h=NH),
                                yn[:, :, :, 0:HD], bcast(rden[:, :, :], HD), ALU.mult).then_inc(yn_ok, 1)
                dve.drain()

            def later_splits(r, x):
                dve.wait_ge(xb1_ok, at(r))
                v.tensor_tensor(res[:, :, :], x, Sx[:, :, 0:C], ALU.subtract)
                v.tensor_tensor(Sx[:, :, C:2 * C], x, Sx[:, :, 0:C], ALU.subtract)
                dve.drain()
                v.tensor_tensor(Sx[:, :, 3 * C:4 * C], res[:, :, :], Sx[:, :, C:2 * C], ALU.subtract).then_inc(sb_ok, 1)
                dve.drain()

            def y_copy(i):
                later_splits(ROUND["y", i], y_all[:, i * TPB:(i + 1) * TPB, :])

            def x_copy(i):
                later_splits(ROUND["x", i], hn[:, :, :])

            def y_sum(i):
                x = x_all[:, i * TPB:(i + 1) * TPB, :]
                dve.wait_ge(wo_ps, at(i))
                v.tensor_tensor(x, x, bank[attention_bank(i)][:, 0:TPB * C].rearrange("p (t c) -> p t c", t=TPB), ALU.add).then_inc(wo_ok, 1)
                dve.drain()
                v.tensor_tensor(sq[:, :, :], x, x, ALU.mult)
                dve.drain()
                v.tensor_reduce(var2[:, i * TPB:(i + 1) * TPB], sq[:, :, :], AX, ALU.add)
                dve.drain()

            def root(b):
                part = var2[:, b * (T // P):(b + 1) * (T // P)]
                v.tensor_scalar(part, part, 1.0 / C, EPS_RMS, ALU.mult, ALU.add).then_inc(var2_ok, 1)

            def inverse_root(b):
                part = var2[:, b * (T // P):(b + 1) * (T // P)]
                dve.wait_ge(sd2_ok, at(b))
                v.reciprocal(part, part)
                dve.drain()

            def x_norm(i):
                v.tensor_tensor(xc[:, :, :], x_all[:, i * TPB:(i + 1) * TPB, :], bcast(var2[:, i * TPB:(i + 1) * TPB], C), ALU.mult)
                dve.drain()
                v.tensor_tensor(hn[:, :, :], xc[:, :, :], ln2b[:, :].unsqueeze(1).to_broadcast([P, TPB, C]), ALU.mult).then_inc(xb_ok, 1)
                dve.drain()

            def x_keep(i):
                dve.wait_ge(lg_ps, at(i))
                v.tensor_copy(lg[:, i * TPB:(i + 1) * TPB, :],
                              bank[router_bank(i)][:, 0:TPB * NE].rearrange("p (t c) -> p t c", t=TPB)).then_inc(lg_ok, 1)
                dve.drain()

            def top_exp(b):
                part = slice(b * (T // P), (b + 1) * (T // P))
                v.tensor_reduce(cols[:, 0, part], lg[:, part, :], AX, ALU.max)
                dve.drain()
                v.tensor_tensor(lg[:, part, :], lg[:, part, :], bcast(cols[:, 0, part], NE), ALU.subtract).then_inc(lm_ok, 1)
                dve.drain()

            def top_parts(b):
                part = slice(b * (T // P), (b + 1) * (T // P))
                return part, pr[:, part, :], tk[:, part, :], tr[:, part, :], [cols[:, i, part] for i in range(4)]

            def top_shares(b):
                _, p_, _, _, c_ = top_parts(b)
                dve.wait_ge(pe_ok, at(b))
                v.tensor_reduce(c_[0], p_, AX, ALU.add)
                dve.drain()
                v.reciprocal(c_[1], c_[0])
                dve.drain()
                v.tensor_tensor(p_, p_, bcast(c_[1], NE), ALU.mult)
                dve.drain()

            def top_take(b, i):
                _, p_, t_, _, c_ = top_parts(b)
                v.tensor_reduce(c_[1 + i], p_, AX, ALU.max)
                dve.drain()
                v.tensor_tensor(t_, p_, bcast(c_[1 + i], NE), ALU.is_equal)
                dve.drain()
                v.tensor_tensor(t_, t_, rank[:, :].unsqueeze(1).to_broadcast([P, T // P, NE]), ALU.mult)
                dve.drain()
                v.tensor_reduce(c_[0], t_, AX, ALU.max)
                dve.drain()
                v.tensor_tensor(t_, t_, bcast(c_[0], NE), ALU.is_equal)
                dve.drain()

            def top_first(b):
                _, p_, t_, w_, _ = top_parts(b)
                top_take(b, 0)
                v.tensor_tensor(w_, t_, p_, ALU.mult)
                dve.drain()
                v.scalar_tensor_tensor(p_, t_, -2.0, p_, ALU.mult, ALU.add)
                dve.drain()

            def top_second(b):
                _, p_, t_, w_, c_ = top_parts(b)
                top_take(b, 1)
                v.tensor_tensor(t_, t_, p_, ALU.mult)
                dve.drain()
                v.tensor_tensor(w_, t_, w_, ALU.add)
                v.scalar_tensor_tensor(c_[0], c_[1], 1e-9, c_[2], ALU.add, ALU.add)
                dve.drain()

            def top_split(b):
                part, _, t_, w_, c_ = top_parts(b)
                v.reciprocal(c_[3], c_[0])
                dve.drain()
                v.tensor_tensor(w_, w_, bcast(c_[3], NE), ALU.mult)
                dve.drain()
                v.tensor_copy(w3s[:, part, 0, 0:NE], w_)
                dve.drain()
                v.tensor_tensor(t_, w_, w3s[:, part, 0, 0:NE], ALU.subtract)
                v.tensor_tensor(w3s[:, part, 1, 0:NE], w_, w3s[:, part, 0, 0:NE], ALU.subtract)
                dve.drain()
                v.tensor_tensor(w3s[:, part, 2, 0:NE], t_, w3s[:, part, 1, 0:NE], ALU.subtract).then_inc(w_ok, 1)
                dve.drain()

            does = {"norm": norm, "y_copy": y_copy, "x_copy": x_copy, "y_sum": y_sum, "root": root, "inverse": inverse_root,
                    "x_norm": x_norm, "x_keep": x_keep, "top_exp": top_exp,
                    "top_shares": top_shares, "top_first": top_first, "top_second": top_second, "top_split": top_split}

            def events(found):
                for e, i in found:
                    if does.get(e):
                        does[e](i)

            for g, (first, last) in enumerate(IN_STEP):
                half = (first + last) // 2
                maxima(first, half)
                if g == 0:
                    post_rotate(NBLK - 1, 6)
                events(EVENTS["dve"][g])
                maxima(half, last)
            for found in EVENTS["dve"][len(STEPS):]:
                events(found)

            def finish(n):
                dve.wait_ge(en_ps, at(n))
                en = bank[7].rearrange("p (t s c) -> p t s c", t=TPB, s=2)
                v.tensor_tensor(xc[:, :, :], block_of(x_all, n), en[:, :, 0, :], ALU.add)
                dve.drain()
                v.tensor_tensor(sq[:, :, :], xc[:, :, :], en[:, :, 1, :], ALU.add).then_inc(en_ok, 1)
                dve.drain()
                wait(dve, out_done, at(n, 0, 16))
                v.tensor_tensor(fin[:, :, :], sq[:, :, :], block_of(h_all, n), ALU.add).then_inc(fin_ok, 1)
                dve.drain()

            def experts(n, q):
                for j in range(NKT):
                    m = min(P, NHID - j * P)
                    slot = (q + j) % 2
                    dve.wait_ge(sg_ok, at(n, j + 1, NKT))
                    v.tensor_tensor(hu[0:m, slot, :], sg[0:m, slot, :], bank[2 + slot][0:m, :], ALU.mult).then_inc(hu_ok, 1)
                    dve.drain()
                    dve.wait_ge(wb_ps, at(n, j + 1, NKT))
                    if j >= SLOTS:
                        dve.wait_ge(w2_done, at(n, j - SLOTS + 1, NKT))
                    else:
                        wait(dve, w2_done, at(n - 1, (NKT - 1 - j) // SLOTS * SLOTS + j + 1, NKT))
                    v.tensor_tensor(hh[0:m, j % SLOTS, :], hu[0:m, slot, :], bank[4 + slot][0:m, :], ALU.mult).then_inc(hh_ok, 1)
                    if j == FINISH_AT and not (isinstance(n, int) and n == 0):
                        finish(n - 1)
                    if isinstance(n, int):
                        events(TILE_EVENTS["dve"][n * NKT + j])

            for n in range(BPS):
                experts(n, n % 2)
            with dve.Fori(BPS // 2, NBLK // 2) as p:
                experts(2 * p, 0)
                experts(2 * p + 1, 1)
            finish(NBLK - 1)

        @block.tensor
        def _(pe):
            mm = nc.tensor.matmul

            def stack_transposes(n, i):
                pe.wait_ge(split_ok[i], at(n))
                if i == 0:
                    wait(pe, ab_ok[1], at(n - 2))
                elif isinstance(n, int) and n == NBLK - 1:
                    pe.wait_ge(ab_ok[1], at(n - 1))
                else:
                    pe.wait_ge(ab_ok[0], at(n + 1))
                dst = bank[0].bitcast(BF16).rearrange("p (s t) -> p s t", s=2)
                for t in range(TPB):
                    for s in range(2):
                        last = nc.tensor.transpose(dst[:, s, t * P:(t + 1) * P], Sx[:, t, s * P:(s + 1) * P], identb[:, :])
                last.then_inc(stacked[i], 1)

            def split3(dst, w, cols, x):
                for k in range(3):
                    last = mm(dst, w[:, k, cols], AB[:, k // 2, x], start=(k == 0), stop=(k == 2))
                return last

            def omega(n, c):
                for e, rT in enumerate((rTe, rTo)):
                    wait(pe, om_ok, at(n, 2 * (c - 1) + e + 1, 2 * TPB))
                    mm(bank[4 + e], rT[:, c * P:(c + 1) * P], qh[:, :, c * P:(c + 1) * P], start=True, stop=True).then_inc(om_ps, 1)

            def qk_products(n, b=2):
                pe.wait_ge(ab_ok[1], at(n))
                split3(bank[b][0:NQK, :], wqk3, slice(0, NQK), slice(0, BLK))
                split3(bank[b + 1][0:NQK, :], wqk3, slice(NQK, 2 * NQK), slice(0, BLK)).then_inc(qk_ps, 1)

            def v_products(n):
                for t in range(TPB):
                    for k in range(3):
                        last = mm(bank[1][:, t * NKV * HD:(t + 1) * NKV * HD], AB[:, k // 2, t * P:(t + 1) * P], wv3[:, k, :],
                                  start=(k == 0), stop=(k == 2))
                last.then_inc(v_ps, 1)

            def main(n, post):
                stack_transposes(n, 0)
                pe.wait_ge(rr_ok, at(n, 2, 2))
                wait(pe, v_ok, at(n - 2))
                for t in range(TPB):
                    last = nc.tensor.transpose(bank[1][:, t * P:(t + 1) * P], rr[:, t, :], ident[:, :])
                last.then_inc(rT_ps, 1)
                pe.wait_ge(ab_ok[0], at(n))
                wait(pe, rope_ok, at(n - 2, 2, 2))
                for p in range(NPAIR):
                    if p >= 2:
                        pe.wait_ge(qh_ok, at(n, p - 1, NPAIR))
                    split3(bank[2 + p % 2], lq3, slice(p * P, (p + 1) * P), slice(0, BLK)).then_inc(qh_ps, 1)
                pe.wait_ge(rT_ok, at(n))
                for c in range(TPB):
                    last = mm(bank[1][:, c * C:(c + 1) * C], rr[:, c, :], rr[:, c, 0:C], start=True, stop=True)
                last.then_inc(cup_ps, 1)
                pe.wait_ge(qh_ok, at(n, NPAIR, NPAIR))
                wait(pe, on_ok, at(n, 0))
                omega(n, 0)
                pe.wait_ge(cup_ok, at(n, 1, 2))
                for c in range(TPB):
                    wait(pe, g_ok, at(n, c - 1, TPB))
                    mm(bank[6 + c % 2], Cd[:, c, :], qh[:, :, c * P:(c + 1) * P], start=True, stop=False).then_inc(inter_done, 1)
                    if c + 1 < TPB:
                        omega(n, c + 1)
                    elif post:
                        stack_transposes(n - 1, 1)
                    for e in range(2):
                        pe.wait_ge(om_ok, at(n, 2 * c + e + 1, 2 * TPB))
                        last = mm(bank[6 + c % 2][e * C:(e + 1) * C, :], rr[:, c, 0:C], om[:, e, :, :], start=False, stop=True)
                    last.then_inc(g_ps, 1)
                if post:
                    qk_products(n - 1)
                pe.wait_ge(g_ok, at(n, TPB, TPB))
                for p in range(NPAIR):
                    for s in range(2):
                        last = mm(bank[4][s * C:(s + 1) * C, 0:2 * P], leS[:, p, :], Gs[:, p, s * 2 * P:(s + 1) * 2 * P],
                                  start=(p == 0), stop=(p == NPAIR - 1))
                last.then_inc(oT_ps, 1)
                if post:
                    pe.wait_ge(cup_ok, at(n, 2, 2))
                    v_products(n - 1)
                pe.wait_ge(oT_ok, at(n))
                for m in range(2):
                    last = nc.tensor.transpose(bank[5][:, m * P:(m + 1) * P], oT[:, m * P:(m + 1) * P], ident[:, :])
                last.then_inc(on_ps, 1)

            pe.wait_ge(init_ok, at(0))
            pe.wait_ge(masks_ok, at(0))
            pe.wait_ge(consts_in, at(0, 96, 16))
            main(0, False)
            with pe.Fori(1, NBLK) as n:
                main(n, True)

            def max_units(first, last):
                for u in range(first, last):
                    j, t, h, together, c = UNITS[u]
                    k = j % BPS
                    w = BLK if c < k else (t + 1) * P
                    pe.wait_ge(qk_in, at(j, 12 * 16, 12 * 16))
                    wait(pe, mx_ok, at(u - (4 if u < U_END[0] else 2)))
                    for i in range(together):
                        dst = unit_bank(u)[:, i * w:(i + 1) * w]
                        last_mm = mm(dst, Qs[0:KSC, j, h + i, t * P:(t + 1) * P], Ks[0:KSC, j - k + c, (h + i) // 2, 0:w], start=True, stop=(c < k))
                        if c == k:
                            last_mm = mm(dst[:, t * P:(t + 1) * P], identb[:, :], neg_t_lt_s[:, :], start=False, stop=True)
                    last_mm.then_inc(mx_ps, 1)

            reader = {}

            def take(b):
                if b in reader:
                    pe.wait_ge(*reader[b])

            def row(j):
                pe.wait_ge(m3_ok, at(j))
                take(6)
                nc.tensor.transpose(bank[6].bitcast(BF16)[0:3 * NH * TPB, 0:P], m3[:, :, :].rearrange("p g c -> p (g c)"),
                                    identb[:, :]).then_inc(mt_ps, 1)
                reader[6] = (mrow_ok, at(j))

            def score(g, hp):
                i, s = STEPS[g]
                d = s - TPB * (i % BPS)
                off = max(0, d) * P
                wait(pe, exp_ok, at(g - 1, hp + 1, 2))
                if s == 0 and hp == 0:
                    pe.wait_ge(m_in, at(i, 48, 48))
                for h in (2 * hp, 2 * hp + 1):
                    last = mm(ps[:, h, off:], Ks[:, i - i % BPS + s // TPB, hp, s % TPB * P:(s % TPB + 1) * P],
                              Qs[:, i, h, off:], start=True, stop=(d < 0))
                    if d >= 0:
                        last = mm(ps[:, h, off:off + P], identb[:, :], neg_s_gt_t[:, :], start=False, stop=True)
                last.then_inc(st_ps, 1)

            def weigh(g, part):
                i, s = STEPS[g]
                off = max(0, s - TPB * (i % BPS)) * P
                lo, hi = max(off, part * (BLK // 2)), (part + 1) * (BLK // 2) if s else (1 - part) * BLK
                if part == 0:
                    pe.wait_ge(exp_ok, at(g, 2, 2))
                    if g == 0:
                        pe.wait_ge(rope_ok, at(NBLK - 1, 2, 2))
                    elif s == 0:
                        wait(pe, yT_ok, at(i - 1))
                for h in range(NH if lo < hi else 0):
                    last = mm(bank[7][h * VW:(h + 1) * VW, lo:hi], Vn[:, i // BPS * (T // P) + s, h // 2 * VW:(h // 2 + 1) * VW],
                              pexp[:, g % 2, h, lo:hi], start=(s == 0), stop=(g == LAST[i]))
                if part == (1 if s else 0):
                    last.then_inc(pv_ok, 1)

            def norm(i):
                pe.wait_ge(yT_ok, at(i))
                take(attention_bank(i))
                for t in range(TPB):
                    last = nc.tensor.transpose(bank[attention_bank(i)][:, t * P:(t + 1) * P], yT[:, t * P:(t + 1) * P], ident[:, :])
                last.then_inc(yn_ps, 1)
                reader[attention_bank(i)] = (yn_ok, at(i))

            def stack(r, b):
                pe.wait_ge(sb_ok, at(r))
                take(b)
                dst = bank[b].bitcast(BF16).rearrange("p (s t) -> p s t", s=2)
                for t in range(TPB):
                    for s in range(2):
                        last = nc.tensor.transpose(dst[:, s, t * P:(t + 1) * P], Sx[:, t, s * P:(s + 1) * P], identb[:, :])
                last.then_inc(stb, 1)
                reader[b] = (abb_ok, at(r))

            def y_stack(i):
                stack(ROUND["y", i], attention_bank(i))

            def x_stack(i):
                stack(ROUND["x", i], router_bank(i))

            def y_product(i):
                pe.wait_ge(late_ok, at(0, 1))
                pe.wait_ge(abb_ok, at(ROUND["y", i]))
                b = attention_bank(i)
                take(b)
                for t in range(TPB):
                    for k in range(3):
                        last = mm(bank[b][:, t * C:(t + 1) * C], AB[:, k // 2, t * P:(t + 1) * P], wo3[:, k, :], start=(k == 0), stop=(k == 2))
                last.then_inc(wo_ps, 1)
                reader[b] = (wo_ok, at(i))

            def x_product(i):
                b = router_bank(i)
                pe.wait_ge(late_ok, at(0, 2))
                pe.wait_ge(abb_ok, at(ROUND["x", i]))
                take(b)
                for t in range(TPB):
                    for k in range(3):
                        last = mm(bank[b][:, t * NE:(t + 1) * NE], ABf[:, i, k // 2, t * P:(t + 1) * P], wr3[:, k, :], start=(k == 0), stop=(k == 2))
                last.then_inc(lg_ps, 1)
                reader[b] = (lg_ok, at(i))

            def turn(i):
                b = router_bank(i)
                pe.wait_ge(w_ok, at(i // BPS))
                take(b)
                for t in range(TPB):
                    last = nc.tensor.transpose(bank[b].bitcast(BF16)[0:3 * EW, t * P:(t + 1) * P],
                                               w3s[:, i * TPB + t, :, :].rearrange("p g e -> p (g e)"), identb[:, :])
                last.then_inc(WT_ps, 1)
                reader[b] = (WT_ok, at(i))

            does = {"row": row, "norm": norm, "y_stack": y_stack, "y_product": y_product, "x_stack": x_stack,
                    "x_product": x_product, "turn": turn}

            def events(found):
                for e, i in found:
                    if does.get(e):
                        does[e](i)

            pe.wait_ge(on_ok, at(NBLK - 1))
            max_units(0, U_END[0])
            row(0)
            stack_transposes(NBLK - 1, 1)
            max_units(U_END[0], U_END[0] + EARLY)
            take(6)
            qk_products(NBLK - 1, 6)
            reader[6] = (rope_ok, at(NBLK - 1, 2, 2))
            v_products(NBLK - 1)
            pe.wait_ge(v_ok, at(NBLK - 1))
            for g in range(len(STEPS)):
                first, last = IN_STEP[g]
                stand = [first + (last - first) * k // 4 for k in range(5)]
                score(g, 0)
                max_units(stand[0], stand[1])
                score(g, 1)
                max_units(stand[1], stand[2])
                if g:
                    weigh(g - 1, 0)
                max_units(stand[2], stand[3])
                if g:
                    weigh(g - 1, 1)
                max_units(stand[3], stand[4])
                events(EVENTS["pe"][g])
            weigh(len(STEPS) - 1, 0)
            weigh(len(STEPS) - 1, 1)
            for found in EVENTS["pe"][len(STEPS):]:
                events(found)

            pe.wait_ge(late_ok, at(0, 4))
            reader[7] = (yT_ok, at(NBLK - 1))
            pe.wait_ge(exp_ok, at(len(STEPS) - 1, 2, 2))
            pe.wait_ge(WT_ok, at(BPS - 1))

            def gates(n, j, q):
                m = min(P, NHID - j * P)
                slot = (q + j) % 2
                wait(pe, hu_ok, at(n, j - 1, NKT))
                for dst, w in ((bank[slot], w13), (bank[2 + slot], w33)):
                    for i in range(3):
                        last = mm(dst[0:m, :], w[:, i, j * P:j * P + m], ABf[:, bass.ds(n, 1), i // 2, :].rearrange("p a t -> p (a t)"),
                                  start=(i == 0), stop=(i == 2))
                last.then_inc(gu_ps, 1)
                wait(pe, hh_ok, at(n, j - 1, NKT))
                mm(bank[4 + slot][0:m, :], selb[:, j * P:j * P + m], WT[:, bass.ds(n, 1), :].rearrange("p a t -> p (a t)"),
                   start=True, stop=True).then_inc(wb_ps, 1)

            def down(n, j):
                m = min(P, NHID - j * P)
                pe.wait_ge(hh_ok, at(n, j + 1, NKT))
                if j == 0:
                    if isinstance(n, int) and n == 0:
                        take(6)
                    else:
                        pe.wait_ge(eT_ok, at(n - 1))
                mm(bank[6][j % 2 * C:(j % 2 + 1) * C, :], w2S[0:m, j, :], hh[0:m, j % SLOTS, :],
                   start=(j < 2), stop=(j >= NKT - 2)).then_inc(w2_done, 1)

            def finish(n):
                pe.wait_ge(eT_ok, at(n))
                if isinstance(n, int):
                    take(7)
                else:
                    pe.wait_ge(en_ok, at(n - 1))
                for t in range(TPB):
                    last = nc.tensor.transpose(bank[7][:, t * P:(t + 1) * P], yT[:, t * P:(t + 1) * P], ident[:, :])
                last.then_inc(en_ps, 1)
                reader[7] = (en_ok, at(n))

            def experts(n, q):
                for j in range(NKT):
                    gates(n, j, q)
                    if j >= 3 and j % 2:
                        down(n, j - 3)
                        down(n, j - 2)
                    if not (isinstance(n, int) and n == 0):
                        if j == 0:
                            down(n - 1, NKT - 3)
                            down(n - 1, NKT - 2)
                        if j == 1:
                            down(n - 1, NKT - 1)
                        if j == FINISH_AT:
                            finish(n - 1)
                    if isinstance(n, int):
                        events(TILE_EVENTS["pe"][n * NKT + j])

            for n in range(BPS):
                experts(n, n % 2)
            with pe.Fori(BPS // 2, NBLK // 2) as p:
                experts(2 * p, 0)
                experts(2 * p + 1, 1)
            for j in range(NKT - 3, NKT):
                down(NBLK - 1, j)
            finish(NBLK - 1)


def rope_tables():
    import numpy as np
    inv_freq = 1.0 / 10000.0 ** (np.arange(0, HD, 2, dtype=np.float32) / HD)
    freqs = np.outer(np.arange(T, dtype=np.float32), inv_freq)
    emb = np.concatenate([freqs, freqs], axis=-1)
    cos, sin = np.cos(emb).astype(np.float32), np.sin(emb).astype(np.float32)
    sin = np.concatenate([-sin[:, :HD // 2], sin[:, HD // 2:]], axis=-1)
    return [np.ascontiguousarray(np.tile(x.T, (NH + NKV, NB))) for x in (cos, sin)]


def kernel(x, L0_tok_shared_embedding, L0_tok_hash_weights_table, L0_attn_Q, L0_attn_E, L0_ffn_ln1_w, L0_ffn_ln2_w,
           L0_ffn_wq, L0_ffn_wk, L0_ffn_wv, L0_ffn_wo, L0_ffn_router_w, L0_ffn_w1, L0_ffn_w2, L0_ffn_w3):
    import ml_dtypes
    import numpy as np
    import concourse.bacc as bacc
    from concourse.bass_utils import run_bass_kernel_spmd

    def twice(w):
        return np.concatenate([w, w], axis=0)

    qk = np.concatenate([L0_ffn_wq, L0_ffn_wk], axis=0)
    rot = np.roll(qk.reshape(NH + NKV, 2, HD // 2, C), 1, axis=1).reshape(NQK, C)
    w2 = np.zeros((NKT * P, C), np.float32)
    w2[:NHID] = L0_ffn_w2.transpose(0, 2, 1).reshape(NHID, C)
    cos, sin = rope_tables()
    arrays = {
        "ids": x.reshape(NT, P).T,
        "table": L0_tok_shared_embedding,
        "hash_w": L0_tok_hash_weights_table,
        "lq": twice(L0_attn_Q.transpose(1, 0, 2).reshape(C, LH * C)),
        "le": L0_attn_E.reshape(NPAIR, 2, C, C).transpose(1, 3, 0, 2).reshape(P, NPAIR, C),
        "ln1": L0_ffn_ln1_w.reshape(1, C),
        "ln2": L0_ffn_ln2_w.reshape(1, C),
        "wqk": twice(qk.T),
        "wrot": twice(rot.T),
        "wv": twice(L0_ffn_wv.T),
        "wo": twice(L0_ffn_wo.T),
        "wr": twice(L0_ffn_router_w.T),
        "w1": twice(L0_ffn_w1.reshape(NHID, C).T),
        "w3": twice(L0_ffn_w3.reshape(NHID, C).T),
        "w2": w2.reshape(NKT, P, C).transpose(1, 0, 2),
        "sel": np.tile(np.arange(NKT * P)[None, :] // HID == np.arange(EW)[:, None], (3, 1)).astype(ml_dtypes.bfloat16),
        "cos": cos,
        "sin": sin,
    }
    arrays = {k: np.ascontiguousarray(a) for k, a in arrays.items()}
    nc = bacc.Bacc("TRN2", target_bir_lowering=False, num_devices=1)
    args = [nc.dram_tensor(k, a.shape, mybir.dt.from_np(a.dtype), kind="ExternalInput").ap() for k, a in arrays.items()]
    out = nc.dram_tensor("out", (NB, T, C), F32, kind="ExternalOutput").ap()
    program(nc, *args, out)
    r = run_bass_kernel_spmd(nc, [arrays], core_ids=[0])
    return r.results[0]["out"]
```

```python
from contextlib import ExitStack

import concourse.bass as bass
from concourse import mybir

F32 = mybir.dt.float32
BF16 = mybir.dt.bfloat16
I32 = mybir.dt.int32
U32 = mybir.dt.uint32
ALU = mybir.AluOpType
ACT = mybir.ActivationFunctionType
AX = mybir.AxisListType.X

P = 128
C = 64
NB, T = 2, 2048
BLK = 512
TPB = BLK // P
NBLK = NB * T // BLK
BPS = T // BLK
NT = NB * T // P
LH = 8
NPAIR = LH // 2
NH, NKV, HD = 4, 2, 16
VW = 32
NQK = (NH + NKV) * HD
NTERM = 6
KSC = NTERM * HD
KROWS = KSC + 3
QPART = [0, 0, 1, 1, 0, 2]
KPART = [0, 1, 0, 1, 2, 0]
NE, HID = 8, 170
EW = 32
NHID = NE * HID
NKT = (NHID + P - 1) // P
HASHP, HASHM, IC, NSPECIAL, VOCAB = 100003, 12500, 4, 4, 25000
HASH_A, HASH_B = (12345, 20011), (6789, 54321)
EPS_LN, EPS_RMS = 1e-5, 1e-6
NEG = -1e30


def at(n, k=1, per=1):
    return per * n + k + 1


def wait(eng, s, value):
    if not (isinstance(value, int) and value < 2):
        eng.wait_ge(s, value)


def bcast(ap, n):
    return ap.unsqueeze(len(ap.shape)).to_broadcast([*ap.shape, n])


def program(nc, ids, table, hash_w, lq, le, ln1, ln2, wqk, wrot, wv, wo, wr, w1, w3, w2, sel, cos, sin, out):
    with ExitStack() as ctx:
        def sb(name, shape, dt=F32):
            return ctx.enter_context(nc.sbuf_tensor(name, shape, dt))

        sems = []

        def sem(name, first=1):
            s = ctx.enter_context(nc.semaphore(name))
            if first:
                sems.append(s)
            return s

        ps = ctx.enter_context(nc.psum_tensor("ps", [P, 8, 512], F32))
        bank = [ps[:, i, :] for i in range(8)]
        parts_dram = nc.dram_tensor("qk_parts", (NBLK, NQK, 3, BLK), BF16, kind="Internal").ap()

        ident = sb("ident", [P, P])
        identb = sb("identb", [P, P], BF16)
        keep_t_ge_u = sb("keep_t_ge_u", [P, P])
        h_all = sb("h_all", [P, NT, C])
        x_all = sb("x_all", [P, NT, C])
        Qs = sb("Qs", [KROWS, NBLK, NH, BLK], BF16)
        Ks = sb("Ks", [KROWS, NBLK, NKV, BLK], BF16)
        Vn = sb("Vn", [P, NT, NKV * VW])
        xid = sb("xid", [P, NT], I32)
        dig = sb("dig", [P, 3, NT], I32)
        hsh = sb("hsh", [P, 2, NT])
        quo = sb("quo", [P, 2, NT], I32)
        quf = sb("quf", [P, 2, NT])
        rows = sb("rows", [P, NT, 3], U32)
        emb = sb("emb", [P, TPB, 2, C])
        embw = sb("embw", [P, TPB, 2])
        t2 = sb("t2", [P, TPB, 2, C])
        xc = sb("xc", [P, TPB, C])
        sq = sb("sq", [P, TPB, C])
        st = sb("st", [P, 5, TPB])
        rn = sb("rn", [P, TPB, C])
        xp = t2[:, :, 0, :]
        rr = sb("rr", [P, TPB, 2 * C])
        res = sb("res", [P, TPB, C])
        Sx = sb("Sx", [P, 2, TPB, 4 * C], BF16)
        AB = sb("AB", [P, 2, 2, BLK], BF16)
        rTe = sb("rTe", [P, BLK])
        rTo = sb("rTo", [P, BLK])
        products = sb("products", [P, 2 * NPAIR, BLK])
        qh = products[:, 0:NPAIR, :]
        Gs = products[:, NPAIR:, :]
        oT = sb("oT", [P, 2 * P])
        Cd = sb("Cd", [P, TPB, P])
        keep = sb("keep", [P, NBLK])
        hn = sb("hn", [P, TPB, C])
        ln1b = sb("ln1b", [P, C])
        csb = sb("csb", [NQK, 2, BLK])
        rp = sb("rp", [NQK, 4, BLK])
        qkp = sb("qkp", [NQK, 3, BLK], BF16)
        wtmp = sb("wtmp", [P, NHID + C + NE])
        wres = sb("wres", [P, NHID])

        def weight3(name, n):
            return sb(name, [P, 3, n], BF16)

        lq3 = weight3("lq3", NPAIR * P)
        wqk3 = weight3("wqk3", 2 * NQK)
        wv3 = weight3("wv3", NKV * HD)
        wo3 = weight3("wo3", C)
        wr3 = weight3("wr3", NE)
        w13 = weight3("w13", NHID)
        w33 = weight3("w33", NHID)
        leS = sb("leS", [P, NPAIR, C])
        w2S = sb("w2S", [P, NKT, C])
        ln2b = sb("ln2b", [P, C])
        selb = sb("selb", [3 * EW, NKT * P], BF16)
        neg_t_lt_s = sb("neg_t_lt_s", [P, P], BF16)
        neg_s_gt_t = sb("neg_s_gt_t", [P, P], BF16)
        mxc = sb("mxc", [P, NH, TPB, BPS])
        mneg = sb("mneg", [P, 2, NH * TPB])
        m3 = sb("m3", [P, 3, NH * TPB], BF16)
        mrow = sb("mrow", [3 * NH * TPB, P], BF16)
        pexp = sb("pexp", [P, 2, NH, BLK])
        om = pexp[:, :, 0:2, :].rearrange("p c e (a t) -> p c e a t", t=P)
        yT = rTe
        rden = sb("rden", [P, TPB, NH])
        y_all = sb("y_all", [P, NT, C])
        ABf = products[:, :, :].bitcast(BF16).rearrange("p a (s t) -> p a s t", s=2)
        var2 = sb("var2", [P, NT])
        lg = sb("lg", [P, NT, NE])
        pr = sb("pr", [P, NT, NE])
        tk = sb("tk", [P, NT, NE])
        tr = sb("tr", [P, NT, NE])
        cols = sb("cols", [P, 4, NT])
        rank = sb("rank", [P, NE])
        w3s = sb("w3s", [P, NT, 3, EW], BF16)
        WT = rp[:, :, :].bitcast(BF16).rearrange("p a (s t) -> p (a s) t", s=2)
        sg, hu, hh = pexp[:, 0, 0:2, :], pexp[:, 0, 2:4, :], pexp[:, 1, :, :]
        SLOTS = NH
        fin = rn

        ids_in, consts_in = sem("ids_in"), sem("consts_in")
        weight_in = sem("weight_in")
        weight_free = sem("weight_free")
        masks_ok = sem("masks_ok")
        init_ok, late_ok = sem("init_ok"), sem("late_ok")
        rows_ok = sem("rows_ok")
        gathered = sem("gathered", first=0)
        emb_used = sem("emb_used")
        var_r = [sem(f"var_r{i}") for i in range(3)]
        xr_ok, x1_ok, split_ok, stacked, ab_ok = ([sem(f"{x}{i}") for i in range(2)] for x in ("xr_ok", "x1_ok", "split_ok", "stacked", "ab_ok"))
        sd_r = [sem(f"sd_r{i}") for i in range(3)]
        rr_ok, sum_ok = sem("rr_ok"), sem("sum_ok")
        rT_ps, rT_ok = sem("rT_ps"), sem("rT_ok")
        cup_ps, cup_ok = sem("cup_ps"), sem("cup_ok")
        qh_ps, qh_ok = sem("qh_ps"), sem("qh_ok")
        om_ps, om_ok = sem("om_ps"), sem("om_ok")
        g_ps, g_ok = sem("g_ps"), sem("g_ok")
        inter_done = sem("inter_done")
        oT_ps, oT_ok = sem("oT_ps"), sem("oT_ok")
        on_ps, on_ok = sem("on_ps"), sem("on_ok")
        qk_ps, v_ps, rope_ok, v_ok = sem("qk_ps"), sem("v_ps"), sem("rope_ok"), sem("v_ok")
        cs_in = sem("cs_in")
        parts_ok = sem("parts_ok")
        parts_out, qk_in = sem("parts_out"), sem("qk_in")
        out_done = sem("out_done")
        mx_ps, mx_ok, m3_ok, mt_ps, mrow_ok, m_in = sem("mx_ps"), sem("mx_ok"), sem("m3_ok"), sem("mt_ps"), sem("mrow_ok"), sem("m_in")
        st_ps, exp_ok, pv_ok = sem("st_ps"), sem("exp_ok"), sem("pv_ok")
        yT_ok, yn_ps, yn_ok = sem("yT_ok"), sem("yn_ps"), sem("yn_ok")
        xb_ok, xb1_ok, sb_ok, stb, abb_ok = sem("xb_ok"), sem("xb1_ok"), sem("sb_ok"), sem("stb"), sem("abb_ok")
        wo_ps, wo_ok = sem("wo_ps"), sem("wo_ok")
        var2_ok, sd2_ok = sem("var2_ok"), sem("sd2_ok")
        lg_ps, lg_ok, lm_ok, pe_ok, w_ok = sem("lg_ps"), sem("lg_ok"), sem("lm_ok"), sem("pe_ok"), sem("w_ok")
        WT_ps, WT_ok = sem("WT_ps"), sem("WT_ok")
        gu_ps, wb_ps, sg_ok, hu_ok, hh_ok, w2_done = sem("gu_ps"), sem("wb_ps"), sem("sg_ok"), sem("hu_ok"), sem("hh_ok"), sem("w2_done")
        eT_ok, en_ps, en_ok, fin_ok = sem("eT_ok"), sem("en_ps"), sem("en_ok"), sem("fin_ok")

        block = ctx.enter_context(nc.Block())
        outv = out.rearrange("b (t p) c -> p (b t) c", p=P)
        WEIGHTS = [(lq, lq3, NPAIR * P), (wqk, wqk3[:, :, 0:NQK], NQK), (wrot, wqk3[:, :, NQK:], NQK), (wv, wv3, NKV * HD),
                   (wo, wo3, C), (wr, wr3, NE), (w1, w13, NHID), (w3, w33, NHID)]
        WEIGHTS_A, WEIGHTS_LAST = 4, 7
        WEIGHT_AT = {4: NHID, 5: NHID + C, 6: 0, 7: 0}
        BLOCKS = [*range(BPS), *reversed(range(BPS, NBLK))]
        REACH = [b % BPS for b in BLOCKS]
        STEPS = [(i, s) for i in range(NBLK) for s in range(TPB * (REACH[i] + 1))]
        LAST = [max(g for g, (i, _) in enumerate(STEPS) if i == k) for k in range(NBLK)]
        UNITS = []
        for j in range(NBLK):
            for t in range(TPB):
                UNITS += [(j, t, h, 1, c) for h in range(NH) for c in range(REACH[j])]
                together = TPB // (t + 1)
                UNITS += [(j, t, h, together, REACH[j]) for h in range(0, NH, together)]
        U_END = [sum(1 for u in UNITS if u[0] <= j) for j in range(NBLK)]

        EARLY = 8

        def tiles(i):
            return slice(BLOCKS[i] * TPB, (BLOCKS[i] + 1) * TPB)

        QH_BANK = (0, 7, 2, 3)

        def attention_bank(i):
            return 6 if i < NBLK - 2 else 7

        def norm_bank(i):
            return 6 if i < NBLK - 1 else 7

        def router_bank(i):
            return 6 if i < BPS else 7

        def unit_bank(u):
            return bank[(6, 7, 4, 5)[u % 4]] if u < U_END[0] else bank[4 + u % 2]

        def step_cost(g):
            i, s = STEPS[g]
            return (NH * 2 + 1) * (BLK - max(0, s - TPB * REACH[i]) * P)

        def plan_units():
            due = [(max(LAST[j - 1] - 3, 1), U_END[j]) for j in range(1, NBLK)]
            done, out = U_END[0] + EARLY, []
            for g in range(len(STEPS)):
                ahead = [(u - done) * step_cost(g) / sum(map(step_cost, range(g, d))) for d, u in due if d > g]
                n = int(max([0, *ahead]) + 0.999)
                out.append((done, done + n))
                done += n
            return out

        IN_STEP = plan_units()
        TOP_TWO = ("top_shares", "top_first", "top_second", "top_split")
        FLUSH = 16
        EVENTS = {e: [[] for _ in range(len(STEPS) + FLUSH)] for e in ("pe", "act", "dve")}
        LAST_BLOCK_EVENTS = [("last_input", {"dve": 0}), ("last_splits", {"act": 0, "dve": 1}), ("last_stack", {"pe": 1, "act": 2}),
                             ("last_qk", {"pe": 3, "dve": 4}), ("last_rotated", {"pe": 4, "dve": 5}), ("last_v", {"pe": 5, "act": 6})]
        bank6_steps = set()
        splits_free = 0

        def put(name, i, **steps):
            for engine, g in steps.items():
                EVENTS[engine][g].append((name, i))

        def free_step(g):
            while g in bank6_steps:
                g += 1
            bank6_steps.add(g)
            return g

        def put_norm(i):
            put("norm", i, act=LAST[i] + 1)
            turned = free_step(LAST[i] + 2)
            put("norm", i, pe=turned, dve=turned + 1)
            return turned

        def put_y(i):
            nonlocal splits_free
            copied = max(put_norm(i) + 1, splits_free)
            stacked = free_step(copied + 2)
            put("y_copy", i, act=copied, dve=copied + 2)
            put("y_stack", i, pe=stacked, act=stacked + 1)
            product = free_step(stacked + 3)
            put("y_product", i, pe=product)
            put("y_sum", i, dve=product + 1)
            splits_free = stacked + 1
            return product + 1

        def put_x(i, g):
            nonlocal splits_free
            start = max(g, splits_free)
            put("x_norm", i, dve=start)
            stacked = free_step(start + 3)
            put("x_copy", i, act=start, dve=start + 2)
            put("x_stack", i, pe=stacked, dve=stacked + 1)
            product = free_step(stacked + 3)
            put("x_product", i, pe=product)
            put("x_keep", i, dve=product + 1)
            splits_free = stacked + 1
            return product + 1

        for name, steps in LAST_BLOCK_EVENTS:
            put(name, NBLK - 1, **steps)
            if "pe" in steps:
                free_step(steps["pe"])
        for j in range(1, NBLK):
            g = free_step(next(g for g, (_, u) in enumerate(IN_STEP) if u >= U_END[j]) + (j > 1))
            put("row", j, pe=g, act=g + 1)
        for i in range(BPS):
            summed = put_y(i)
        put("root", 0, dve=summed, act=summed)
        put("inverse", 0, dve=summed + 1)
        routed = summed + 1
        for i in range(BPS):
            routed = put_x(i, summed + 1)
        put("top_exp", 0, dve=routed, act=routed + 1)
        for d, name in enumerate(TOP_TWO):
            put(name, 0, dve=routed + 2 + 2 * d)
        for i in range(BPS):
            g = free_step(routed + 3 + 2 * len(TOP_TWO))
            put("turn", i, pe=g, dve=g + 1)
        for i in range(BPS, NBLK - 2):
            put_y(i)
        put_norm(NBLK - 2)
        FINISH_AT = 3
        TILE_EVENTS = {e: [[] for _ in range(BPS * NKT)] for e in ("pe", "act", "dve")}
        bank7_tiles = {n * NKT + FINISH_AT for n in range(1, BPS)}

        def beside(name, i, **tiles):
            for engine, g in tiles.items():
                TILE_EVENTS[engine][g].append((name, i))

        def free_tile(g):
            while g in bank7_tiles:
                g += 1
            bank7_tiles.add(g)
            return g

        beside("norm", NBLK - 1, pe=free_tile(1), dve=1)
        y_at = 0
        for i in (NBLK - 2, NBLK - 1):
            beside("y_copy", i, act=y_at, dve=y_at + 1)
            stack_at = free_tile(y_at + 3)
            beside("y_stack", i, pe=stack_at, act=stack_at)
            product_at = free_tile(stack_at + 2)
            beside("y_product", i, pe=product_at)
            beside("y_sum", i, dve=product_at)
            y_at = stack_at + 1
        beside("root", 1, dve=product_at, act=product_at + 1)
        beside("inverse", 1, dve=product_at + 2)
        x_at = product_at + 2
        for i in range(BPS, NBLK):
            beside("x_norm", i, dve=x_at)
            beside("x_copy", i, act=x_at + 2, dve=x_at + 2)
            stack_at = free_tile(x_at + 4)
            beside("x_stack", i, pe=stack_at, act=stack_at)
            product_at = free_tile(stack_at + 2)
            beside("x_product", i, pe=product_at)
            beside("x_keep", i, dve=product_at)
            x_at = stack_at - 1
        beside("top_exp", 1, dve=product_at, act=product_at + 1)
        for d, name in enumerate(TOP_TWO):
            beside(name, 1, dve=product_at + 2 + 2 * d)
        for i in range(BPS, NBLK):
            g = free_tile(product_at + 2 + 2 * len(TOP_TWO))
            beside("turn", i, pe=g, act=g)
        ROUND = {(e[0], i): r for r, (e, i) in enumerate([x for ev in (*EVENTS["act"], *TILE_EVENTS["act"]) for x in ev if x[0] in ("y_copy", "x_copy")])}

        @block.sync
        def _(sp):
            for s in sems:
                sp.sem_inc(s, 1)
            sp.dma_start(xid[:, :], ids).then_inc(ids_in, 16)
            sp.dma_start(leS[:, :, :], le).then_inc(consts_in, 16)
            sp.dma_start(ln1b[:, :], ln1.to_broadcast([P, C])).then_inc(consts_in, 16)
            sp.dma_start(ln2b[:, :], ln2.to_broadcast([P, C])).then_inc(consts_in, 16)
            sp.dma_start(w2S[:, :, :], w2).then_inc(consts_in, 16)
            sp.dma_start(selb[:, :], sel).then_inc(consts_in, 16)

            def load_weights(first, last):
                for i in range(first, last):
                    src, _, n = WEIGHTS[i]
                    wait(sp, weight_free, at(i - 1))
                    sp.dma_start(wtmp[:, 0:n], src).then_inc(weight_in, 16)

            load_weights(0, WEIGHTS_A)
            sp.wait_ge(weight_free, at(WEIGHTS_A - 1))
            for i in range(WEIGHTS_A, WEIGHTS_LAST):
                src, _, n = WEIGHTS[i]
                sp.dma_start(wtmp[:, WEIGHT_AT[i]:WEIGHT_AT[i] + n], src).then_inc(weight_in, 16)
            with sp.Fori(0, NBLK) as n:
                sp.wait_ge(rope_ok, at(n, 0, 2))
                sp.dma_start(csb[:, 0, :], cos[:, bass.ts(n, BLK)]).then_inc(cs_in, 16)
                sp.dma_start(csb[:, 1, :], sin[:, bass.ts(n, BLK)]).then_inc(cs_in, 16)
                sp.wait_ge(parts_ok, at(n))
                sp.dma_start(parts_dram[bass.ts(n, 1), :, :, :].rearrange("a p s t -> (a p) s t"), qkp[:, :, :]).then_inc(parts_out, 16)
                sp.wait_ge(parts_out, at(n, 16, 16))
                for g in range(NTERM):
                    src = parts_dram[bass.ts(n, 1), 0:NH * HD, QPART[g], :].rearrange("a (h d) t -> d (a h) t", d=HD)
                    sp.dma_start(Qs[g * HD:(g + 1) * HD, bass.ts(n, 1), :, :].rearrange("p a h t -> p (a h) t"), src).then_inc(qk_in, 16)
                    src = parts_dram[bass.ts(n, 1), NH * HD:NQK, KPART[g], :].rearrange("a (h d) t -> d (a h) t", d=HD)
                    sp.dma_start(Ks[g * HD:(g + 1) * HD, bass.ts(n, 1), :, :].rearrange("p a h t -> p (a h) t"), src).then_inc(qk_in, 16)
            sp.wait_ge(qk_in, at(NBLK - 1, 12 * 16, 12 * 16))
            load_weights(WEIGHTS_LAST, len(WEIGHTS))
            with sp.Fori(0, NBLK) as n:
                sp.wait_ge(fin_ok, at(n))
                sp.dma_start(outv[:, bass.ts(n, TPB), :], fin[:, :, :]).then_inc(out_done, 16)
            sp.wait_ge(out_done, at(NBLK - 1, 16, 16))

        @block.gpsimd
        def _(pool):
            nc.gpsimd.memset(ident[:, :], 0.0)
            nc.gpsimd.memset(keep_t_ge_u[:, :], 1.0)
            nc.gpsimd.memset(Vn[:, :, :], 0.0)
            pool.drain()
            nc.gpsimd.memset(Ks[KSC:KROWS, :, :, :], 1.0)
            pool.drain()
            nc.gpsimd.affine_select(out=ident[:, :], in_=ident[:, :], compare_op=ALU.not_equal, fill=1.0,
                                    base=0, pattern=[[-1, P]], channel_multiplier=1)
            nc.gpsimd.affine_select(out=keep_t_ge_u[:, :], in_=keep_t_ge_u[:, :], compare_op=ALU.is_ge, fill=0.0,
                                    base=0, pattern=[[1, P]], channel_multiplier=-1)
            nc.gpsimd.memset(neg_t_lt_s[:, :], 0.0)
            nc.gpsimd.memset(neg_s_gt_t[:, :], 0.0)
            for e in range(NE):
                nc.gpsimd.memset(rank[:, e:e + 1], float(NE - e))
            pool.drain()
            nc.gpsimd.affine_select(out=neg_t_lt_s[:, :], in_=neg_t_lt_s[:, :], compare_op=ALU.is_ge, fill=NEG,
                                    base=0, pattern=[[-1, P]], channel_multiplier=1)
            nc.gpsimd.affine_select(out=neg_s_gt_t[:, :], in_=neg_s_gt_t[:, :], compare_op=ALU.is_ge, fill=NEG,
                                    base=0, pattern=[[1, P]], channel_multiplier=-1)
            for g in range(NKV):
                nc.gpsimd.memset(Vn[:, :, g * VW + HD:g * VW + HD + 1], 1.0)
            pool.drain()
            nc.gpsimd.tensor_copy(identb[:, :], ident[:, :]).then_inc(masks_ok, 1)
            pool.wait_ge(rows_ok, at(0))
            g = nc.gpsimd

            def gather(n):
                wait(pool, emb_used, at(n, 0))
                for t in range(TPB):
                    for h in range(2):
                        pool.indirect_dma_start(emb[:, t, h, :], None, table,
                                                bass.IndirectOffsetOnAxis(ap=rows[:, n * TPB + t, h:h + 1], axis=0)).then_inc(gathered, 16)
                    pool.indirect_dma_start(embw[:, t, :], None, hash_w,
                                            bass.IndirectOffsetOnAxis(ap=rows[:, n * TPB + t, 2:3], axis=0)).then_inc(gathered, 16)

            def rotated(n):
                pool.wait_ge(rope_ok, at(n, 2, 2))
                wait(pool, parts_out, at(n, 0, 16))
                g.tensor_tensor(rp[:, 0, :], rp[:, 1, :], rp[:, 2, :], ALU.add)
                g.tensor_tensor(qkp[:, 0, :], rp[:, 1, :], rp[:, 2, :], ALU.add).then_inc(sum_ok, 1)
                pool.drain()
                g.tensor_tensor(rp[:, 3, :], rp[:, 0, :], qkp[:, 0, :], ALU.subtract)
                g.tensor_tensor(qkp[:, 1, :], rp[:, 0, :], qkp[:, 0, :], ALU.subtract)
                pool.drain()
                g.tensor_tensor(qkp[:, 2, :], rp[:, 3, :], qkp[:, 1, :], ALU.subtract).then_inc(parts_ok, 1)

            gather(0)
            gather(1)
            for n in range(NBLK - 1):
                if n + 2 < NBLK:
                    gather(n + 2)
                if n:
                    rotated(n - 1)

            def split_weights(first, last):
                for i in range(first, last):
                    _, dst, n = WEIGHTS[i]
                    src = wtmp[:, WEIGHT_AT[i]:WEIGHT_AT[i] + n]
                    pool.wait_ge(weight_in, at(0, 16 * last, 16))
                    g.tensor_copy(dst[:, 0, :], src)
                    pool.drain()
                    g.tensor_tensor(wres[:, 0:n], src, dst[:, 0, :], ALU.subtract).then_inc(weight_free, 1)
                    pool.drain()
                    g.tensor_copy(dst[:, 1, :], wres[:, 0:n])
                    pool.drain()
                    g.tensor_tensor(dst[0:C, 2, :], wres[0:C, 0:n], dst[0:C, 1, :], ALU.subtract)
                    g.tensor_copy(dst[C:P, 2, :], dst[C:P, 0, :]).then_inc(late_ok, 1)
                    pool.drain()

            split_weights(WEIGHTS_A, WEIGHTS_LAST)
            rotated(NBLK - 2)
            rotated(NBLK - 1)
            split_weights(WEIGHTS_LAST, len(WEIGHTS))

        @block.scalar
        def _(act):
            a = nc.scalar

            def split_copies(n, i, src):
                act.wait_ge(xr_ok[i], at(n))
                wait(act, stacked[i], at(n - 1))
                a.activation(Sx[:, i, :, 0:C], src, ACT.Copy).then_inc(x1_ok[i], 1)
                a.activation(Sx[:, i, :, 2 * C:3 * C], src, ACT.Copy).then_inc(x1_ok[i], 1)

            def sqrt(n, i):
                act.wait_ge(var_r[i], at(n))
                a.activation(st[:, 2 + i, :], st[:, 2 + i, :], ACT.Sqrt).then_inc(sd_r[i], 1)

            def evac_ab(n, i, b):
                act.wait_ge(stacked[i], at(n))
                a.activation(AB[:, i, :, :], bank[b].bitcast(BF16).rearrange("p (s t) -> p s t", s=2), ACT.Copy).then_inc(ab_ok[i], 1)

            def g_copy(n, c):
                act.wait_ge(g_ps, at(n, c + 1, TPB))
                a.activation(Gs[:, :, c * P:(c + 1) * P], bank[6 + c % 2].rearrange("p (a t) -> p a t", a=NPAIR),
                             ACT.Copy).then_inc(g_ok, 1)

            def v_copy(n, b=6):
                act.wait_ge(v_ps, at(n))
                act.wait_ge(v_ps, 1)
                a.activation(Vn[:, bass.ts(n, TPB), :].rearrange("p t (g w) -> p t g w", g=NKV)[:, :, :, 0:HD],
                             bank[b][:, 0:TPB * NKV * HD].rearrange("p (t g d) -> p t g d", t=TPB, g=NKV),
                             ACT.Copy).then_inc(v_ok, 1)

            def double_r(n):
                wait(act, g_ps, at(n, 0, TPB))
                a.activation(rr[:, :, 0:C], rn[:, :, :], ACT.Copy).then_inc(rr_ok, 1)
                a.activation(rr[:, :, C:2 * C], rn[:, :, :], ACT.Copy).then_inc(rr_ok, 1)

            def main(n, post, prep):
                act.wait_ge(rT_ps, at(n))
                a.activation(rTe[0:C, :], bank[1][0:C, :], ACT.Copy)
                a.activation(rTo[C:P, :], bank[1][C:P, :], ACT.Copy).then_inc(rT_ok, 1)
                for p in range(NPAIR):
                    act.wait_ge(qh_ps, at(n, p + 1, NPAIR))
                    a.activation(qh[:, p, :], bank[QH_BANK[p]], ACT.Copy).then_inc(qh_ok, 1)
                if post:
                    sqrt(n - 1, 1)
                g_copy(n, 0)
                if prep:
                    sqrt(n + 1, 0)
                g_copy(n, 1)
                if post:
                    sqrt(n - 1, 2)
                g_copy(n, 2)
                g_copy(n, 3)
                if post:
                    split_copies(n - 1, 1, hn[:, :, :])
                if prep:
                    split_copies(n + 1, 0, rn[:, :, :])
                act.wait_ge(oT_ps, at(n))
                a.activation(oT[:, :], bank[4][:, 0:2 * P], ACT.Copy).then_inc(oT_ok, 1)
                if post:
                    evac_ab(n - 1, 1, 7)
                if prep:
                    double_r(n + 1)
                    evac_ab(n + 1, 0, 0)
                if post:
                    v_copy(n - 1)

            sqrt(0, 0)
            split_copies(0, 0, rn[:, :, :])
            double_r(0)
            evac_ab(0, 0, 0)
            main(0, False, True)
            with act.Fori(1, NBLK - 1) as n:
                main(n, True, True)
            main(NBLK - 1, True, False)
            sqrt(NBLK - 1, 1)
            sqrt(NBLK - 1, 2)
            def row(j):
                act.wait_ge(mt_ps, at(j))
                wait(act, m_in, at(j, 0, 48))
                a.activation(mrow[:, :], bank[6].bitcast(BF16)[0:3 * NH * TPB, 0:P], ACT.Copy).then_inc(mrow_ok, 1)
                act.wait_ge(mrow_ok, at(j))
                for g in range(3):
                    act.dma_start(Qs[KSC + g:KSC + g + 1, BLOCKS[j], :, :].rearrange("p h (i t) -> p (h i) t", t=P),
                                  mrow[g * NH * TPB:(g + 1) * NH * TPB, :]).then_inc(m_in, 16)

            def norm(i):
                act.wait_ge(pv_ok, at(LAST[i]))
                wait(act, yn_ps, at(i - 1))
                a.activation(yT[:, :], bank[7], ACT.Copy).then_inc(yT_ok, 1)

            def first_split(r, src):
                wait(act, stb, at(r - 1))
                a.activation(Sx[:, 1, :, 0:C], src, ACT.Copy)
                a.activation(Sx[:, 1, :, 2 * C:3 * C], src, ACT.Copy).then_inc(xb1_ok, 1)

            def y_copy(i):
                act.wait_ge(yn_ok, at(i))
                first_split(ROUND["y", i], y_all[:, tiles(i), :])

            def x_copy(i):
                act.wait_ge(xb_ok, at(i))
                first_split(ROUND["x", i], hn[:, :, :])

            def stack_copy(r, dst, misc):
                act.wait_ge(stb, at(r))
                a.activation(dst, bank[misc].bitcast(BF16).rearrange("p (s t) -> p s t", s=2), ACT.Copy).then_inc(abb_ok, 1)

            def y_stack(i):
                wait(act, wo_ps, at(i - 1))
                stack_copy(ROUND["y", i], AB[:, 1, :, :], attention_bank(i))

            def x_stack(i):
                stack_copy(ROUND["x", i], ABf[:, i, :, :], router_bank(i))

            def root(b):
                act.wait_ge(var2_ok, at(b))
                part = var2[:, b * (T // P):(b + 1) * (T // P)]
                a.activation(part, part, ACT.Sqrt).then_inc(sd2_ok, 1)

            def top_exp(b):
                act.wait_ge(lm_ok, at(b))
                part = slice(b * (T // P), (b + 1) * (T // P))
                a.activation(pr[:, part, :], lg[:, part, :], ACT.Exp).then_inc(pe_ok, 1)

            def turn(i):
                act.wait_ge(parts_ok, at(NBLK - 1))
                act.wait_ge(WT_ps, at(i))
                a.activation(WT[:, i, :], bank[router_bank(i)].bitcast(BF16)[0:3 * EW, 0:BLK], ACT.Copy).then_inc(WT_ok, 1)

            does = {"row": row, "norm": norm, "y_copy": y_copy, "x_copy": x_copy, "y_stack": y_stack, "x_stack": x_stack,
                    "root": root, "top_exp": top_exp, "turn": turn,
                    "last_splits": lambda n: split_copies(n, 1, hn[:, :, :]), "last_stack": lambda n: evac_ab(n, 1, 6), "last_v": v_copy}

            def events(found):
                for e, i in found:
                    if does.get(e):
                        does[e](i)

            row(0)
            for g, (i, s) in enumerate(STEPS):
                off = max(0, s - TPB * REACH[i]) * P
                for hp in range(2):
                    act.wait_ge(st_ps, at(g, hp + 1, 2))
                    wait(act, pv_ok, at(g - 2))
                    a.activation(pexp[:, g % 2, 2 * hp:2 * hp + 2, off:], ps[:, 2 * hp:2 * hp + 2, off:], ACT.Exp,
                                 scale=float(HD) ** -0.5).then_inc(exp_ok, 1)
                events(EVENTS["act"][g])
            for found in EVENTS["act"][len(STEPS):]:
                events(found)
            norm(NBLK - 1)


            def finish_copy(n):
                act.wait_ge(w2_done, at(n, NKT, NKT))
                wait(act, en_ps, at(n - 1))
                a.activation(yT[:, :], bank[6], ACT.Copy).then_inc(eT_ok, 1)

            def experts(n, q):
                for j in range(NKT):
                    m = min(P, NHID - j * P)
                    slot = (q + j) % 2
                    act.wait_ge(gu_ps, at(n, j + 1, NKT))
                    wait(act, hu_ok, at(n, j - 1, NKT))
                    a.activation(sg[0:m, slot, :], bank[slot][0:m, :], ACT.Silu).then_inc(sg_ok, 1)
                    if j == 1 and not (isinstance(n, int) and n == 0):
                        finish_copy(n - 1)
                    if isinstance(n, int):
                        events(TILE_EVENTS["act"][n * NKT + j])

            for n in range(BPS):
                experts(n, n % 2)
            with act.Fori(BPS // 2, NBLK // 2) as p:
                experts(2 * p, 0)
                experts(2 * p + 1, 1)
            finish_copy(NBLK - 1)

        @block.vector
        def _(dve):
            v = nc.vector
            v.memset(rTe[:, :], 0.0)
            v.memset(w3s[:, :, :, :], 0.0)
            v.memset(rTo[:, :], 0.0)
            v.memset(Cd[:, :, :], 0.0)
            v.memset(keep[:, :], 1.0)
            dve.drain()
            for s in range(1, NB + 1):
                v.memset(keep[:, s * BPS - 1:s * BPS], 0.0)
            dve.wait_ge(ids_in, at(0, 16, 16))
            v.tensor_scalar(dig[:, 0, :], xid[:, :], 63, None, ALU.bitwise_and)
            v.tensor_scalar(dig[:, 1, :], xid[:, :], 6, 63, ALU.logical_shift_right, ALU.bitwise_and)
            v.tensor_scalar(dig[:, 2, :], xid[:, :], 12, None, ALU.logical_shift_right)
            dve.drain()

            def reduce_mod(m):
                v.tensor_scalar(quo[:, :, :], hsh[:, :, :], 1.0 / m, None, ALU.mult)
                dve.drain()
                v.tensor_copy(quf[:, :, :], quo[:, :, :])
                dve.drain()
                v.scalar_tensor_tensor(hsh[:, :, :], quf[:, :, :], -float(m), hsh[:, :, :], ALU.mult, ALU.add)
                dve.drain()
                v.tensor_scalar(quf[:, :, :], hsh[:, :, :], 0.0, float(m), ALU.is_lt, ALU.mult)
                dve.drain()
                v.tensor_tensor(hsh[:, :, :], hsh[:, :, :], quf[:, :, :], ALU.add)
                dve.drain()
                v.tensor_scalar(quf[:, :, :], hsh[:, :, :], float(m), -float(m), ALU.is_ge, ALU.mult)
                dve.drain()
                v.tensor_tensor(hsh[:, :, :], hsh[:, :, :], quf[:, :, :], ALU.add)
                dve.drain()

            c = [[float(a * 64 ** k % HASHP) for k in range(3)] for a in HASH_A]
            for i in range(2):
                v.tensor_scalar(hsh[:, i, :], dig[:, 2, :], c[i][2], float(HASH_B[i]), ALU.mult, ALU.add)
            dve.drain()
            for k in (1, 0):
                for i in range(2):
                    v.scalar_tensor_tensor(hsh[:, i, :], dig[:, k, :], c[i][k], hsh[:, i, :], ALU.mult, ALU.add)
                dve.drain()
            reduce_mod(HASHP)
            reduce_mod(HASHM)
            x2 = xid[:, :].unsqueeze(1).to_broadcast([P, 2, NT])
            v.tensor_scalar(hsh[:, :, :], hsh[:, :, :], float(IC), None, ALU.add)
            dve.drain()
            v.tensor_tensor(quf[:, :, :], x2, hsh[:, :, :], ALU.subtract)
            dve.drain()
            v.scalar_tensor_tensor(quf[:, :, :], x2, float(NSPECIAL), quf[:, :, :], ALU.is_lt, ALU.mult)
            dve.drain()
            v.tensor_tensor(rows[:, :, 0:2].rearrange("p t i -> p i t"), hsh[:, :, :], quf[:, :, :], ALU.add)
            v.tensor_scalar(rows[:, :, 2], xid[:, :], float(VOCAB - 1), None, ALU.min)
            dve.drain()
            v.tensor_copy(quf[:, :, :], quf[:, :, :]).then_inc(rows_ok, 1)

            for i, (_, dst, n) in enumerate(WEIGHTS[:WEIGHTS_A]):
                dve.wait_ge(weight_in, at(0, 16 * (i + 1), 16))
                v.tensor_copy(dst[:, 0, :], wtmp[:, 0:n])
                dve.drain()
                v.tensor_tensor(wres[:, 0:n], wtmp[:, 0:n], dst[:, 0, :], ALU.subtract).then_inc(weight_free, 1)
                v.tensor_copy(dst[C:P, 2, :], dst[C:P, 0, :])
                dve.drain()
                v.tensor_copy(dst[:, 1, :], wres[:, 0:n])
                dve.drain()
                v.tensor_tensor(dst[0:C, 2, :], wres[0:C, 0:n], dst[0:C, 1, :], ALU.subtract)
                dve.drain()
            v.tensor_copy(quf[:, :, :], quf[:, :, :]).then_inc(init_ok, 1)
            dve.wait_ge(masks_ok, at(0))

            def mean_square(n, i, x, eps):
                v.tensor_tensor(sq[:, :, :], x, x, ALU.mult)
                dve.drain()
                v.tensor_reduce(st[:, 1, :], sq[:, :, :], AX, ALU.add)
                dve.drain()
                v.tensor_scalar(st[:, 2 + i, :], st[:, 1, :], 1.0 / C, eps, ALU.mult, ALU.add).then_inc(var_r[i], 1)

            def inverse(n, i):
                dve.wait_ge(sd_r[i], at(n))
                v.reciprocal(st[:, 2 + i, :], st[:, 2 + i, :])
                dve.drain()

            def center(dst, x):
                v.tensor_reduce(st[:, 0, :], x, AX, ALU.add)
                dve.drain()
                v.scalar_tensor_tensor(dst, bcast(st[:, 0, :], C), -1.0 / C, x, ALU.mult, ALU.add)
                dve.drain()

            def split_rest(n, i, x):
                dve.wait_ge(x1_ok[i], at(n, 1, 2))
                v.tensor_tensor(res[:, :, :], x, Sx[:, i, :, 0:C], ALU.subtract)
                v.tensor_tensor(Sx[:, i, :, C:2 * C], x, Sx[:, i, :, 0:C], ALU.subtract)
                dve.drain()
                v.tensor_tensor(Sx[:, i, :, 3 * C:4 * C], res[:, :, :], Sx[:, i, :, C:2 * C], ALU.subtract).then_inc(split_ok[i], 1)
                dve.drain()

            def block_of(x, n):
                return x[:, bass.ds(n * TPB, TPB), :]

            def prep_embed(n):
                h0 = block_of(h_all, n)
                dve.wait_ge(gathered, 16 * 3 * TPB * (n + 1))
                v.tensor_tensor(t2[:, :, :, :], emb[:, :, :, :], bcast(embw[:, :, :], C), ALU.mult).then_inc(emb_used, 1)
                dve.drain()
                v.tensor_tensor(h0, t2[:, :, 0, :], t2[:, :, 1, :], ALU.add)
                dve.drain()

            def prep_center(n):
                center(xp, block_of(h_all, n))
                mean_square(n, 0, xp, EPS_LN)

            def prep_norm(n):
                inverse(n, 0)
                wait(dve, rr_ok, at(n, 0, 2))
                v.tensor_tensor(rn[:, :, :], xp, bcast(st[:, 2, :], C), ALU.mult).then_inc(xr_ok[0], 1)
                dve.drain()

            def post_add(n):
                h = block_of(h_all, n).rearrange("p (s m) d -> p m s d", s=2)
                dve.wait_ge(on_ps, at(n))
                v.tensor_tensor(h, h, bank[5][:, 0:2 * P].rearrange("p (m s d) -> p m s d", m=2, s=2), ALU.add).then_inc(on_ok, 1)
                dve.drain()

            def post_center(n):
                center(xc[:, :, :], block_of(h_all, n))
                mean_square(n, 1, xc[:, :, :], EPS_LN)

            def post_norm(n):
                inverse(n, 1)
                v.tensor_tensor(block_of(x_all, n), xc[:, :, :], bcast(st[:, 3, :], C), ALU.mult)
                dve.drain()
                mean_square(n, 2, block_of(x_all, n), EPS_RMS)

            def post_input(n):
                inverse(n, 2)
                v.tensor_tensor(xc[:, :, :], block_of(x_all, n), bcast(st[:, 4, :], C), ALU.mult)
                dve.drain()
                v.tensor_tensor(hn[:, :, :], xc[:, :, :], ln1b[:, :].unsqueeze(1).to_broadcast([P, TPB, C]), ALU.mult).then_inc(xr_ok[1], 1)
                dve.drain()

            def post_rotate(n):
                dve.wait_ge(qk_ps, at(n, 2, 2))
                dve.wait_ge(cs_in, at(n, 32, 32))
                wait(dve, sum_ok, at(n, 0))
                for i in range(2):
                    v.tensor_tensor(rp[:, 1 + i, :], bank[2 + i][0:NQK, :], csb[:, i, :], ALU.mult).then_inc(rope_ok, 1)

            def last_rotate(i):
                n = NBLK - 1
                dve.wait_ge(qk_ps, at(n, 1 + i, 2))
                dve.wait_ge(cs_in, at(n, 32, 32))
                dve.wait_ge(sum_ok, at(n, 0))
                v.tensor_tensor(rp[:, 1 + i, :], bank[6][0:NQK, :], csb[:, i, :], ALU.mult).then_inc(rope_ok, 1)

            def omega_mask(n, c):
                for e in range(2):
                    dve.wait_ge(om_ps, at(n, 2 * c + e + 1, 2 * TPB))
                    wait(dve, g_ps, at(n, c - 1, TPB))
                    v.tensor_tensor(om[:, c % 2, e, :, :], bank[4 + e].rearrange("p (a t) -> p a t", a=NPAIR),
                                    keep_t_ge_u[:, :].unsqueeze(1).to_broadcast([P, NPAIR, P]), ALU.mult).then_inc(om_ok, 1)

            def main(n, post, prep):
                if post:
                    post_center(n - 1)
                if prep:
                    prep_embed(n + 1)
                omega_mask(n, 0)
                dve.wait_ge(cup_ps, at(n))
                for c in range(TPB - 1):
                    for s in (slice(0, C), slice(C, P)):
                        last = v.tensor_tensor(Cd[s, c + 1, s], Cd[s, c, s], bank[1][s, c * C:(c + 1) * C], ALU.add)
                    dve.drain()
                last.then_inc(cup_ok, 1)
                omega_mask(n, 1)
                dve.wait_ge(inter_done, at(n, 1, TPB))
                for s in (slice(0, C), slice(C, P)):
                    v.tensor_tensor(Cd[s, 0, s], Cd[s, 3, s], bank[1][s, 3 * C:4 * C], ALU.add)
                dve.drain()
                for s in (slice(0, C), slice(C, P)):
                    last = v.tensor_scalar(Cd[s, 0, s], Cd[s, 0, s], keep[s, bass.ds(n, 1)], None, ALU.mult)
                last.then_inc(cup_ok, 1)
                dve.drain()
                if prep:
                    prep_center(n + 1)
                omega_mask(n, 2)
                if post:
                    post_norm(n - 1)
                omega_mask(n, 3)
                if post:
                    post_input(n - 1)
                if prep:
                    prep_norm(n + 1)
                if post:
                    split_rest(n - 1, 1, hn[:, :, :])
                if prep:
                    split_rest(n + 1, 0, rn[:, :, :])
                post_add(n)
                if post:
                    post_rotate(n - 1)

            prep_embed(0)
            prep_center(0)
            prep_norm(0)
            split_rest(0, 0, rn[:, :, :])
            main(0, False, True)
            with dve.Fori(1, NBLK - 1) as n:
                main(n, True, True)
            main(NBLK - 1, True, False)

            def maxima(first, last):
                for u in range(first, last):
                    j, t, h, together, c = UNITS[u]
                    k = REACH[j]
                    w = BLK if c < k else (t + 1) * P
                    dve.wait_ge(mx_ps, at(u))
                    v.tensor_reduce(mxc[:, h:h + together, t, c], unit_bank(u)[:, 0:together * w].rearrange("p (h s) -> p h s", s=w),
                                    AX, ALU.max).then_inc(mx_ok, 1)
                    if u + 1 < U_END[j]:
                        continue
                    dve.drain()
                    if k:
                        v.tensor_reduce(mneg[:, 0, :], mxc[:, :, :, 0:k + 1].rearrange("p h i c -> p (h i) c"), AX, ALU.max, negate=True)
                    else:
                        v.tensor_scalar(mneg[:, 0, :], mxc[:, :, :, 0].rearrange("p h i -> p (h i)"), -1.0, None, ALU.mult)
                    dve.drain()
                    wait(dve, mt_ps, at(j - 1))
                    v.tensor_copy(m3[:, 0, :], mneg[:, 0, :])
                    dve.drain()
                    v.tensor_tensor(mneg[:, 1, :], mneg[:, 0, :], m3[:, 0, :], ALU.subtract)
                    v.tensor_tensor(m3[:, 1, :], mneg[:, 0, :], m3[:, 0, :], ALU.subtract)
                    dve.drain()
                    v.tensor_tensor(m3[:, 2, :], mneg[:, 1, :], m3[:, 1, :], ALU.subtract).then_inc(m3_ok, 1)
                    dve.drain()

            maxima(0, 3)
            post_center(NBLK - 1)
            maxima(3, 6)
            post_norm(NBLK - 1)
            maxima(6, U_END[0])
            maxima(U_END[0], U_END[0] + EARLY)

            def norm(i):
                dve.wait_ge(yn_ps, at(i))
                yn = bank[norm_bank(i)].rearrange("p (t h w) -> p t h w", t=TPB, h=NH)
                v.reciprocal(rden[:, :, :], yn[:, :, :, HD])
                dve.drain()
                v.tensor_tensor(y_all[:, tiles(i), :].rearrange("p t (h d) -> p t h d", h=NH),
                                yn[:, :, :, 0:HD], bcast(rden[:, :, :], HD), ALU.mult).then_inc(yn_ok, 1)
                dve.drain()

            def later_splits(r, x):
                dve.wait_ge(xb1_ok, at(r))
                v.tensor_tensor(res[:, :, :], x, Sx[:, 1, :, 0:C], ALU.subtract)
                v.tensor_tensor(Sx[:, 1, :, C:2 * C], x, Sx[:, 1, :, 0:C], ALU.subtract)
                dve.drain()
                v.tensor_tensor(Sx[:, 1, :, 3 * C:4 * C], res[:, :, :], Sx[:, 1, :, C:2 * C], ALU.subtract).then_inc(sb_ok, 1)
                dve.drain()

            def y_copy(i):
                later_splits(ROUND["y", i], y_all[:, tiles(i), :])

            def x_copy(i):
                later_splits(ROUND["x", i], hn[:, :, :])

            def y_sum(i):
                x = x_all[:, tiles(i), :]
                dve.wait_ge(wo_ps, at(i))
                v.tensor_tensor(x, x, bank[attention_bank(i)][:, 0:TPB * C].rearrange("p (t c) -> p t c", t=TPB), ALU.add).then_inc(wo_ok, 1)
                dve.drain()
                v.tensor_tensor(sq[:, :, :], x, x, ALU.mult)
                dve.drain()
                v.tensor_reduce(var2[:, tiles(i)], sq[:, :, :], AX, ALU.add)
                dve.drain()

            def root(b):
                part = var2[:, b * (T // P):(b + 1) * (T // P)]
                v.tensor_scalar(part, part, 1.0 / C, EPS_RMS, ALU.mult, ALU.add).then_inc(var2_ok, 1)

            def inverse_root(b):
                part = var2[:, b * (T // P):(b + 1) * (T // P)]
                dve.wait_ge(sd2_ok, at(b))
                v.reciprocal(part, part)
                dve.drain()

            def x_norm(i):
                v.tensor_tensor(xc[:, :, :], x_all[:, i * TPB:(i + 1) * TPB, :], bcast(var2[:, i * TPB:(i + 1) * TPB], C), ALU.mult)
                dve.drain()
                v.tensor_tensor(hn[:, :, :], xc[:, :, :], ln2b[:, :].unsqueeze(1).to_broadcast([P, TPB, C]), ALU.mult).then_inc(xb_ok, 1)
                dve.drain()

            def x_stack(i):
                dve.wait_ge(stb, at(ROUND["x", i]))
                v.tensor_copy(ABf[:, i, :, :], bank[6].bitcast(BF16).rearrange("p (s t) -> p s t", s=2)).then_inc(abb_ok, 1)

            def turn(i):
                dve.wait_ge(parts_ok, at(NBLK - 1))
                dve.wait_ge(WT_ps, at(i))
                v.tensor_copy(WT[:, i, :], bank[6].bitcast(BF16)[0:3 * EW, 0:BLK]).then_inc(WT_ok, 1)

            def x_keep(i):
                dve.wait_ge(lg_ps, at(i))
                v.tensor_copy(lg[:, i * TPB:(i + 1) * TPB, :],
                              bank[router_bank(i)][:, 0:TPB * NE].rearrange("p (t c) -> p t c", t=TPB)).then_inc(lg_ok, 1)
                dve.drain()

            def top_exp(b):
                part = slice(b * (T // P), (b + 1) * (T // P))
                v.tensor_reduce(cols[:, 0, part], lg[:, part, :], AX, ALU.max)
                dve.drain()
                v.tensor_tensor(lg[:, part, :], lg[:, part, :], bcast(cols[:, 0, part], NE), ALU.subtract).then_inc(lm_ok, 1)
                dve.drain()

            def top_parts(b):
                part = slice(b * (T // P), (b + 1) * (T // P))
                return part, pr[:, part, :], tk[:, part, :], tr[:, part, :], [cols[:, i, part] for i in range(4)]

            def top_shares(b):
                _, p_, _, _, c_ = top_parts(b)
                dve.wait_ge(pe_ok, at(b))
                v.tensor_reduce(c_[0], p_, AX, ALU.add)
                dve.drain()
                v.reciprocal(c_[1], c_[0])
                dve.drain()
                v.tensor_tensor(p_, p_, bcast(c_[1], NE), ALU.mult)
                dve.drain()

            def top_take(b, i):
                _, p_, t_, _, c_ = top_parts(b)
                v.tensor_reduce(c_[1 + i], p_, AX, ALU.max)
                dve.drain()
                v.tensor_tensor(t_, p_, bcast(c_[1 + i], NE), ALU.is_equal)
                dve.drain()
                v.tensor_tensor(t_, t_, rank[:, :].unsqueeze(1).to_broadcast([P, T // P, NE]), ALU.mult)
                dve.drain()
                v.tensor_reduce(c_[0], t_, AX, ALU.max)
                dve.drain()
                v.tensor_tensor(t_, t_, bcast(c_[0], NE), ALU.is_equal)
                dve.drain()

            def top_first(b):
                _, p_, t_, w_, _ = top_parts(b)
                top_take(b, 0)
                v.tensor_tensor(w_, t_, p_, ALU.mult)
                dve.drain()
                v.scalar_tensor_tensor(p_, t_, -2.0, p_, ALU.mult, ALU.add)
                dve.drain()

            def top_second(b):
                _, p_, t_, w_, c_ = top_parts(b)
                top_take(b, 1)
                v.tensor_tensor(t_, t_, p_, ALU.mult)
                dve.drain()
                v.tensor_tensor(w_, t_, w_, ALU.add)
                v.scalar_tensor_tensor(c_[0], c_[1], 1e-9, c_[2], ALU.add, ALU.add)
                dve.drain()

            def top_split(b):
                part, _, t_, w_, c_ = top_parts(b)
                v.reciprocal(c_[3], c_[0])
                dve.drain()
                v.tensor_tensor(w_, w_, bcast(c_[3], NE), ALU.mult)
                dve.drain()
                v.tensor_copy(w3s[:, part, 0, 0:NE], w_)
                dve.drain()
                v.tensor_tensor(t_, w_, w3s[:, part, 0, 0:NE], ALU.subtract)
                v.tensor_tensor(w3s[:, part, 1, 0:NE], w_, w3s[:, part, 0, 0:NE], ALU.subtract)
                dve.drain()
                v.tensor_tensor(w3s[:, part, 2, 0:NE], t_, w3s[:, part, 1, 0:NE], ALU.subtract).then_inc(w_ok, 1)
                dve.drain()

            does = {"norm": norm, "y_copy": y_copy, "x_copy": x_copy, "y_sum": y_sum, "root": root, "inverse": inverse_root,
                    "x_norm": x_norm, "x_stack": x_stack, "turn": turn, "x_keep": x_keep, "top_exp": top_exp,
                    "last_input": post_input, "last_splits": lambda n: split_rest(n, 1, hn[:, :, :]),
                    "last_qk": lambda n: last_rotate(0), "last_rotated": lambda n: last_rotate(1),
                    "top_shares": top_shares, "top_first": top_first, "top_second": top_second, "top_split": top_split}

            def events(found):
                for e, i in found:
                    if does.get(e):
                        does[e](i)

            for g, (first, last) in enumerate(IN_STEP):
                half = (first + last) // 2
                maxima(first, half)
                events(EVENTS["dve"][g])
                maxima(half, last)
            for found in EVENTS["dve"][len(STEPS):]:
                events(found)

            def finish(n):
                dve.wait_ge(en_ps, at(n))
                en = bank[7].rearrange("p (t s c) -> p t s c", t=TPB, s=2)
                v.tensor_tensor(xc[:, :, :], block_of(x_all, n), en[:, :, 0, :], ALU.add)
                dve.drain()
                v.tensor_tensor(sq[:, :, :], xc[:, :, :], en[:, :, 1, :], ALU.add).then_inc(en_ok, 1)
                dve.drain()
                wait(dve, out_done, at(n, 0, 16))
                v.tensor_tensor(fin[:, :, :], sq[:, :, :], block_of(h_all, n), ALU.add).then_inc(fin_ok, 1)
                dve.drain()

            def experts(n, q):
                for j in range(NKT):
                    m = min(P, NHID - j * P)
                    slot = (q + j) % 2
                    dve.wait_ge(sg_ok, at(n, j + 1, NKT))
                    v.tensor_tensor(hu[0:m, slot, :], sg[0:m, slot, :], bank[2 + slot][0:m, :], ALU.mult).then_inc(hu_ok, 1)
                    dve.drain()
                    dve.wait_ge(wb_ps, at(n, j + 1, NKT))
                    if j >= SLOTS:
                        dve.wait_ge(w2_done, at(n, j - SLOTS + 1, NKT))
                    else:
                        wait(dve, w2_done, at(n - 1, (NKT - 1 - j) // SLOTS * SLOTS + j + 1, NKT))
                    v.tensor_tensor(hh[0:m, j % SLOTS, :], hu[0:m, slot, :], bank[4 + slot][0:m, :], ALU.mult).then_inc(hh_ok, 1)
                    if j == FINISH_AT and not (isinstance(n, int) and n == 0):
                        finish(n - 1)
                    if isinstance(n, int):
                        events(TILE_EVENTS["dve"][n * NKT + j])

            for n in range(BPS):
                experts(n, n % 2)
            with dve.Fori(BPS // 2, NBLK // 2) as p:
                experts(2 * p, 0)
                experts(2 * p + 1, 1)
            finish(NBLK - 1)

        @block.tensor
        def _(pe):
            mm = nc.tensor.matmul

            def stack_transposes(n, i, b):
                pe.wait_ge(split_ok[i], at(n))
                pe.wait_ge(x1_ok[i], at(n, 2, 2))
                dst = bank[b].bitcast(BF16).rearrange("p (s t) -> p s t", s=2)
                for t in range(TPB):
                    for s in range(2):
                        last = nc.tensor.transpose(dst[:, s, t * P:(t + 1) * P], Sx[:, i, t, s * P:(s + 1) * P], identb[:, :])
                last.then_inc(stacked[i], 1)

            def split3(dst, w, cols, i):
                for k in range(3):
                    last = mm(dst, w[:, k, cols], AB[:, i, k // 2, :], start=(k == 0), stop=(k == 2))
                return last

            def omega(n, c):
                for e, rT in enumerate((rTe, rTo)):
                    wait(pe, om_ok, at(n, 2 * (c - 1) + e + 1, 2 * TPB))
                    mm(bank[4 + e], rT[:, c * P:(c + 1) * P], qh[:, :, c * P:(c + 1) * P], start=True, stop=True).then_inc(om_ps, 1)

            def qk_products(n):
                pe.wait_ge(ab_ok[1], at(n))
                for i in range(2):
                    split3(bank[2 + i][0:NQK, :], wqk3, slice(i * NQK, (i + 1) * NQK), 1).then_inc(qk_ps, 1)

            def v_products(n, b=6):
                for t in range(TPB):
                    for k in range(3):
                        last = mm(bank[b][:, t * NKV * HD:(t + 1) * NKV * HD], AB[:, 1, k // 2, t * P:(t + 1) * P], wv3[:, k, :],
                                  start=(k == 0), stop=(k == 2))
                last.then_inc(v_ps, 1)

            def main(n, post, prep):
                pe.wait_ge(rr_ok, at(n, 2, 2))
                wait(pe, cup_ok, at(n, 0, 2))
                for t in range(TPB):
                    last = nc.tensor.transpose(bank[1][:, t * P:(t + 1) * P], rr[:, t, :], ident[:, :])
                last.then_inc(rT_ps, 1)
                pe.wait_ge(ab_ok[0], at(n))
                for p in range(NPAIR):
                    if p == 2:
                        wait(pe, rope_ok, at(n - 2, 2, 2))
                    split3(bank[QH_BANK[p]], lq3, slice(p * P, (p + 1) * P), 0).then_inc(qh_ps, 1)
                pe.wait_ge(rT_ok, at(n))
                for c in range(TPB):
                    last = mm(bank[1][:, c * C:(c + 1) * C], rr[:, c, :], rr[:, c, 0:C], start=True, stop=True)
                last.then_inc(cup_ps, 1)
                pe.wait_ge(qh_ok, at(n, NPAIR, NPAIR))
                wait(pe, on_ok, at(n, 0))
                omega(n, 0)
                for c in range(TPB):
                    if c == 1:
                        pe.wait_ge(cup_ok, at(n, 1, 2))
                    if c == 0:
                        wait(pe, v_ok, at(n - 2))
                    wait(pe, g_ok, at(n, c - 1, TPB))
                    mm(bank[6 + c % 2], Cd[:, c, :], qh[:, :, c * P:(c + 1) * P], start=True, stop=False).then_inc(inter_done, 1)
                    if c + 1 < TPB:
                        omega(n, c + 1)
                    for e in range(2):
                        pe.wait_ge(om_ok, at(n, 2 * c + e + 1, 2 * TPB))
                        last = mm(bank[6 + c % 2][e * C:(e + 1) * C, :], rr[:, c, 0:C], om[:, c % 2, e, :, :], start=False, stop=True)
                    last.then_inc(g_ps, 1)
                pe.wait_ge(g_ok, at(n, TPB, TPB))
                for p in range(NPAIR):
                    for s in range(2):
                        last = mm(bank[4][s * C:(s + 1) * C, 0:2 * P], leS[:, p, :], Gs[:, p, s * 2 * P:(s + 1) * 2 * P],
                                  start=(p == 0), stop=(p == NPAIR - 1))
                last.then_inc(oT_ps, 1)
                if post:
                    stack_transposes(n - 1, 1, 7)
                if prep:
                    stack_transposes(n + 1, 0, 0)
                pe.wait_ge(oT_ok, at(n))
                for m in range(2):
                    last = nc.tensor.transpose(bank[5][:, m * P:(m + 1) * P], oT[:, m * P:(m + 1) * P], ident[:, :])
                last.then_inc(on_ps, 1)
                if post:
                    qk_products(n - 1)
                    v_products(n - 1)

            pe.wait_ge(init_ok, at(0))
            pe.wait_ge(masks_ok, at(0))
            pe.wait_ge(consts_in, at(0, 80, 16))
            stack_transposes(0, 0, 0)
            main(0, False, True)
            with pe.Fori(1, NBLK - 1) as n:
                main(n, True, True)
            main(NBLK - 1, True, False)

            def max_units(first, last):
                for u in range(first, last):
                    j, t, h, together, c = UNITS[u]
                    k = REACH[j]
                    w = BLK if c < k else (t + 1) * P
                    pe.wait_ge(qk_in, at(BLOCKS[j], 12 * 16, 12 * 16))
                    wait(pe, mx_ok, at(u - (4 if u < U_END[0] else 2)))
                    for i in range(together):
                        dst = unit_bank(u)[:, i * w:(i + 1) * w]
                        last_mm = mm(dst, Qs[0:KSC, BLOCKS[j], h + i, t * P:(t + 1) * P], Ks[0:KSC, j // BPS * BPS + c, (h + i) // 2, 0:w], start=True, stop=(c < k))
                        if c == k:
                            last_mm = mm(dst[:, t * P:(t + 1) * P], identb[:, :], neg_t_lt_s[:, :], start=False, stop=True)
                    last_mm.then_inc(mx_ps, 1)

            reader = {}

            def take(b):
                if b in reader:
                    pe.wait_ge(*reader[b])

            def row(j):
                pe.wait_ge(m3_ok, at(j))
                take(6)
                nc.tensor.transpose(bank[6].bitcast(BF16)[0:3 * NH * TPB, 0:P], m3[:, :, :].rearrange("p g c -> p (g c)"),
                                    identb[:, :]).then_inc(mt_ps, 1)
                reader[6] = (mrow_ok, at(j))

            def score(g, hp):
                i, s = STEPS[g]
                d = s - TPB * REACH[i]
                off = max(0, d) * P
                wait(pe, exp_ok, at(g - 1, hp + 1, 2))
                if s == 0 and hp == 0:
                    pe.wait_ge(m_in, at(i, 48, 48))
                for h in (2 * hp, 2 * hp + 1):
                    last = mm(ps[:, h, off:], Ks[:, i // BPS * BPS + s // TPB, hp, s % TPB * P:(s % TPB + 1) * P],
                              Qs[:, BLOCKS[i], h, off:], start=True, stop=(d < 0))
                    if d >= 0:
                        last = mm(ps[:, h, off:off + P], identb[:, :], neg_s_gt_t[:, :], start=False, stop=True)
                last.then_inc(st_ps, 1)

            def weigh(g, part):
                i, s = STEPS[g]
                off = max(0, s - TPB * REACH[i]) * P
                lo, hi = max(off, part * (BLK // 2)), (part + 1) * (BLK // 2) if s else (1 - part) * BLK
                if part == 0:
                    pe.wait_ge(exp_ok, at(g, 2, 2))
                    if s == 0:
                        wait(pe, yT_ok, at(i - 1))
                for h in range(NH if lo < hi else 0):
                    last = mm(bank[7][h * VW:(h + 1) * VW, lo:hi], Vn[:, i // BPS * (T // P) + s, h // 2 * VW:(h // 2 + 1) * VW],
                              pexp[:, g % 2, h, lo:hi], start=(s == 0), stop=(g == LAST[i]))
                if part == (1 if s else 0):
                    last.then_inc(pv_ok, 1)

            def norm(i):
                pe.wait_ge(yT_ok, at(i))
                take(norm_bank(i))
                for t in range(TPB):
                    last = nc.tensor.transpose(bank[norm_bank(i)][:, t * P:(t + 1) * P], yT[:, t * P:(t + 1) * P], ident[:, :])
                last.then_inc(yn_ps, 1)
                reader[norm_bank(i)] = (yn_ok, at(i))

            def stack(r, b):
                pe.wait_ge(sb_ok, at(r))
                take(b)
                dst = bank[b].bitcast(BF16).rearrange("p (s t) -> p s t", s=2)
                for t in range(TPB):
                    for s in range(2):
                        last = nc.tensor.transpose(dst[:, s, t * P:(t + 1) * P], Sx[:, 1, t, s * P:(s + 1) * P], identb[:, :])
                last.then_inc(stb, 1)
                reader[b] = (abb_ok, at(r))

            def y_stack(i):
                stack(ROUND["y", i], attention_bank(i))

            def x_stack(i):
                stack(ROUND["x", i], router_bank(i))

            def y_product(i):
                pe.wait_ge(late_ok, at(0, 1))
                pe.wait_ge(abb_ok, at(ROUND["y", i]))
                b = attention_bank(i)
                take(b)
                for t in range(TPB):
                    for k in range(3):
                        last = mm(bank[b][:, t * C:(t + 1) * C], AB[:, 1, k // 2, t * P:(t + 1) * P], wo3[:, k, :], start=(k == 0), stop=(k == 2))
                last.then_inc(wo_ps, 1)
                reader[b] = (wo_ok, at(i))

            def x_product(i):
                b = router_bank(i)
                pe.wait_ge(late_ok, at(0, 2))
                pe.wait_ge(abb_ok, at(ROUND["x", i]))
                take(b)
                for t in range(TPB):
                    for k in range(3):
                        last = mm(bank[b][:, t * NE:(t + 1) * NE], ABf[:, i, k // 2, t * P:(t + 1) * P], wr3[:, k, :], start=(k == 0), stop=(k == 2))
                last.then_inc(lg_ps, 1)
                reader[b] = (lg_ok, at(i))

            def turn(i):
                b = router_bank(i)
                pe.wait_ge(w_ok, at(i // BPS))
                take(b)
                for t in range(TPB):
                    last = nc.tensor.transpose(bank[b].bitcast(BF16)[0:3 * EW, t * P:(t + 1) * P],
                                               w3s[:, i * TPB + t, :, :].rearrange("p g e -> p (g e)"), identb[:, :])
                last.then_inc(WT_ps, 1)
                reader[b] = (WT_ok, at(i))

            def last_stack(n):
                take(6)
                stack_transposes(n, 1, 6)
                reader[6] = (ab_ok[1], at(n))

            def last_qk(n, i=0):
                pe.wait_ge(ab_ok[1], at(n))
                take(6)
                split3(bank[6][0:NQK, :], wqk3, slice(i * NQK, (i + 1) * NQK), 1).then_inc(qk_ps, 1)
                reader[6] = (rope_ok, at(n, 1 + i, 2))

            def last_v(n):
                take(6)
                v_products(n)
                reader[6] = (v_ok, at(n))

            does = {"last_stack": last_stack, "last_qk": last_qk, "last_rotated": lambda n: last_qk(n, 1), "last_v": last_v,
                    "row": row, "norm": norm, "y_stack": y_stack, "y_product": y_product, "x_stack": x_stack,
                    "x_product": x_product, "turn": turn}

            def events(found):
                for e, i in found:
                    if does.get(e):
                        does[e](i)

            pe.wait_ge(on_ok, at(NBLK - 1))
            pe.wait_ge(v_ok, at(NBLK - 2))
            pe.wait_ge(rope_ok, at(NBLK - 2, 2, 2))
            max_units(0, U_END[0])
            row(0)
            max_units(U_END[0], U_END[0] + EARLY)
            for g in range(len(STEPS)):
                first, last = IN_STEP[g]
                stand = [first + (last - first) * k // 4 for k in range(5)]
                score(g, 0)
                max_units(stand[0], stand[1])
                score(g, 1)
                max_units(stand[1], stand[2])
                if g:
                    weigh(g - 1, 0)
                max_units(stand[2], stand[3])
                if g:
                    weigh(g - 1, 1)
                max_units(stand[3], stand[4])
                events(EVENTS["pe"][g])
            weigh(len(STEPS) - 1, 0)
            weigh(len(STEPS) - 1, 1)
            for found in EVENTS["pe"][len(STEPS):]:
                events(found)

            pe.wait_ge(late_ok, at(0, 4))
            reader[7] = (yT_ok, at(NBLK - 1))
            pe.wait_ge(exp_ok, at(len(STEPS) - 1, 2, 2))
            pe.wait_ge(WT_ok, at(BPS - 1))

            def gates(n, j, q):
                m = min(P, NHID - j * P)
                slot = (q + j) % 2
                wait(pe, hu_ok, at(n, j - 1, NKT))
                for dst, w in ((bank[slot], w13), (bank[2 + slot], w33)):
                    for i in range(3):
                        last = mm(dst[0:m, :], w[:, i, j * P:j * P + m], ABf[:, bass.ds(n, 1), i // 2, :].rearrange("p a t -> p (a t)"),
                                  start=(i == 0), stop=(i == 2))
                last.then_inc(gu_ps, 1)
                wait(pe, hh_ok, at(n, j - 1, NKT))
                mm(bank[4 + slot][0:m, :], selb[:, j * P:j * P + m], WT[:, bass.ds(n, 1), :].rearrange("p a t -> p (a t)"),
                   start=True, stop=True).then_inc(wb_ps, 1)

            def down(n, j):
                m = min(P, NHID - j * P)
                pe.wait_ge(hh_ok, at(n, j + 1, NKT))
                if j == 0:
                    if isinstance(n, int) and n == 0:
                        take(6)
                    else:
                        pe.wait_ge(eT_ok, at(n - 1))
                mm(bank[6][j % 2 * C:(j % 2 + 1) * C, :], w2S[0:m, j, :], hh[0:m, j % SLOTS, :],
                   start=(j < 2), stop=(j >= NKT - 2)).then_inc(w2_done, 1)

            def finish(n):
                pe.wait_ge(eT_ok, at(n))
                if isinstance(n, int):
                    take(7)
                else:
                    pe.wait_ge(en_ok, at(n - 1))
                for t in range(TPB):
                    last = nc.tensor.transpose(bank[7][:, t * P:(t + 1) * P], yT[:, t * P:(t + 1) * P], ident[:, :])
                last.then_inc(en_ps, 1)
                reader[7] = (en_ok, at(n))

            def experts(n, q):
                for j in range(NKT):
                    gates(n, j, q)
                    if j >= 3 and j % 2:
                        down(n, j - 3)
                        down(n, j - 2)
                    if not (isinstance(n, int) and n == 0):
                        if j == 0:
                            down(n - 1, NKT - 3)
                            down(n - 1, NKT - 2)
                        if j == 1:
                            down(n - 1, NKT - 1)
                        if j == FINISH_AT:
                            finish(n - 1)
                    if isinstance(n, int):
                        events(TILE_EVENTS["pe"][n * NKT + j])

            for n in range(BPS):
                experts(n, n % 2)
            with pe.Fori(BPS // 2, NBLK // 2) as p:
                experts(2 * p, 0)
                experts(2 * p + 1, 1)
            for j in range(NKT - 3, NKT):
                down(NBLK - 1, j)
            finish(NBLK - 1)


def rope_tables():
    import numpy as np
    inv_freq = 1.0 / 10000.0 ** (np.arange(0, HD, 2, dtype=np.float32) / HD)
    freqs = np.outer(np.arange(T, dtype=np.float32), inv_freq)
    emb = np.concatenate([freqs, freqs], axis=-1)
    cos, sin = np.cos(emb).astype(np.float32), np.sin(emb).astype(np.float32)
    sin = np.concatenate([-sin[:, :HD // 2], sin[:, HD // 2:]], axis=-1)
    return [np.ascontiguousarray(np.tile(x.T, (NH + NKV, NB))) for x in (cos, sin)]


def kernel(x, L0_tok_shared_embedding, L0_tok_hash_weights_table, L0_attn_Q, L0_attn_E, L0_ffn_ln1_w, L0_ffn_ln2_w,
           L0_ffn_wq, L0_ffn_wk, L0_ffn_wv, L0_ffn_wo, L0_ffn_router_w, L0_ffn_w1, L0_ffn_w2, L0_ffn_w3):
    import ml_dtypes
    import numpy as np
    import concourse.bacc as bacc
    from concourse.bass_utils import run_bass_kernel_spmd

    def twice(w):
        return np.concatenate([w, w], axis=0)

    qk = np.concatenate([L0_ffn_wq, L0_ffn_wk], axis=0)
    rot = np.roll(qk.reshape(NH + NKV, 2, HD // 2, C), 1, axis=1).reshape(NQK, C)
    w2 = np.zeros((NKT * P, C), np.float32)
    w2[:NHID] = L0_ffn_w2.transpose(0, 2, 1).reshape(NHID, C)
    cos, sin = rope_tables()
    arrays = {
        "ids": x.reshape(NT, P).T,
        "table": L0_tok_shared_embedding,
        "hash_w": L0_tok_hash_weights_table,
        "lq": twice(L0_attn_Q.transpose(1, 0, 2).reshape(C, LH * C)),
        "le": L0_attn_E.reshape(NPAIR, 2, C, C).transpose(1, 3, 0, 2).reshape(P, NPAIR, C),
        "ln1": L0_ffn_ln1_w.reshape(1, C),
        "ln2": L0_ffn_ln2_w.reshape(1, C),
        "wqk": twice(qk.T),
        "wrot": twice(rot.T),
        "wv": twice(L0_ffn_wv.T),
        "wo": twice(L0_ffn_wo.T),
        "wr": twice(L0_ffn_router_w.T),
        "w1": twice(L0_ffn_w1.reshape(NHID, C).T),
        "w3": twice(L0_ffn_w3.reshape(NHID, C).T),
        "w2": w2.reshape(NKT, P, C).transpose(1, 0, 2),
        "sel": np.tile(np.arange(NKT * P)[None, :] // HID == np.arange(EW)[:, None], (3, 1)).astype(ml_dtypes.bfloat16),
        "cos": cos,
        "sin": sin,
    }
    arrays = {k: np.ascontiguousarray(a) for k, a in arrays.items()}
    nc = bacc.Bacc("TRN2", target_bir_lowering=False, num_devices=1)
    args = [nc.dram_tensor(k, a.shape, mybir.dt.from_np(a.dtype), kind="ExternalInput").ap() for k, a in arrays.items()]
    out = nc.dram_tensor("out", (NB, T, C), F32, kind="ExternalOutput").ap()
    program(nc, *args, out)
    r = run_bass_kernel_spmd(nc, [arrays], core_ids=[0])
    return r.results[0]["out"]
```
